# Optimizing a Trainium2 kernel written in Bass

```python
import numpy as np
import jax
import jax.numpy as jnp

def _softmax(x, axis=-1):
    return jax.nn.softmax(x, axis=axis)

def _gelu(x):
    return jax.nn.gelu(x, approximate=True)

def _silu(x):
    return jax.nn.silu(x)

def _sigmoid(x):
    return jax.nn.sigmoid(x)

def _layernorm(x, axis=-1, eps=1e-05):
    m = jnp.mean(x, axis=axis, keepdims=True)
    v = jnp.var(x, axis=axis, keepdims=True)
    return (x - m) / jnp.sqrt(v + eps)

def _scatter_add(tgt, idx, src, axis=0):
    return tgt.at[idx].add(src)

def _segment_sum(src, seg, n):
    return jax.ops.segment_sum(src, seg, n)
kernel_name = 'mk_cond_seq_d4_seqx_r8_f46517'

def setup_inputs(seed: int=0):
    np.random.seed(seed)
    _w = jnp.asarray

    def _rec_inputs():
        import jax
        import jax.numpy as jnp
        _rk = jax.random.key(seed)
        x = 1.648e-05 + 1 * jax.random.normal(jax.random.fold_in(_rk, 1), (128, 32, 128), jnp.float32)
        _lenS = 32 - jax.random.randint(jax.random.fold_in(_rk, 7), (128,), 0, max(1, 32 // 4) + 1, jnp.int32)
        _lenS2 = 32 - jax.random.randint(jax.random.fold_in(_rk, 8), (128,), 0, max(1, 32 // 4) + 1, jnp.int32)
        cond_1024 = 0.00191187 + 0.999416 * jax.random.normal(jax.random.fold_in(_rk, 11), (128, 128), jnp.float32)
        _validS = jnp.arange(32)[None, :] < _lenS[:, None]
        _validS2 = jnp.arange(32)[None, :] < _lenS2[:, None]
        _causal = jnp.tril(jnp.ones((32, 32), dtype=bool))
        mask_BxSxSx11_ik0 = jnp.where(jnp.ones((128, 32, 32, 11), dtype=bool), 0, 1).astype(jnp.int32)
        return (x, cond_1024, mask_BxSxSx11_ik0)
    x, cond_1024, mask_BxSxSx11_ik0 = _rec_inputs()

    def _L0_cond_setup():
        import jax, jax.numpy as jnp
        import numpy as np
        NONGT = 20
        H = 16
        NEG = -9000000000000000.0

        def _gat_attention(self_feat, cond_adj, label_bias, Wq, bq, Wk, bk, Wout, bout):
            B, N, F = self_feat.shape
            ng = min(NONGT, N)
            dh = F // H
            kv = self_feat[:, :ng]
            qh = (self_feat @ Wq.T + bq).reshape(B, N, H, dh)
            kh = (kv @ Wk.T + bk).reshape(B, ng, H, dh)
            aff = jnp.einsum('bnhd,bmhd->bnhm', qh, kh) * (1.0 / np.sqrt(dh))
            mask = cond_adj[:, :, None, :] > 0
            aff = jnp.where(mask, aff, NEG) + label_bias[:, :, None, :]
            w = jax.nn.softmax(aff, axis=-1)
            out_t = jnp.einsum('bnhm,bmf->bnhf', w, kv)
            out = jnp.einsum('bnhf,hgf->bnhg', out_t, Wout) + bout.reshape(H, F // H)
            return out.reshape(B, N, F)

        def _forward(v, q, adj, W_self, b_self, w_bias, b_bias, Wq, bq, Wk, bk, Wout, bout):
            adj_f = adj.astype(jnp.float32)
            exp_v = v
            row_zero = exp_v.sum(-1) == 0
            q_exp = jnp.where(row_zero[..., None], 0.0, q[:, None, :])
            vcq = jnp.concatenate([exp_v, q_exp], axis=-1)
            self_feat = vcq @ W_self.T + b_self
            output = self_feat
            for d in range(2):
                A = adj_f if d == 0 else jnp.swapaxes(adj_f, 1, 2)
                A = A[:, :, :NONGT, :]
                cond = A.sum(-1)
                vb = A @ w_bias + b_bias
                output = output + _gat_attention(self_feat, cond, vb, Wq[d], bq[d], Wk[d], bk[d], Wout[d], bout[d])
            rel = jax.nn.relu(output)
            return exp_v + rel
        key = jax.random.key(seed)
        ks = jax.random.split(key, 8)
        B, N, L, F, Q = (32, 36, 11, 128, 128)
        IN = F + Q
        s = 0.02
        return {'v': jax.random.normal(ks[0], (B, N, F), jnp.float32), 'q': jax.random.normal(ks[1], (B, Q), jnp.float32), 'adj': jax.random.randint(ks[2], (B, N, N, L), 0, 2, jnp.int32), 'W_self': jax.random.normal(ks[3], (F, IN), jnp.float32) * s, 'b_self': jnp.zeros((F,), jnp.float32), 'w_bias': jax.random.normal(ks[4], (L,), jnp.float32) * s, 'b_bias': jnp.zeros((), jnp.float32), 'Wq': jax.random.normal(ks[5], (2, F, F), jnp.float32) * s, 'bq': jnp.zeros((2, F), jnp.float32), 'Wk': jax.random.normal(ks[6], (2, F, F), jnp.float32) * s, 'bk': jnp.zeros((2, F), jnp.float32), 'Wout': jax.random.normal(ks[7], (2, H, F // H, F), jnp.float32) * s, 'bout': jnp.zeros((2, F), jnp.float32)}
    _L0_cond_all = _L0_cond_setup()
    _L0_cond_in = {k: v for k, v in _L0_cond_all.items() if k in ('W_self', 'b_self', 'w_bias', 'b_bias', 'Wq', 'bq', 'Wk', 'bk', 'Wout', 'bout')}
    del _L0_cond_all

    def _L1_cond_setup():
        import jax, jax.numpy as jnp
        import numpy as np
        D = 128
        H = 16
        HD = 4 * D
        B, T = (4, 128)
        EPS = 1e-05

        def _layernorm(x, g, b):
            mu = jnp.mean(x, axis=-1, keepdims=True)
            var = jnp.mean(jnp.square(x - mu), axis=-1, keepdims=True)
            return (x - mu) * jax.lax.rsqrt(var + EPS) * g + b

        def _attention(x, Wqkv, Wproj, bproj):
            b, t, c = x.shape
            hd = c // H
            qkv = (x @ Wqkv).reshape(b, t, 3, H, hd).transpose(2, 0, 3, 1, 4)
            q, k, v = (qkv[0], qkv[1], qkv[2])
            scale = hd ** (-0.5)
            scores = jnp.einsum('bhqd,bhkd->bhqk', q, k) * scale
            causal = jnp.tril(jnp.ones((t, t), bool))
            scores = jnp.where(causal, scores, -jnp.inf)
            attn = jax.nn.softmax(scores, axis=-1)
            out = jnp.einsum('bhqk,bhkd->bhqd', attn, v)
            out = out.transpose(0, 2, 1, 3).reshape(b, t, c)
            return out @ Wproj + bproj
        key = jax.random.key(seed)
        ks = jax.random.split(key, 12)
        s = 0.02
        return {'x': jax.random.normal(ks[0], (B, T, D), jnp.float32), 'condition': jax.random.normal(ks[1], (B, D), jnp.float32), 'Wqkv': jax.random.normal(ks[2], (D, 3 * D), jnp.float32) * s, 'Wproj': jax.random.normal(ks[3], (D, D), jnp.float32) * s, 'bproj': jnp.zeros((D,), jnp.float32), 'W1': jax.random.normal(ks[4], (D, HD), jnp.float32) * s, 'b1': jnp.zeros((HD,), jnp.float32), 'W2': jax.random.normal(ks[5], (HD, D), jnp.float32) * s, 'b2': jnp.zeros((D,), jnp.float32), 'g1': jnp.ones((D,), jnp.float32), 'be1': jnp.zeros((D,), jnp.float32), 'g2': jnp.ones((D,), jnp.float32), 'be2': jnp.zeros((D,), jnp.float32), 'Wada': jax.random.normal(ks[6], (D, 6 * D), jnp.float32) * s, 'bada': jax.random.normal(ks[7], (6 * D,), jnp.float32) * s}
    _L1_cond_all = _L1_cond_setup()
    _L1_cond_in = {k: v for k, v in _L1_cond_all.items() if k in ('Wqkv', 'Wproj', 'bproj', 'W1', 'b1', 'W2', 'b2', 'g1', 'be1', 'g2', 'be2', 'Wada', 'bada')}
    del _L1_cond_all

    def _L2_cond_setup():
        import jax, jax.numpy as jnp
        import numpy as np
        DIM = 128
        FF_MULT = 2
        EPS = 1e-06

        def _ln(x):
            mu = jnp.mean(x, axis=-1, keepdims=True)
            var = jnp.mean(jnp.square(x - mu), axis=-1, keepdims=True)
            return (x - mu) * jax.lax.rsqrt(var + EPS)
        key = jax.random.key(seed)
        ks = jax.random.split(key, 12)
        b, n, d = (4, 256, DIM)
        h = FF_MULT * d
        s = lambda fan_in: 1.0 / np.sqrt(fan_in)
        return {'x': jax.random.normal(ks[0], (b, n, d), jnp.float32), 't': jax.random.normal(ks[1], (b, d), jnp.float32), 'ada_w': jax.random.normal(ks[2], (d, 6 * d), jnp.float32) * s(d), 'ada_b': jnp.zeros((6 * d,), jnp.float32), 'ssm_w1': jax.random.normal(ks[3], (d, d), jnp.float32) * s(d), 'ssm_b1': jnp.zeros((d,), jnp.float32), 'ssm_w2': jax.random.normal(ks[4], (d, d), jnp.float32) * s(d), 'ssm_b2': jnp.zeros((d,), jnp.float32), 'ff_w1': jax.random.normal(ks[5], (d, h), jnp.float32) * s(d), 'ff_b1': jnp.zeros((h,), jnp.float32), 'ff_w2': jax.random.normal(ks[6], (h, d), jnp.float32) * s(h), 'ff_b2': jnp.zeros((d,), jnp.float32)}
    _L2_cond_all = _L2_cond_setup()
    _L2_cond_in = {k: v for k, v in _L2_cond_all.items() if k in ('ada_w', 'ada_b', 'ssm_w1', 'ssm_b1', 'ssm_w2', 'ssm_b2', 'ff_w1', 'ff_b1', 'ff_w2', 'ff_b2')}
    del _L2_cond_all

    def _L3_cond_setup():
        import jax, jax.numpy as jnp
        import numpy as np
        B, N, D, H = (4, 128, 128, 16)
        DFF = 4 * D
        GATE_SCALE = 0.1
        LN_EPS = 1e-05

        def _layernorm(v, g, b):
            mu = jnp.mean(v, axis=-1, keepdims=True)
            var = jnp.mean(jnp.square(v - mu), axis=-1, keepdims=True)
            return (v - mu) * jax.lax.rsqrt(var + LN_EPS) * g + b

        def _attention(y, qkv_w, qkv_b, proj_w, proj_b):
            Bq, Nq, C = y.shape
            dh = C // H
            qkv = (y @ qkv_w + qkv_b).reshape(Bq, Nq, 3, H, dh)
            q, k, v = jnp.moveaxis(qkv, 2, 0)
            scale = dh ** (-0.5)
            attn = jnp.einsum('bqhd,bkhd->bhqk', q, k) * scale
            attn = jax.nn.softmax(attn, axis=-1)
            out = jnp.einsum('bhqk,bkhd->bqhd', attn, v).reshape(Bq, Nq, C)
            return out @ proj_w + proj_b
        key = jax.random.key(seed)
        ks = jax.random.split(key, 32)
        s = 0.02

        def w(k, shape):
            return jax.random.normal(k, shape, dtype=jnp.float32) * s
        inp = {'x': jax.random.normal(ks[0], (B, N, D), dtype=jnp.float32), 'cond': jax.random.normal(ks[1], (B, D), dtype=jnp.float32), 'g1_w': w(ks[2], (D, D)), 'g1_b': w(ks[3], (D,)), 'b1_w': w(ks[4], (D, D)), 'b1_b': w(ks[5], (D,)), 'a1_w': w(ks[6], (D, D)), 'a1_b': w(ks[7], (D,)), 'g2_w': w(ks[8], (D, D)), 'g2_b': w(ks[9], (D,)), 'b2_w': w(ks[10], (D, D)), 'b2_b': w(ks[11], (D,)), 'a2_w': w(ks[12], (D, D)), 'a2_b': w(ks[13], (D,)), 'ln1_g': jnp.ones((D,), jnp.float32), 'ln1_b': jnp.zeros((D,), jnp.float32), 'ln2_g': jnp.ones((D,), jnp.float32), 'ln2_b': jnp.zeros((D,), jnp.float32), 'qkv_w': w(ks[14], (D, 3 * D)), 'qkv_b': w(ks[15], (3 * D,)), 'proj_w': w(ks[16], (D, D)), 'proj_b': w(ks[17], (D,)), 'fc1_w': w(ks[18], (D, DFF)), 'fc1_b': w(ks[19], (DFF,)), 'fc2_w': w(ks[20], (DFF, D)), 'fc2_b': w(ks[21], (D,))}
        return inp
    _L3_cond_all = _L3_cond_setup()
    _L3_cond_in = {k: v for k, v in _L3_cond_all.items() if k in ('g1_w', 'g1_b', 'b1_w', 'b1_b', 'a1_w', 'a1_b', 'g2_w', 'g2_b', 'b2_w', 'b2_b', 'a2_w', 'a2_b', 'ln1_g', 'ln1_b', 'ln2_g', 'ln2_b', 'qkv_w', 'qkv_b', 'proj_w', 'proj_b', 'fc1_w', 'fc1_b', 'fc2_w', 'fc2_b')}
    del _L3_cond_all
    return {'x': x, 'cond_1024': cond_1024, 'mask_BxSxSx11_ik0': mask_BxSxSx11_ik0, 'L0_cond_W_self': _L0_cond_in['W_self'], 'L0_cond_b_self': _L0_cond_in['b_self'], 'L0_cond_w_bias': _L0_cond_in['w_bias'], 'L0_cond_b_bias': _L0_cond_in['b_bias'], 'L0_cond_Wq': _L0_cond_in['Wq'], 'L0_cond_bq': _L0_cond_in['bq'], 'L0_cond_Wk': _L0_cond_in['Wk'], 'L0_cond_bk': _L0_cond_in['bk'], 'L0_cond_Wout': _L0_cond_in['Wout'], 'L0_cond_bout': _L0_cond_in['bout'], 'L1_cond_Wqkv': _L1_cond_in['Wqkv'], 'L1_cond_Wproj': _L1_cond_in['Wproj'], 'L1_cond_bproj': _L1_cond_in['bproj'], 'L1_cond_W1': _L1_cond_in['W1'], 'L1_cond_b1': _L1_cond_in['b1'], 'L1_cond_W2': _L1_cond_in['W2'], 'L1_cond_b2': _L1_cond_in['b2'], 'L1_cond_g1': _L1_cond_in['g1'], 'L1_cond_be1': _L1_cond_in['be1'], 'L1_cond_g2': _L1_cond_in['g2'], 'L1_cond_be2': _L1_cond_in['be2'], 'L1_cond_Wada': _L1_cond_in['Wada'], 'L1_cond_bada': _L1_cond_in['bada'], 'L2_cond_ada_w': _L2_cond_in['ada_w'], 'L2_cond_ada_b': _L2_cond_in['ada_b'], 'L2_cond_ssm_w1': _L2_cond_in['ssm_w1'], 'L2_cond_ssm_b1': _L2_cond_in['ssm_b1'], 'L2_cond_ssm_w2': _L2_cond_in['ssm_w2'], 'L2_cond_ssm_b2': _L2_cond_in['ssm_b2'], 'L2_cond_ff_w1': _L2_cond_in['ff_w1'], 'L2_cond_ff_b1': _L2_cond_in['ff_b1'], 'L2_cond_ff_w2': _L2_cond_in['ff_w2'], 'L2_cond_ff_b2': _L2_cond_in['ff_b2'], 'L3_cond_g1_w': _L3_cond_in['g1_w'], 'L3_cond_g1_b': _L3_cond_in['g1_b'], 'L3_cond_b1_w': _L3_cond_in['b1_w'], 'L3_cond_b1_b': _L3_cond_in['b1_b'], 'L3_cond_a1_w': _L3_cond_in['a1_w'], 'L3_cond_a1_b': _L3_cond_in['a1_b'], 'L3_cond_g2_w': _L3_cond_in['g2_w'], 'L3_cond_g2_b': _L3_cond_in['g2_b'], 'L3_cond_b2_w': _L3_cond_in['b2_w'], 'L3_cond_b2_b': _L3_cond_in['b2_b'], 'L3_cond_a2_w': _L3_cond_in['a2_w'], 'L3_cond_a2_b': _L3_cond_in['a2_b'], 'L3_cond_ln1_g': _L3_cond_in['ln1_g'], 'L3_cond_ln1_b': _L3_cond_in['ln1_b'], 'L3_cond_ln2_g': _L3_cond_in['ln2_g'], 'L3_cond_ln2_b': _L3_cond_in['ln2_b'], 'L3_cond_qkv_w': _L3_cond_in['qkv_w'], 'L3_cond_qkv_b': _L3_cond_in['qkv_b'], 'L3_cond_proj_w': _L3_cond_in['proj_w'], 'L3_cond_proj_b': _L3_cond_in['proj_b'], 'L3_cond_fc1_w': _L3_cond_in['fc1_w'], 'L3_cond_fc1_b': _L3_cond_in['fc1_b'], 'L3_cond_fc2_w': _L3_cond_in['fc2_w'], 'L3_cond_fc2_b': _L3_cond_in['fc2_b']}

def reference(x, cond_1024, mask_BxSxSx11_ik0, L0_cond_W_self, L0_cond_b_self, L0_cond_w_bias, L0_cond_b_bias, L0_cond_Wq, L0_cond_bq, L0_cond_Wk, L0_cond_bk, L0_cond_Wout, L0_cond_bout, L1_cond_Wqkv, L1_cond_Wproj, L1_cond_bproj, L1_cond_W1, L1_cond_b1, L1_cond_W2, L1_cond_b2, L1_cond_g1, L1_cond_be1, L1_cond_g2, L1_cond_be2, L1_cond_Wada, L1_cond_bada, L2_cond_ada_w, L2_cond_ada_b, L2_cond_ssm_w1, L2_cond_ssm_b1, L2_cond_ssm_w2, L2_cond_ssm_b2, L2_cond_ff_w1, L2_cond_ff_b1, L2_cond_ff_w2, L2_cond_ff_b2, L3_cond_g1_w, L3_cond_g1_b, L3_cond_b1_w, L3_cond_b1_b, L3_cond_a1_w, L3_cond_a1_b, L3_cond_g2_w, L3_cond_g2_b, L3_cond_b2_w, L3_cond_b2_b, L3_cond_a2_w, L3_cond_a2_b, L3_cond_ln1_g, L3_cond_ln1_b, L3_cond_ln2_g, L3_cond_ln2_b, L3_cond_qkv_w, L3_cond_qkv_b, L3_cond_proj_w, L3_cond_proj_b, L3_cond_fc1_w, L3_cond_fc1_b, L3_cond_fc2_w, L3_cond_fc2_b):
    import jax
    import jax.numpy as jnp

    def _L0_cond_ref(v, q, adj, W_self, b_self, w_bias, b_bias, Wq, bq, Wk, bk, Wout, bout):
        import jax, jax.numpy as jnp
        import numpy as np
        NONGT = 20
        H = 16
        NEG = -9000000000000000.0

        def _gat_attention(self_feat, cond_adj, label_bias, Wq, bq, Wk, bk, Wout, bout):
            B, N, F = self_feat.shape
            ng = min(NONGT, N)
            dh = F // H
            kv = self_feat[:, :ng]
            qh = (self_feat @ Wq.T + bq).reshape(B, N, H, dh)
            kh = (kv @ Wk.T + bk).reshape(B, ng, H, dh)
            aff = jnp.einsum('bnhd,bmhd->bnhm', qh, kh) * (1.0 / np.sqrt(dh))
            mask = cond_adj[:, :, None, :] > 0
            aff = jnp.where(mask, aff, NEG) + label_bias[:, :, None, :]
            w = jax.nn.softmax(aff, axis=-1)
            out_t = jnp.einsum('bnhm,bmf->bnhf', w, kv)
            out = jnp.einsum('bnhf,hgf->bnhg', out_t, Wout) + bout.reshape(H, F // H)
            return out.reshape(B, N, F)

        def _forward(v, q, adj, W_self, b_self, w_bias, b_bias, Wq, bq, Wk, bk, Wout, bout):
            adj_f = adj.astype(jnp.float32)
            exp_v = v
            row_zero = exp_v.sum(-1) == 0
            q_exp = jnp.where(row_zero[..., None], 0.0, q[:, None, :])
            vcq = jnp.concatenate([exp_v, q_exp], axis=-1)
            self_feat = vcq @ W_self.T + b_self
            output = self_feat
            for d in range(2):
                A = adj_f if d == 0 else jnp.swapaxes(adj_f, 1, 2)
                A = A[:, :, :NONGT, :]
                cond = A.sum(-1)
                vb = A @ w_bias + b_bias
                output = output + _gat_attention(self_feat, cond, vb, Wq[d], bq[d], Wk[d], bk[d], Wout[d], bout[d])
            rel = jax.nn.relu(output)
            return exp_v + rel
        return _forward(v, q, adj, W_self, b_self, w_bias, b_bias, Wq, bq, Wk, bk, Wout, bout)

    def _L1_cond_ref(x, condition, Wqkv, Wproj, bproj, W1, b1, W2, b2, g1, be1, g2, be2, Wada, bada):
        import jax, jax.numpy as jnp
        import numpy as np
        D = 128
        H = 16
        HD = 4 * D
        B, T = (4, 128)
        EPS = 1e-05

        def _layernorm(x, g, b):
            mu = jnp.mean(x, axis=-1, keepdims=True)
            var = jnp.mean(jnp.square(x - mu), axis=-1, keepdims=True)
            return (x - mu) * jax.lax.rsqrt(var + EPS) * g + b

        def _attention(x, Wqkv, Wproj, bproj):
            b, t, c = x.shape
            hd = c // H
            qkv = (x @ Wqkv).reshape(b, t, 3, H, hd).transpose(2, 0, 3, 1, 4)
            q, k, v = (qkv[0], qkv[1], qkv[2])
            scale = hd ** (-0.5)
            scores = jnp.einsum('bhqd,bhkd->bhqk', q, k) * scale
            causal = jnp.tril(jnp.ones((t, t), bool))
            scores = jnp.where(causal, scores, -jnp.inf)
            attn = jax.nn.softmax(scores, axis=-1)
            out = jnp.einsum('bhqk,bhkd->bhqd', attn, v)
            out = out.transpose(0, 2, 1, 3).reshape(b, t, c)
            return out @ Wproj + bproj
        mod = jax.nn.silu(condition) @ Wada + bada
        sh_a, sc_a, gt_a, sh_m, sc_m, gt_m = jnp.split(mod, 6, axis=1)
        xn = _layernorm(x, g1, be1)
        xm = xn * (1.0 + sc_a[:, None, :]) + sh_a[:, None, :]
        x = x + gt_a[:, None, :] * _attention(xm, Wqkv, Wproj, bproj)
        xn = _layernorm(x, g2, be2)
        xm = xn * (1.0 + sc_m[:, None, :]) + sh_m[:, None, :]
        h = jax.nn.gelu(xm @ W1 + b1, approximate=False)
        x = x + gt_m[:, None, :] * (h @ W2 + b2)
        return x

    def _L2_cond_ref(x, t, ada_w, ada_b, ssm_w1, ssm_b1, ssm_w2, ssm_b2, ff_w1, ff_b1, ff_w2, ff_b2):
        import jax, jax.numpy as jnp
        import numpy as np
        DIM = 128
        FF_MULT = 2
        EPS = 1e-06

        def _ln(x):
            mu = jnp.mean(x, axis=-1, keepdims=True)
            var = jnp.mean(jnp.square(x - mu), axis=-1, keepdims=True)
            return (x - mu) * jax.lax.rsqrt(var + EPS)
        emb = jnp.dot(jax.nn.silu(t), ada_w) + ada_b
        shift_msa, scale_msa, gate_msa, shift_mlp, scale_mlp, gate_mlp = jnp.split(emb, 6, axis=-1)
        norm = _ln(x) * (1.0 + scale_msa[:, None]) + shift_msa[:, None]
        h = jax.nn.gelu(jnp.dot(norm, ssm_w1) + ssm_b1, approximate=False)
        ssm_out = jnp.dot(h, ssm_w2) + ssm_b2
        x = x + gate_msa[:, None] * ssm_out
        norm2 = _ln(x) * (1.0 + scale_mlp[:, None]) + shift_mlp[:, None]
        hf = jax.nn.gelu(jnp.dot(norm2, ff_w1) + ff_b1, approximate=True)
        ff_out = jnp.dot(hf, ff_w2) + ff_b2
        x = x + gate_mlp[:, None] * ff_out
        return x

    def _L3_cond_ref(x, cond, g1_w, g1_b, b1_w, b1_b, a1_w, a1_b, g2_w, g2_b, b2_w, b2_b, a2_w, a2_b, ln1_g, ln1_b, ln2_g, ln2_b, qkv_w, qkv_b, proj_w, proj_b, fc1_w, fc1_b, fc2_w, fc2_b):
        import jax, jax.numpy as jnp
        import numpy as np
        B, N, D, H = (4, 128, 128, 16)
        DFF = 4 * D
        GATE_SCALE = 0.1
        LN_EPS = 1e-05

        def _layernorm(v, g, b):
            mu = jnp.mean(v, axis=-1, keepdims=True)
            var = jnp.mean(jnp.square(v - mu), axis=-1, keepdims=True)
            return (v - mu) * jax.lax.rsqrt(var + LN_EPS) * g + b

        def _attention(y, qkv_w, qkv_b, proj_w, proj_b):
            Bq, Nq, C = y.shape
            dh = C // H
            qkv = (y @ qkv_w + qkv_b).reshape(Bq, Nq, 3, H, dh)
            q, k, v = jnp.moveaxis(qkv, 2, 0)
            scale = dh ** (-0.5)
            attn = jnp.einsum('bqhd,bkhd->bhqk', q, k) * scale
            attn = jax.nn.softmax(attn, axis=-1)
            out = jnp.einsum('bhqk,bkhd->bqhd', attn, v).reshape(Bq, Nq, C)
            return out @ proj_w + proj_b
        gamma1 = cond @ g1_w + g1_b
        beta1 = cond @ b1_w + b1_b
        alpha1 = jnp.tanh(cond @ a1_w + a1_b) * GATE_SCALE
        gamma2 = cond @ g2_w + g2_b
        beta2 = cond @ b2_w + b2_b
        alpha2 = jnp.tanh(cond @ a2_w + a2_b) * GATE_SCALE
        y = _layernorm(x, ln1_g, ln1_b)
        y = y * (1.0 + gamma1[:, None, :]) + beta1[:, None, :]
        y = _attention(y, qkv_w, qkv_b, proj_w, proj_b)
        x = x + y * alpha1[:, None, :]
        z = _layernorm(x, ln2_g, ln2_b)
        z = z * (1.0 + gamma2[:, None, :]) + beta2[:, None, :]
        z = jax.nn.gelu(z @ fc1_w + fc1_b, approximate=False) @ fc2_w + fc2_b
        x = x + z * alpha2[:, None, :]
        return x
    x = _L0_cond_ref(x, cond_1024, mask_BxSxSx11_ik0, L0_cond_W_self, L0_cond_b_self, L0_cond_w_bias, L0_cond_b_bias, L0_cond_Wq, L0_cond_bq, L0_cond_Wk, L0_cond_bk, L0_cond_Wout, L0_cond_bout)
    x = _L1_cond_ref(x, cond_1024, L1_cond_Wqkv, L1_cond_Wproj, L1_cond_bproj, L1_cond_W1, L1_cond_b1, L1_cond_W2, L1_cond_b2, L1_cond_g1, L1_cond_be1, L1_cond_g2, L1_cond_be2, L1_cond_Wada, L1_cond_bada)
    x = _L2_cond_ref(x, cond_1024, L2_cond_ada_w, L2_cond_ada_b, L2_cond_ssm_w1, L2_cond_ssm_b1, L2_cond_ssm_w2, L2_cond_ssm_b2, L2_cond_ff_w1, L2_cond_ff_b1, L2_cond_ff_w2, L2_cond_ff_b2)
    x = _L3_cond_ref(x, cond_1024, L3_cond_g1_w, L3_cond_g1_b, L3_cond_b1_w, L3_cond_b1_b, L3_cond_a1_w, L3_cond_a1_b, L3_cond_g2_w, L3_cond_g2_b, L3_cond_b2_w, L3_cond_b2_b, L3_cond_a2_w, L3_cond_a2_b, L3_cond_ln1_g, L3_cond_ln1_b, L3_cond_ln2_g, L3_cond_ln2_b, L3_cond_qkv_w, L3_cond_qkv_b, L3_cond_proj_w, L3_cond_proj_b, L3_cond_fc1_w, L3_cond_fc1_b, L3_cond_fc2_w, L3_cond_fc2_b)
    return x

_drawn_inputs = setup_inputs


def setup_inputs(seed=0):
    import zlib

    import numpy as np

    out = dict(_drawn_inputs(seed))
    spreads = {'L0_cond_b_self': (0.0, 0.1),
     'L0_cond_bq': (0.0, 0.1),
     'L0_cond_bk': (0.0, 0.1),
     'L0_cond_bout': (0.0, 0.1),
     'L1_cond_bproj': (0.0, 0.653),
     'L1_cond_b1': (0.0, 0.8),
     'L1_cond_b2': (0.0, 0.635),
     'L1_cond_g1': (1.0, 0.6),
     'L1_cond_be1': (0.0, 0.8),
     'L1_cond_g2': (1.0, 0.6),
     'L1_cond_be2': (0.0, 0.8),
     'L2_cond_ada_b': (0.0, 0.1),
     'L2_cond_ssm_b1': (0.0, 0.647),
     'L2_cond_ssm_b2': (0.0, 0.466),
     'L2_cond_ff_b1': (0.0, 0.789),
     'L2_cond_ff_b2': (0.0, 0.594),
     'L3_cond_ln1_g': (1.0, 0.6),
     'L3_cond_ln1_b': (0.0, 0.8),
     'L3_cond_ln2_g': (1.0, 0.6),
     'L3_cond_ln2_b': (0.0, 0.8)}
    factors = {'L1_cond_Wqkv': 8.0,
     'L1_cond_Wproj': 8.0,
     'L1_cond_W1': 7.803,
     'L1_cond_W2': 7.123,
     'L1_cond_Wada': 2.887,
     'L1_cond_bada': 8.0,
     'L3_cond_g1_w': 8.0,
     'L3_cond_g1_b': 8.0,
     'L3_cond_b1_w': 8.0,
     'L3_cond_b1_b': 22.125,
     'L3_cond_a1_w': 8.0,
     'L3_cond_a1_b': 8.0,
     'L3_cond_g2_w': 8.0,
     'L3_cond_g2_b': 8.0,
     'L3_cond_b2_w': 8.0,
     'L3_cond_b2_b': 31.85,
     'L3_cond_a2_w': 8.0,
     'L3_cond_a2_b': 8.0,
     'L3_cond_qkv_w': 8.0,
     'L3_cond_qkv_b': 39.83,
     'L3_cond_proj_w': 8.0,
     'L3_cond_proj_b': 64.0,
     'L3_cond_fc1_w': 8.0,
     'L3_cond_fc1_b': 62.894,
     'L3_cond_fc2_w': 8.0,
     'L3_cond_fc2_b': 64.0}
    for name, (base, spread) in spreads.items():
        noise = np.random.default_rng([zlib.crc32(name.encode()), seed]).standard_normal(out[name].shape)
        drawn = base * np.exp(spread * noise) if base else spread * noise
        out[name] = jnp.asarray(drawn.astype(out[name].dtype))
    for name, factor in factors.items():
        out[name] = (out[name] * factor).astype(out[name].dtype)
    return out
```

```python
from contextlib import ExitStack

import numpy as np

import concourse.bass as bass
from concourse import mybir

F32 = mybir.dt.float32
BF16 = mybir.dt.bfloat16
I32 = mybir.dt.int32
ALU = mybir.AluOpType
ACT = mybir.ActivationFunctionType
AX_X = mybir.AxisListType.X

P = 128
B, S, D = 128, 32, 128
L = 11
NONGT = 20
H, HD = 16, 8
GH = 4
NG = H // GH
STREAMS = 2
T = 4
BT = P // S
NB = T * BT
C = T * P
NIT = B * S // (C * STREAMS)
VW = GH * HD + GH
SCALE = float(HD) ** -0.5
NEG = 9000000000000000.0
CAUSAL = -float(2 ** 100)
PAIRS = 2

BLOCKS = [
    ("attn", 1, 0, None),
    ("mlp", 1, 4, "Gelu"),
    ("mlp", 2, 1, "Gelu"),
    ("mlp", 2, 2, "Gelu_apprx_tanh"),
    ("attn", 3, 0, None),
    ("mlp", 3, 4, "Gelu"),
]
NBLK = len(BLOCKS)
EPS = [1e-5, 1e-5, 1e-6, 1e-6, 1e-5, 1e-5]

VECTORS = [
    ("L0_cond_b_self", 1), ("L0_cond_bq", 2), ("L0_cond_bk", 2),
    ("L1_cond_bproj", 1), ("L1_cond_b1", 4), ("L1_cond_b2", 1), ("L1_cond_g1", 1), ("L1_cond_be1", 1),
    ("L1_cond_g2", 1), ("L1_cond_be2", 1), ("L1_cond_bada", 6),
    ("L2_cond_ada_b", 6), ("L2_cond_ssm_b1", 1), ("L2_cond_ssm_b2", 1), ("L2_cond_ff_b1", 2), ("L2_cond_ff_b2", 1),
    ("L3_cond_g1_b", 1), ("L3_cond_b1_b", 1), ("L3_cond_a1_b", 1), ("L3_cond_g2_b", 1), ("L3_cond_b2_b", 1),
    ("L3_cond_a2_b", 1), ("L3_cond_ln1_g", 1), ("L3_cond_ln1_b", 1), ("L3_cond_ln2_g", 1), ("L3_cond_ln2_b", 1),
    ("L3_cond_qkv_b", 3), ("L3_cond_proj_b", 1), ("L3_cond_fc1_b", 4), ("L3_cond_fc2_b", 1),
]
ROW = {}
NROWS = 0
for _name, _k in VECTORS:
    ROW[_name] = NROWS
    NROWS += _k

DIRECT = [
    ("L1_cond_Wqkv", 1, 384), ("L1_cond_Wproj", 1, 128), ("L1_cond_W1", 1, 512), ("L1_cond_W2", 4, 128),
    ("L2_cond_ssm_w1", 1, 128), ("L2_cond_ssm_w2", 1, 128), ("L2_cond_ff_w1", 1, 256), ("L2_cond_ff_w2", 2, 128),
    ("L3_cond_qkv_w", 1, 384), ("L3_cond_proj_w", 1, 128), ("L3_cond_fc1_w", 1, 512), ("L3_cond_fc2_w", 4, 128),
]
MODW = [("L1_cond_Wada", 6), ("L2_cond_ada_w", 6), ("L3_cond_g1_w", 1), ("L3_cond_b1_w", 1), ("L3_cond_a1_w", 1),
        ("L3_cond_g2_w", 1), ("L3_cond_b2_w", 1), ("L3_cond_a2_w", 1)]

ATTN_OF_BLOCK = {0: 2, 4: 3}
NATT = 4


def list_fills():
    names = ["xT", "qcT", "self", "bias0", "bias1"]
    for d in range(2):
        names += [f"q a{d}", f"k a{d}", f"v a{d}", f"o01 a{d}", f"o23 a{d}"]
    names += ["self01", "self23"]
    for j, (kind, _, hidden, _) in enumerate(BLOCKS):
        names.append(f"xn{j}")
        if kind == "attn":
            a = ATTN_OF_BLOCK[j]
            names += [f"q a{a}", f"k a{a}", f"v a{a}", f"o01 a{a}", f"o23 a{a}", f"oT a{a}"]
        else:
            names += [f"h{j}.{u}" for u in range(hidden)]
        names += [f"y{j}", f"yT{j}"]
    return names


FILLS = list_fills()
NF = len(FILLS)
FILL = {name: n for n, name in enumerate(FILLS)}
assert NF % 2 == 0
HIDDEN_BEFORE = [sum(b[2] for b in BLOCKS[:j]) for j in range(NBLK + 1)]
NHID = HIDDEN_BEFORE[-1]


def list_stages():
    stages = [("graph_in", 0), ("graph_bias", 0)]
    for d in range(2):
        stages += [("qkv", d), ("softmax", d), ("values", d)]
    stages.append(("graph_out", 0))
    for j, (kind, *_rest) in enumerate(BLOCKS):
        stages += [("stats", j), ("norm", j), ("modulate", j)]
        if kind == "attn":
            a = ATTN_OF_BLOCK[j]
            stages += [("qkv", a), ("softmax", a), ("values", a), ("project", j)]
        else:
            stages += [("hidden", j), ("down", j)]
        stages.append(("residual", j))
    stages.append(("store", 0))
    return stages


STAGES = list_stages()
LAG = 6


def order():
    out = []
    for n in range(len(STAGES) + LAG):
        if n < len(STAGES):
            out.append((*STAGES[n], 0))
        if n >= LAG:
            out.append((*STAGES[n - LAG], 1))
    return out


ORDER = order()


USES = [(a, s) for kind, a, s in ORDER if kind == "softmax"]
SLOT = {use: n for n, use in enumerate(USES)}
assert USES[-1][0] == NATT - 1
NSLOT = len(SLOT)


def build(nc, t_in, out):
    with ExitStack() as ctx:
        def sb(name, shape, dt=F32):
            return ctx.enter_context(nc.sbuf_tensor(name, shape, dt))

        def sem(name):
            return ctx.enter_context(nc.semaphore(name))

        def per_stream(make, name, *args):
            return [make(f"{name}_{s}", *args) for s in range(STREAMS)]

        ident = sb("ident", [P, P])
        ident16 = sb("ident16", [P, P], BF16)
        spread = sb("spread", [P, BT, GH, S])
        col_i = sb("col_i", [P, P], I32)
        part_i = sb("part_i", [P, P], I32)
        col = sb("col", [P, P])
        part = sb("part", [P, P])
        part32 = sb("part32", [P, S])
        quad = sb("quad", [P, S])
        later = sb("later", [P, S])
        head_lo = sb("head_lo", [P, GH])
        head_hi = sb("head_hi", [P, GH])
        qmask = sb("qmask", [P, GH])
        vcol = sb("vcol", [P, GH, HD])
        vmask = sb("vmask", [P, GH, HD])
        causal = sb("causal", [P, S], BF16)
        neg_half = sb("neg_half", [P, T])
        wait_slot = sb("wait_slot", [P, 1])
        zero_col = sb("zero_col", [P, 1])
        rows = sb("rows", [NROWS, D])
        cols = sb("cols", [P, NROWS])
        qb_col = sb("qb_col", [P, NATT])
        wb = sb("wb", [P, L])
        bb = sb("bb", [P, 1])
        bout = sb("bout", [P, 2, D])
        bout_sum = sb("bout_sum", [P, D])
        w = {name: sb(f"w_{name}", [P, k, n]) for name, k, n in DIRECT}
        wT = sb("wT", [P, 8, D])
        cond_in = sb("cond_in", [P, D])
        condT = sb("condT", [P, B])
        siluT = sb("siluT", [P, B])
        sig = sb("sig", [P, B])
        mod = sb("mod", [P, 3 * NBLK, B])

        x_in = per_stream(sb, "x_in", [P, T, D])
        q_in = per_stream(sb, "q_in", [P, T, D])
        adj = per_stream(sb, "adj", [P, T * S, L], I32)
        u_sum = per_stream(sb, "u_sum", [P, T * S])
        c_sum = per_stream(sb, "c_sum", [P, T * S])
        edge = per_stream(sb, "edge", [P, 2, T, S])
        bias = per_stream(sb, "bias", [P, 2, NB, NONGT])
        row_sum = per_stream(sb, "row_sum", [P, T])
        row_flag = per_stream(sb, "row_flag", [P, T])
        x = per_stream(sb, "x", [P, T, D])
        xn = per_stream(sb, "xn", [P, T, D])
        xm0 = per_stream(sb, "xm0", [P, C])
        xm = per_stream(sb, "xm", [P, C])
        xT = xm0
        sfT = xm
        stats = per_stream(sb, "stats", [P, T, 6])
        mv = per_stream(sb, "mv", [P, T, 2])
        veps = per_stream(sb, "veps", [P, T])
        rstd = per_stream(sb, "rstd", [P, T])
        modc = per_stream(sb, "modc", [P, 3 * NBLK, NB])
        qT = per_stream(sb, "qT", [P, C])
        kT = per_stream(sb, "kT", [P, C])
        qbd = per_stream(sb, "qbd", [P, NB, GH, S])
        v = per_stream(sb, "v", [P, T, D])
        vrep = per_stream(sb, "vrep", [P, T, BT, D])
        adj_w = [r[:].rearrange("p t b f -> p (t b f)")[:, 0:T * S * L].rearrange("p (m l) -> p m l", l=L) for r in vrep]
        vbd = per_stream(sb, "vbd", [P, NB, NG, VW])
        prob_g = per_stream(sb, "prob_g", [P, NG, NB, S])
        prob = per_stream(sb, "prob", [P, NG, NB, S])
        probT = [q[:].rearrange("p b h n -> p (b h n)").rearrange("p (g b n) -> p g b n", g=NG, n=S) for q in qbd]
        mx = per_stream(sb, "mx", [P, NG, NB])
        recip = per_stream(sb, "recip", [P, T * NG, GH])
        o = [per_stream(sb, "o0", [P, T, D]), xn]
        oT = per_stream(sb, "oT", [P, C])
        qcT = oT
        yT = [a[:].rearrange("p t f -> p (t f)") for a in v]
        hT = [[prob[s][:, u].rearrange("p b m -> p (b m)") for u in range(4)] for s in range(STREAMS)]

        flat = [q[:].rearrange("p b h n -> p (b h n)") for q in qbd]
        flat += [q[:].rearrange("p g b m -> p (g b m)") for q in prob]
        wmod, place = {}, {"L1_cond_Wada": (0, 0), "L2_cond_ada_w": (0, 6 * D)}
        for n_, (name_, _) in enumerate(MODW[2:]):
            place[name_] = (1, n_ * D)
        for name_, k_ in MODW:
            i_, at_ = place[name_]
            wmod[name_] = flat[i_][:, at_:at_ + k_ * D]
        raw = flat[2][:, 0:8 * D].rearrange("p (a i) -> p a i", a=8)
        sc1 = flat[3][:, 0:NBLK * B].rearrange("p (j b) -> p j b", j=NBLK)
        alpha = flat[3][:, NBLK * B:(NBLK + 2) * B].rearrange("p (j b) -> p j b", j=2)

        work = [[ctx.enter_context(nc.psum_tensor(f"work_{s}{i}", [P, C], F32)) for i in range(2)]
                for s in range(STREAMS)]
        score = ctx.enter_context(nc.psum_tensor("score", [P, NG, NB * S], F32))

        vec_loaded = sem("vec_loaded")
        bcast_loaded = sem("bcast_loaded")
        raw_loaded = sem("raw_loaded")
        wmod_loaded = sem("wmod_loaded")
        w_loaded = sem("w_loaded")
        const_step = sem("const_step")
        masks_step = sem("masks_step")
        spread_ready = sem("spread_ready")
        setup_filled = sem("setup_filled")
        cond_ready = sem("cond_ready")
        cols_ready = sem("cols_ready")
        sig_ready = sem("sig_ready")
        silu_ready = sem("silu_ready")
        wT_ready = sem("wT_ready")
        sc1_ready = sem("sc1_ready")
        alpha_ready = sem("alpha_ready")
        mod_ready = sem("mod_ready")
        x_loaded = per_stream(sem, "x_loaded")
        q_loaded = per_stream(sem, "q_loaded")
        adj_loaded = per_stream(sem, "adj_loaded")
        v_spread = per_stream(sem, "v_spread")
        x_stored = per_stream(sem, "x_stored")
        filled = per_stream(sem, "filled")
        xT_ready = per_stream(sem, "xT_ready")
        qcT_ready = per_stream(sem, "qcT_ready")
        sf_ready = per_stream(sem, "sf_ready")
        bias_ready = per_stream(sem, "bias_ready")
        q_ready = per_stream(sem, "q_ready")
        k_ready = per_stream(sem, "k_ready")
        v_ready = per_stream(sem, "v_ready")
        qbd_ready = per_stream(sem, "qbd_ready")
        vbd_ready = per_stream(sem, "vbd_ready")
        exped = per_stream(sem, "exped")
        oT_ready = per_stream(sem, "oT_ready")
        h_ready = per_stream(sem, "h_ready")
        flag_ready = per_stream(sem, "flag_ready")
        rsum_ready = per_stream(sem, "rsum_ready")
        qm_ready = per_stream(sem, "qm_ready")
        adjw_ready = per_stream(sem, "adjw_ready")
        edge_step = per_stream(sem, "edge_step")
        edge_ready = per_stream(sem, "edge_ready")
        biased = per_stream(sem, "biased")
        maxed = per_stream(sem, "maxed")
        shifted = per_stream(sem, "shifted")
        turned = per_stream(sem, "turned")
        recip_ready = per_stream(sem, "recip_ready")
        o_ready = per_stream(sem, "o_ready")
        osum_step = per_stream(sem, "osum_step")
        out_step = per_stream(sem, "out_step")
        x_ready = per_stream(sem, "x_ready")
        stats_ready = per_stream(sem, "stats_ready")
        mv_ready = per_stream(sem, "mv_ready")
        veps_ready = per_stream(sem, "veps_ready")
        rstd_ready = per_stream(sem, "rstd_ready")
        xn_ready = per_stream(sem, "xn_ready")
        scaled = per_stream(sem, "scaled")
        xm_ready = per_stream(sem, "xm_ready")
        modc_ready = per_stream(sem, "modc_ready")
        y_ready = per_stream(sem, "y_ready")
        scored = sem("scored")

        x_tok = t_in["x"].rearrange("b n f -> (b n) f").rearrange("(c t p) f -> c p t f", t=T, p=P)
        out_tok = out.rearrange("b n f -> (b n) f").rearrange("(c t p) f -> c p t f", t=T, p=P)
        adj_tok = t_in["mask_BxSxSx11_ik0"].rearrange("b n m l -> (b n) (m l)").rearrange(
            "(c t p) e -> c p t e", t=T, p=P)
        cond_tok = t_in["cond_1024"].rearrange("(c t b) f -> c b t f", t=T, b=BT)

        def vec(name, k=0):
            return cols[:, ROW[name] + k:ROW[name] + k + 1]

        def bank(s, name):
            return work[s][FILL[name] % 2]

        def count(it, per, k):
            return it * per + k

        def await_fill(eng, it, s, name):
            eng.wait_ge(filled[s], count(it, NF, FILL[name] + 1))

        def await_x(eng, it, s, k):
            eng.wait_ge(x_ready[s], count(it, NBLK + 1, k + 1))

        read_by = {"xT": (xT_ready, 1, 1), "qcT": (qcT_ready, 1, 1), "self": (sf_ready, 1, 1),
                   "bias0": (bias_ready, 2, 1), "bias1": (bias_ready, 2, 2),
                   "self01": (out_step, 2, 1), "self23": (out_step, 2, 2)}
        for a_ in range(NATT):
            read_by[f"q a{a_}"] = (q_ready, NATT, a_ + 1)
            read_by[f"k a{a_}"] = (k_ready, NATT, a_ + 1)
            read_by[f"v a{a_}"] = (v_ready, NATT, a_ + 1)
            read_by[f"o01 a{a_}"] = (o_ready, 2 * NATT, 2 * a_ + 1)
            read_by[f"o23 a{a_}"] = (o_ready, 2 * NATT, 2 * a_ + 2)
        for j_, a_ in ATTN_OF_BLOCK.items():
            read_by[f"oT a{a_}"] = (oT_ready, 2, a_ - 1)
        for j_ in range(NBLK):
            read_by[f"xn{j_}"] = (scaled, NBLK, j_ + 1)
            read_by[f"y{j_}"] = (y_ready, NBLK, j_ + 1)
            read_by[f"yT{j_}"] = (x_ready, NBLK + 1, j_ + 3)
            for u_ in range(BLOCKS[j_][2]):
                read_by[f"h{j_}.{u_}"] = (h_ready, NHID, HIDDEN_BEFORE[j_] + u_ + 1)

        def await_bank(eng, it, s, name):
            n = FILL[name]
            if n < 2:
                await_x(eng, it, s, 0)
            else:
                signal, per, k = read_by[FILLS[n - 2]]
                eng.wait_ge(signal[s], count(it, per, k))

        def await_score_bank(eng, it, a, s, pair):
            n = SLOT[a, s]
            pa, ps = USES[n - 1]
            if n == 0:
                await_x(eng, it, ps, 0)
            elif pa < 2:
                eng.wait_ge(biased[ps], count(it, 2 * PAIRS, pa * PAIRS + pair + 1))
            else:
                eng.wait_ge(shifted[ps], count(it, NATT * PAIRS, pa * PAIRS + pair + 1))

        def await_pair(eng, it, a, s, pair):
            eng.wait_ge(scored, count(it, NSLOT * PAIRS, SLOT[a, s] * PAIRS + pair + 1))

        def q_weight(a):
            return {0: wT[:, 2, :], 1: wT[:, 3, :], 2: w["L1_cond_Wqkv"][:, 0, 0:D],
                    3: w["L3_cond_qkv_w"][:, 0, 0:D]}[a]

        def k_weight(a):
            return {0: wT[:, 4, :], 1: wT[:, 5, :], 2: w["L1_cond_Wqkv"][:, 0, D:2 * D],
                    3: w["L3_cond_qkv_w"][:, 0, D:2 * D]}[a]

        def v_weight(a):
            return {0: wT[:, 6, :], 1: wT[:, 7, :], 2: w["L1_cond_Wqkv"][:, 0, 2 * D:3 * D],
                    3: w["L3_cond_qkv_w"][:, 0, 2 * D:3 * D]}[a]

        def modw(j):
            layer, second = BLOCKS[j][1], j % 2
            if layer == 3:
                n = ("g2", "b2", "a2") if second else ("g1", "b1", "a1")
                return [wmod[f"L3_cond_{q}_w"] for q in n]
            m = wmod["L1_cond_Wada" if layer == 1 else "L2_cond_ada_w"]
            return [m[:, (3 * second + k) * D:(3 * second + k + 1) * D] for k in (1, 0, 2)]

        def modb(j):
            layer, second = BLOCKS[j][1], j % 2
            if layer == 3:
                n = ("g2", "b2", "a2") if second else ("g1", "b1", "a1")
                return [vec(f"L3_cond_{q}_b") for q in n]
            m = "L1_cond_bada" if layer == 1 else "L2_cond_ada_b"
            return [vec(m, 3 * second + k) for k in (1, 0, 2)]

        GAIN = {0: ("L1_cond_g1", "L1_cond_be1"), 1: ("L1_cond_g2", "L1_cond_be2"),
                4: ("L3_cond_ln1_g", "L3_cond_ln1_b"), 5: ("L3_cond_ln2_g", "L3_cond_ln2_b")}
        OUT_BIAS = ["L1_cond_bproj", "L1_cond_b2", "L2_cond_ssm_b2", "L2_cond_ff_b2", "L3_cond_proj_b",
                    "L3_cond_fc2_b"]
        HID_BIAS = [None, "L1_cond_b1", "L2_cond_ssm_b1", "L2_cond_ff_b1", None, "L3_cond_fc1_b"]
        UP = [None, "L1_cond_W1", "L2_cond_ssm_w1", "L2_cond_ff_w1", None, "L3_cond_fc1_w"]
        DOWN = [None, "L1_cond_W2", "L2_cond_ssm_w2", "L2_cond_ff_w2", None, "L3_cond_fc2_w"]
        PROJ = {0: "L1_cond_Wproj", 4: "L3_cond_proj_w"}

        SETUP_BANKS = [work[0][0], work[0][1], work[1][0], work[1][1], score[:, 0], score[:, 1],
                       score[:, 2], score[:, 3], work[0][0]]

        block = ctx.enter_context(nc.Block())

        @block.sync
        def _(sp):
            def load_inputs(c, s):
                sp.dma_start(x_in[s][:], x_tok[c]).then_inc(x_loaded[s], 16)
                for b in range(BT):
                    src = cond_tok[c, b].unsqueeze(0).broadcast_to([S, T, D])
                    sp.dma_start(q_in[s][S * b:S * b + S], src).then_inc(q_loaded[s], 16)
                sp.dma_start(adj[s][:].rearrange("p (t m) l -> p t (m l)", t=T), adj_tok[c]).then_inc(adj_loaded[s], 16)

            sp.dma_start(cond_in[:], t_in["cond_1024"]).then_inc(vec_loaded, 16)
            for name, k in VECTORS:
                src = t_in[name]
                if len(src.shape) == 2:
                    src = src.rearrange("a n -> (a n)")
                sp.dma_start(rows[ROW[name]:ROW[name] + k, :], src.rearrange("(k n) -> k n", k=k)).then_inc(vec_loaded, 16)
            sp.dma_start(raw[:, 0:2, :], t_in["L0_cond_W_self"].rearrange("f (a i) -> f a i", a=2)).then_inc(raw_loaded, 16)
            sp.dma_start(raw[:, 2:4, :], t_in["L0_cond_Wq"].rearrange("a f i -> f a i")).then_inc(raw_loaded, 16)
            sp.dma_start(raw[:, 4:6, :], t_in["L0_cond_Wk"].rearrange("a f i -> f a i")).then_inc(raw_loaded, 16)
            sp.dma_start(raw[:, 6:8, :], t_in["L0_cond_Wout"].rearrange("a h g f -> (h g) a f")).then_inc(raw_loaded, 16)
            for name, k in MODW:
                sp.dma_start(wmod[name], t_in[name]).then_inc(wmod_loaded, 16)
            for s in range(STREAMS):
                load_inputs(s, s)
            for name, k, n in DIRECT:
                sp.dma_start(w[name][:], t_in[name].rearrange("(k p) n -> p k n", p=P)).then_inc(w_loaded, 16)

            for s in range(STREAMS):
                sp.sem_inc(x_stored[s], 16)

            with sp.Fori(0, NIT) as it:
                for kind, a, s in ORDER:
                    if kind == "values":
                        sp.wait_ge(v_ready[s], count(it, NATT, a + 1))
                        for b in range(BT):
                            for h in range(GH):
                                sp.dma_start(vrep[s][S * h:S * h + S, :, b, :],
                                             v[s][S * b:S * b + S]).then_inc(v_spread[s], 16)
                    if kind == "stats" and a == 0:
                        await_x(sp, it, s, 1)
                        load_inputs((it * STREAMS + STREAMS + s) % (NIT * STREAMS), s)
                    if kind == "store":
                        await_x(sp, it, s, NBLK + 1)
                        sp.dma_start(out_tok[it * STREAMS + s], x[s][:]).then_inc(x_stored[s], 16)
            for s in range(STREAMS):
                sp.wait_ge(x_stored[s], 16 * (NIT + 1))
                sp.wait_ge(x_loaded[s], 16 * (NIT + 1))
                sp.wait_ge(q_loaded[s], 16 * BT * (NIT + 1))
                sp.wait_ge(adj_loaded[s], 16 * (NIT + 1))

        @block.gpsimd
        def _(pool):
            pool.dma_start(wb[:], t_in["L0_cond_w_bias"].unsqueeze(0).broadcast_to([P, L])).then_inc(bcast_loaded, 16)
            pool.dma_start(bb[:], t_in["L0_cond_b_bias"].rearrange("(a b) -> a b", a=1).broadcast_to([P, 1])).then_inc(bcast_loaded, 16)
            pool.dma_start(bout[:].rearrange("p a f -> p (a f)"),
                           t_in["L0_cond_bout"].rearrange("a f -> (a f)").unsqueeze(0).broadcast_to([P, 2 * D])
                           ).then_inc(bcast_loaded, 16)
            pool.memset(ident[:], 0.0).then_inc(const_step, 1)
            pool.iota(col_i[:], [[1, P]], base=0, channel_multiplier=0).then_inc(const_step, 1)
            pool.iota(part_i[:], [[0, P]], base=0, channel_multiplier=1).then_inc(const_step, 1)
            pool.memset(neg_half[:], -0.5).then_inc(const_step, 1)
            pool.memset(zero_col[:], 0.0).then_inc(const_step, 1)
            pool.wait_ge(const_step, 1)
            pool.affine_select(out=ident[:], in_=ident[:], compare_op=ALU.not_equal, fill=1.0, base=0,
                               pattern=[[-1, P]], channel_multiplier=1).then_inc(const_step, 1)
            for s in range(STREAMS):
                pool.memset(prob_g[s][:], 0.0).then_inc(const_step, 1)
            pool.wait_ge(masks_step, 10)
            for s in range(STREAMS):
                pool.tensor_copy(vbd[s][:, :, :, GH * HD:VW].rearrange("p b g h -> p (b g) h"),
                                 vmask[:, :, 0].unsqueeze(1).broadcast_to([P, NB * NG, GH])).then_inc(const_step, 1)
            pool.wait_ge(bcast_loaded, 16 * 3)
            pool.tensor_tensor(bout_sum[:], bout[:, 0], bout[:, 1], ALU.add).then_inc(const_step, 1)
            pool.wait_ge(sig_ready, 1)
            pool.tensor_tensor(siluT[:], condT[:], sig[:], ALU.mult).then_inc(silu_ready, 1)
            pool.wait_ge(const_step, 11)
            pool.wait_ge(mod_ready, NBLK)

            with pool.Fori(0, NIT) as it:
                for kind, a, s in ORDER:
                    if kind == "graph_in":
                        pool.tensor_copy(modc[s][:], mod[:, :, bass.ds(it * (STREAMS * NB) + s * NB, NB)]
                                         ).then_inc(modc_ready[s], 1)
                        pool.wait_ge(q_loaded[s], count(it, 16 * BT, 16 * BT))
                        pool.wait_ge(flag_ready[s], count(it, 1, 1))
                        pool.tensor_tensor(q_in[s][:], q_in[s][:], row_flag[s][:].unsqueeze(2).broadcast_to([P, T, D]),
                                           ALU.mult).then_inc(qm_ready[s], 1)
                    if kind == "qkv":
                        pool.wait_ge(q_ready[s], count(it, NATT, a + 1))
                        pool.tensor_tensor(qbd[s][:],
                                           qT[s][:].rearrange("p (b n) -> p b n", n=S).unsqueeze(2).broadcast_to([P, NB, GH, S]),
                                           qmask[:].unsqueeze(1).unsqueeze(3).broadcast_to([P, NB, GH, S]),
                                           ALU.mult).then_inc(qbd_ready[s], 1)
                    if kind == "values":
                        pool.wait_ge(v_spread[s], count(it, 16 * BT * GH * NATT, 16 * BT * GH * (a + 1)))
                        pool.tensor_tensor(vbd[s][:, :, :, 0:GH * HD].rearrange("p b g c -> p (b g) c"),
                                           vrep[s][:].rearrange("p t b (g c) -> p (t b g) c", g=NG),
                                           vmask[:].rearrange("p h d -> p (h d)").unsqueeze(1).broadcast_to([P, NB * NG, GH * HD]),
                                           ALU.mult).then_inc(vbd_ready[s], 1)
                    if kind == "graph_out":
                        pool.wait_ge(o_ready[s], count(it, 2 * NATT, 4))
                        pool.tensor_tensor(o[0][s][:], o[0][s][:], o[1][s][:], ALU.add).then_inc(osum_step[s], 1)
                        pool.wait_ge(osum_step[s], count(it, 2, 1))
                        pool.tensor_tensor(o[0][s][:], o[0][s][:], bout_sum[:].unsqueeze(1).broadcast_to([P, T, D]),
                                           ALU.add).then_inc(osum_step[s], 1)
                    if kind == "stats":
                        pool.wait_ge(veps_ready[s], count(it, NBLK, a + 1))
                        pool.tensor_tensor(rstd[s][:], veps[s][:], neg_half[:], ALU.pow).then_inc(rstd_ready[s], 1)

        @block.scalar
        def _(act):
            act.wait_ge(setup_filled, 1)
            act.activation(condT[:], SETUP_BANKS[0][:, 0:B], ACT.Copy).then_inc(cond_ready, 1)
            act.activation(sig[:], SETUP_BANKS[0][:, 0:B], ACT.Exp, scale=-1.0).then_inc(cond_ready, 1)
            act.activation(cols[:], SETUP_BANKS[0][:, B:B + NROWS], ACT.Copy).then_inc(cols_ready, 1)
            for g in range(2):
                act.wait_ge(setup_filled, 2 + g)
                act.activation(wT[:, 4 * g:4 * g + 4, :].rearrange("p a n -> p (a n)"), SETUP_BANKS[1 + g][:],
                               ACT.Copy).then_inc(wT_ready, 1)
            act.wait_ge(cols_ready, 1)
            for j in (4, 5):
                act.wait_ge(setup_filled, 4 + j)
                act.wait_ge(sc1_ready, 2 * j + 2)
                act.activation(alpha[:, j - 4], SETUP_BANKS[3 + j][:, 2 * B:3 * B], ACT.Tanh, bias=modb(j)[2]
                               ).then_inc(alpha_ready, 1)
            act.wait_ge(const_step, 11)
            act.wait_ge(masks_step, 15)

            with act.Fori(0, NIT) as it:
                for kind, a, s in ORDER:
                    if kind == "graph_in":
                        await_fill(act, it, s, "xT")
                        act.activation(xT[s][:], bank(s, "xT")[:], ACT.Copy).then_inc(xT_ready[s], 1)
                        await_fill(act, it, s, "qcT")
                        act.activation(qcT[s][:], bank(s, "qcT")[:], ACT.Copy).then_inc(qcT_ready[s], 1)
                        await_fill(act, it, s, "self")
                        act.activation(sfT[s][:], bank(s, "self")[:], ACT.Identity, bias=vec("L0_cond_b_self")
                                       ).then_inc(sf_ready[s], 1)
                    if kind == "graph_bias":
                        for d in range(2):
                            await_fill(act, it, s, f"bias{d}")
                            act.activation(bias[s][:, d], bank(s, f"bias{d}")[:].rearrange("p (b m) -> p b m", m=S)[:, :, 0:NONGT],
                                           ACT.Copy).then_inc(bias_ready[s], 1)
                    if kind == "qkv":
                        await_fill(act, it, s, f"q a{a}")
                        act.activation(qT[s][:], bank(s, f"q a{a}")[:], ACT.Identity, scale=SCALE, bias=qb_col[:, a:a + 1]
                                       ).then_inc(q_ready[s], 1)
                        kb = {0: vec("L0_cond_bk", 0), 1: vec("L0_cond_bk", 1), 2: zero_col[:], 3: vec("L3_cond_qkv_b", 1)}[a]
                        await_fill(act, it, s, f"k a{a}")
                        act.activation(kT[s][:], bank(s, f"k a{a}")[:], ACT.Identity, bias=kb).then_inc(k_ready[s], 1)
                        await_fill(act, it, s, f"v a{a}")
                        act.activation(v[s][:].rearrange("p t f -> p (t f)"), bank(s, f"v a{a}")[:], ACT.Copy
                                       ).then_inc(v_ready[s], 1)
                    if kind == "softmax":
                        for pair in range(PAIRS):
                            act.wait_ge(shifted[s], count(it, NATT * PAIRS, a * PAIRS + pair + 1))
                            if a < 2:
                                e = prob_g[s][:, 2 * pair:2 * pair + 2, :, 0:NONGT].rearrange("p g b m -> p (g b) m")
                            else:
                                e = prob[s][:, 2 * pair:2 * pair + 2]
                            act.activation(e, e, ACT.Exp).then_inc(exped[s], 1)
                    if kind == "project":
                        att = ATTN_OF_BLOCK[a]
                        await_fill(act, it, s, f"oT a{att}")
                        act.activation(oT[s][:], bank(s, f"oT a{att}")[:], ACT.Identity,
                                       bias=zero_col[:] if att == 2 else vec("L3_cond_qkv_b", 2)).then_inc(oT_ready[s], 1)
                    if kind == "hidden":
                        for u in range(BLOCKS[a][2]):
                            await_fill(act, it, s, f"h{a}.{u}")
                            f = ACT.Gelu if BLOCKS[a][3] == "Gelu" else ACT.Gelu_apprx_tanh
                            act.activation(hT[s][u], bank(s, f"h{a}.{u}")[:], f, bias=vec(HID_BIAS[a], u)
                                           ).then_inc(h_ready[s], 1)

        @block.vector
        def _(dve):
            dve.wait_ge(const_step, 6)
            dve.tensor_copy(ident16[:], ident[:]).then_inc(spread_ready, 1)
            dve.tensor_copy(spread[:], ident[:].rearrange("p (b n) -> p b n", n=S).unsqueeze(2).broadcast_to([P, BT, GH, S])
                            ).then_inc(spread_ready, 1)
            dve.tensor_copy(col[:], col_i[:]).then_inc(masks_step, 1)
            dve.tensor_copy(part[:], part_i[:]).then_inc(masks_step, 1)
            dve.wait_ge(masks_step, 2)
            dve.transpose(part32[:], col[:, 0:S]).then_inc(masks_step, 1)
            dve.tensor_copy(vcol[:], col[:, 0:P].rearrange("p (h n) -> p h n", n=S)[:, :, 0:1].broadcast_to([P, GH, HD])
                            ).then_inc(masks_step, 1)
            dve.wait_ge(masks_step, 4)
            dve.tensor_tensor(quad[:], part[:, 0:S], part32[:], ALU.subtract).then_inc(masks_step, 1)
            head8 = col[:, 0:S].rearrange("p (h d) -> p h d", d=HD)[:, :, 0]
            dve.tensor_tensor(head_lo[:], part32[:, 0:GH], head8, ALU.subtract).then_inc(masks_step, 1)
            dve.wait_ge(masks_step, 6)
            dve.tensor_scalar(head_hi[:], head_lo[:], float(HD), None, ALU.is_lt).then_inc(masks_step, 1)
            dve.tensor_scalar(qmask[:], head_lo[:], 0.0, None, ALU.is_ge).then_inc(masks_step, 1)
            dve.wait_ge(masks_step, 8)
            dve.tensor_tensor(qmask[:], qmask[:], head_hi[:], ALU.mult).then_inc(masks_step, 1)
            dve.tensor_tensor(vmask[:].rearrange("p h d -> p (h d)"), vcol[:].rearrange("p h d -> p (h d)"), quad[:],
                              ALU.is_equal).then_inc(masks_step, 1)
            dve.tensor_tensor(later[:], col[:, 0:S], part32[:], ALU.is_gt).then_inc(masks_step, 1)
            dve.wait_ge(masks_step, 11)
            dve.tensor_scalar(causal[:], later[:], CAUSAL, None, ALU.mult).then_inc(masks_step, 1)
            dve.wait_ge(cond_ready, 2)
            dve.tensor_scalar(sig[:], sig[:], 1.0, None, ALU.add).then_inc(cond_ready, 1)
            dve.wait_ge(cond_ready, 3)
            dve.reciprocal(sig[:], sig[:]).then_inc(sig_ready, 1)
            dve.wait_ge(cols_ready, 1)
            dve.tensor_scalar(qb_col[:, 0:2], cols[:, ROW["L0_cond_bq"]:ROW["L0_cond_bq"] + 2], SCALE, None, ALU.mult
                              ).then_inc(masks_step, 1)
            dve.tensor_scalar(qb_col[:, 3:4], vec("L3_cond_qkv_b", 0), SCALE, None, ALU.mult).then_inc(masks_step, 1)
            dve.memset(qb_col[:, 2:3], 0.0).then_inc(masks_step, 1)
            for j in range(NBLK):
                ps = SETUP_BANKS[3 + j]
                sc_b, sh_b, gt_b = modb(j)
                dve.wait_ge(setup_filled, 4 + j)
                scale, shift, gate = mod[:, 3 * j], mod[:, 3 * j + 1], mod[:, 3 * j + 2]
                if j in GAIN:
                    g, be = (vec(n) for n in GAIN[j])
                    dve.tensor_scalar(sc1[:, j], ps[:, 0:B], sc_b, 1.0, ALU.add, ALU.add).then_inc(sc1_ready, 1)
                    dve.tensor_scalar(shift, ps[:, B:2 * B], sh_b, None, ALU.add).then_inc(sc1_ready, 1)
                else:
                    dve.tensor_scalar(scale, ps[:, 0:B], sc_b, 1.0, ALU.add, ALU.add).then_inc(sc1_ready, 1)
                    dve.tensor_scalar(shift, ps[:, B:2 * B], sh_b, None, ALU.add).then_inc(sc1_ready, 1)
                dve.wait_ge(sc1_ready, 2 * j + 2)
                if BLOCKS[j][1] < 3:
                    last = dve.tensor_scalar(gate, ps[:, 2 * B:3 * B], gt_b, None, ALU.add)
                else:
                    dve.wait_ge(alpha_ready, j - 3)
                    last = dve.tensor_scalar(gate, alpha[:, j - 4], 0.1, None, ALU.mult)
                if j in GAIN:
                    dve.tensor_scalar(scale, sc1[:, j], g, None, ALU.mult)
                    last = dve.scalar_tensor_tensor(out=shift, in0=sc1[:, j], scalar=be, in1=shift, op0=ALU.mult, op1=ALU.add)
                last.then_inc(mod_ready, 1)
            for s in range(STREAMS):
                dve.memset(mx[s][:], 0.0).then_inc(x_ready[s], 1)

            with dve.Fori(0, NIT) as it:
                def chain(sem_, per, k):
                    dve.wait_ge(sem_, count(it, per, k))

                for kind, a, s in ORDER:
                    if kind == "graph_in":
                        dve.wait_ge(x_loaded[s], count(it, 16, 16))
                        dve.tensor_reduce(row_sum[s][:], x_in[s][:], AX_X, ALU.add).then_inc(rsum_ready[s], 1)
                        chain(rsum_ready[s], 1, 1)
                        dve.tensor_scalar(row_flag[s][:], row_sum[s][:], 0.0, None, ALU.not_equal).then_inc(flag_ready[s], 1)
                        dve.wait_ge(bcast_loaded, 16 * 3)
                        dve.wait_ge(adj_loaded[s], count(it, 16, 16))
                        dve.tensor_tensor(adj_w[s], adj[s][:], wb[:].unsqueeze(1).broadcast_to([P, T * S, L]),
                                          ALU.mult).then_inc(adjw_ready[s], 1)
                        dve.tensor_reduce(c_sum[s][:], adj[s][:], AX_X, ALU.add).then_inc(edge_step[s], 1)
                        dve.wait_ge(adjw_ready[s], count(it, 1, 1))
                        dve.tensor_reduce(u_sum[s][:], adj_w[s], AX_X, ALU.add).then_inc(edge_step[s], 1)
                        chain(edge_step[s], 4, 1)
                        dve.tensor_scalar(c_sum[s][:], c_sum[s][:], 0.0, NEG, ALU.is_gt, ALU.mult).then_inc(edge_step[s], 1)
                        chain(edge_step[s], 4, 2)
                        dve.tensor_scalar(u_sum[s][:], u_sum[s][:], bb[:], None, ALU.add).then_inc(edge_step[s], 1)
                        chain(edge_step[s], 4, 4)
                        dve.scalar_tensor_tensor(out=edge[s][:, 0].rearrange("p t m -> p (t m)"), in0=c_sum[s][:], scalar=-NEG,
                                                 in1=u_sum[s][:], op0=ALU.add, op1=ALU.add).then_inc(edge_ready[s], 1)
                        chain(edge_ready[s], 2, 1)
                        dve.transpose(edge[s][:, 1].rearrange("p t m -> p (t m)"), edge[s][:, 0].rearrange("p t m -> p (t m)")
                                      ).then_inc(edge_ready[s], 1)
                    if kind == "softmax":
                        step = a * PAIRS
                        n = NATT * PAIRS
                        if a < 2:
                            pg = prob_g[s]
                            dve.wait_ge(bias_ready[s], count(it, 2, a + 1))
                            for pair in range(PAIRS):
                                await_pair(dve, it, a, s, pair)
                                for g in (2 * pair, 2 * pair + 1):
                                    last = dve.tensor_tensor(pg[:, g, :, 0:NONGT],
                                                             score[:, g].rearrange("p (b m) -> p b m", m=S)[:, :, 0:NONGT],
                                                             bias[s][:, a], ALU.add)
                                last.then_inc(biased[s], 1)
                            src = [pg[:, 2 * q:2 * q + 2, :, 0:NONGT].rearrange("p g b m -> p (g b) m") for q in range(PAIRS)]
                            dst = src
                            for pair in range(PAIRS):
                                chain(biased[s], 2 * PAIRS, PAIRS * a + pair + 1)
                                dve.tensor_reduce(mx[s][:, 2 * pair:2 * pair + 2].rearrange("p g b -> p (g b)"), src[pair], AX_X,
                                                  ALU.max).then_inc(maxed[s], 1)
                        else:
                            src = [score[:, 2 * q:2 * q + 2].rearrange("p g (b m) -> p (g b) m", m=S) for q in range(PAIRS)]
                            dst = [prob[s][:, 2 * q:2 * q + 2].rearrange("p g b m -> p (g b) m") for q in range(PAIRS)]
                            for pair in range(PAIRS):
                                await_pair(dve, it, a, s, pair)
                                dve.tensor_reduce(mx[s][:, 2 * pair:2 * pair + 2].rearrange("p g b -> p (g b)"), src[pair], AX_X,
                                                  ALU.max).then_inc(maxed[s], 1)
                        width = NONGT if a < 2 else S
                        for pair in range(PAIRS):
                            chain(maxed[s], n, step + pair + 1)
                            m = mx[s][:, 2 * pair:2 * pair + 2].rearrange("p g b -> p (g b)").unsqueeze(2)
                            dve.tensor_tensor(dst[pair], src[pair], m.broadcast_to([P, 2 * NB, width]), ALU.subtract
                                              ).then_inc(shifted[s], 1)
                        pr = prob_g[s] if a < 2 else prob[s]
                        for pair in range(PAIRS):
                            dve.wait_ge(exped[s], count(it, n, step + pair + 1))
                            dve.transpose(probT[s][:, 2 * pair:2 * pair + 2].rearrange("p g b n -> p (g b n)"),
                                          pr[:, 2 * pair:2 * pair + 2].rearrange("p g b n -> p (g b n)")
                                          ).then_inc(turned[s], 1)
                    if kind == "values":
                        dst = o[a] if a < 2 else o[0]
                        halves = [("o01", 0), ("o23", 1)]
                        sums, vals = [], []
                        for name, i in halves:
                            ps = bank(s, f"{name} a{a}")[:, 0:2 * NG * VW].rearrange("p (q c) -> p q c", c=VW)
                            sums.append(ps[:, :, GH * HD:VW])
                            vals.append(ps[:, :, 0:GH * HD].rearrange("p q (h d) -> p q h d", d=HD))
                        half = 2 * NG
                        for name, i in halves:
                            await_fill(dve, it, s, f"{name} a{a}")
                            dve.reciprocal(recip[s][:, half * i:half * i + half], sums[i]).then_inc(recip_ready[s], 1)
                        for name, i in halves:
                            chain(recip_ready[s], 2 * NATT, 2 * a + i + 1)
                            dve.tensor_tensor(dst[s][:, 2 * i:2 * i + 2].rearrange("p t (g h d) -> p (t g) h d", g=NG, h=GH),
                                              vals[i], recip[s][:, half * i:half * i + half].unsqueeze(3).broadcast_to([P, half, GH, HD]),
                                              ALU.mult).then_inc(o_ready[s], 1)
                    if kind == "graph_out":
                        dve.wait_ge(osum_step[s], count(it, 2, 2))
                        dve.wait_ge(x_stored[s], count(it, 16, 16))
                        for i, name in enumerate(("self01", "self23")):
                            await_fill(dve, it, s, name)
                            dve.tensor_tensor(o[1][s][:, 2 * i:2 * i + 2], bank(s, name)[:, 0:2 * D].rearrange("p (t f) -> p t f", f=D),
                                              o[0][s][:, 2 * i:2 * i + 2], ALU.add).then_inc(out_step[s], 1)
                        chain(out_step[s], 2, 2)
                        dve.scalar_tensor_tensor(out=x[s][:].rearrange("p t f -> p (t f)"), in0=o[1][s][:].rearrange("p t f -> p (t f)"),
                                                 scalar=0.0, in1=x_in[s][:].rearrange("p t f -> p (t f)"), op0=ALU.max,
                                                 op1=ALU.add).then_inc(x_ready[s], 1)
                    if kind == "stats":
                        await_x(dve, it, s, a + 1)
                        for t in range(T):
                            dve.bn_stats(stats[s][:, t], x[s][:, t]).then_inc(stats_ready[s], 1)
                        chain(stats_ready[s], T * NBLK, T * a + T)
                        dve.memset(wait_slot[:], 0.0)
                        for t in range(T):
                            dve.bn_aggr(mv[s][:, t], stats[s][:, t]).then_inc(mv_ready[s], 1)
                        chain(mv_ready[s], T * NBLK, T * a + T)
                        dve.tensor_scalar(veps[s][:], mv[s][:, :, 1], EPS[a], None, ALU.add).then_inc(veps_ready[s], 1)
                    if kind == "norm":
                        dve.wait_ge(rstd_ready[s], count(it, NBLK, a + 1))
                        for t in range(T):
                            last = dve.tensor_scalar(xn[s][:, t], x[s][:, t], mv[s][:, t, 0:1], rstd[s][:, t:t + 1],
                                                     ALU.subtract, ALU.mult)
                            last.then_inc(xn_ready[s], 1)
                    if kind == "modulate":
                        if a == 0:
                            dve.wait_ge(modc_ready[s], count(it, 1, 1))
                        await_fill(dve, it, s, f"xn{a}")
                        ps = bank(s, f"xn{a}")[:].rearrange("p (b n) -> p b n", n=S)
                        dve.tensor_tensor(xm0[s][:].rearrange("p (b n) -> p b n", n=S), ps,
                                          modc[s][:, 3 * a].unsqueeze(2).broadcast_to([P, NB, S]), ALU.mult).then_inc(scaled[s], 1)
                        chain(scaled[s], NBLK, a + 1)
                        dve.tensor_tensor(xm[s][:].rearrange("p (b n) -> p b n", n=S), xm0[s][:].rearrange("p (b n) -> p b n", n=S),
                                          modc[s][:, 3 * a + 1].unsqueeze(2).broadcast_to([P, NB, S]), ALU.add).then_inc(xm_ready[s], 1)
                    if kind in ("project", "down"):
                        await_fill(dve, it, s, f"y{a}")
                        dve.scalar_tensor_tensor(out=yT[s].rearrange("p (b n) -> p b n", n=S),
                                                 in0=bank(s, f"y{a}")[:].rearrange("p (b n) -> p b n", n=S),
                                                 scalar=vec(OUT_BIAS[a]), in1=modc[s][:, 3 * a + 2].unsqueeze(2).broadcast_to([P, NB, S]),
                                                 op0=ALU.add, op1=ALU.mult).then_inc(y_ready[s], 1)
                    if kind == "residual":
                        await_fill(dve, it, s, f"yT{a}")
                        dve.tensor_tensor(x[s][:].rearrange("p t f -> p (t f)"), bank(s, f"yT{a}")[:],
                                          x[s][:].rearrange("p t f -> p (t f)"), ALU.add).then_inc(x_ready[s], 1)

        @block.tensor
        def _(pe):
            pe.wait_ge(const_step, 6)
            pe.wait_ge(vec_loaded, 16 * (len(VECTORS) + 1))
            pe.transpose(SETUP_BANKS[0][:, 0:B], cond_in[:], ident[:])
            pe.transpose(SETUP_BANKS[0][:, B:B + NROWS], rows[:], ident[0:NROWS, 0:NROWS]).then_inc(setup_filled, 1)
            pe.wait_ge(raw_loaded, 16 * 4)
            for g in range(2):
                for k in range(4):
                    last = pe.transpose(SETUP_BANKS[1 + g][:, k * D:(k + 1) * D], raw[:, 4 * g + k], ident[:])
                last.then_inc(setup_filled, 1)
            pe.wait_ge(wmod_loaded, 16 * len(MODW))
            pe.wait_ge(silu_ready, 1)
            pe.wait_ge(cols_ready, 1)
            for j in range(NBLK):
                for k, wk in enumerate(modw(j)):
                    last = pe.matmul(SETUP_BANKS[3 + j][:, k * B:(k + 1) * B], wk, siluT[:] if BLOCKS[j][1] < 3 else condT[:],
                                     start=True, stop=True)
                last.then_inc(setup_filled, 1)
            pe.wait_ge(w_loaded, 16 * len(DIRECT))
            pe.wait_ge(wT_ready, 2)
            pe.wait_ge(spread_ready, 2)
            pe.wait_ge(masks_step, 15)
            pe.wait_ge(mod_ready, NBLK)
            pe.wait_ge(const_step, 11)

            with pe.Fori(0, NIT) as it:
                def transposes(s, name, src):
                    ps = bank(s, name)
                    for t in range(T):
                        last = pe.transpose(ps[:, t * P:(t + 1) * P], src(t), ident[:])
                    last.then_inc(filled[s], 1)

                for kind, a, s in ORDER:
                    if kind == "graph_in":
                        pe.wait_ge(x_loaded[s], count(it, 16, 16))
                        await_bank(pe, it, s, "xT")
                        transposes(s, "xT", lambda t: x_in[s][:, t])
                        await_bank(pe, it, s, "qcT")
                        pe.wait_ge(qm_ready[s], count(it, 1, 1))
                        transposes(s, "qcT", lambda t: q_in[s][:, t])
                        await_bank(pe, it, s, "self")
                        pe.wait_ge(xT_ready[s], count(it, 1, 1))
                        pe.matmul(bank(s, "self")[:], wT[:, 0], xT[s][:], start=True, stop=False)
                        pe.wait_ge(qcT_ready[s], count(it, 1, 1))
                        pe.matmul(bank(s, "self")[:], wT[:, 1], qcT[s][:], start=False, stop=True).then_inc(filled[s], 1)
                    if kind == "graph_bias":
                        for d in range(2):
                            await_bank(pe, it, s, f"bias{d}")
                            pe.wait_ge(edge_ready[s], count(it, 2, d + 1))
                            ps = bank(s, f"bias{d}")[:].rearrange("p (t b m) -> p t b m", t=T, m=S)
                            for b in range(BT):
                                last = pe.matmul(ps[:, :, b, 0:NONGT], spread[:, b].rearrange("p h n -> p (h n)"),
                                                 edge[s][:, d, :, 0:NONGT], start=True, stop=True)
                            last.then_inc(filled[s], 1)
                    if kind == "qkv":
                        if a < 2:
                            pe.wait_ge(sf_ready[s], count(it, 1, 1))
                        else:
                            pe.wait_ge(xm_ready[s], count(it, NBLK, 1 if a == 2 else 5))
                        src = sfT[s] if a < 2 else xm[s]
                        await_bank(pe, it, s, f"q a{a}")
                        pe.matmul(bank(s, f"q a{a}")[:], q_weight(a), src[:], start=True, stop=True).then_inc(filled[s], 1)
                        await_bank(pe, it, s, f"k a{a}")
                        pe.matmul(bank(s, f"k a{a}")[:], k_weight(a), src[:], start=True, stop=True).then_inc(filled[s], 1)
                        await_bank(pe, it, s, f"v a{a}")
                        for t in range(T):
                            last = pe.matmul(bank(s, f"v a{a}")[:, t * D:(t + 1) * D], src[:, t * P:(t + 1) * P], v_weight(a),
                                             start=True, stop=True)
                        last.then_inc(filled[s], 1)
                    if kind == "softmax":
                        width = NONGT if a < 2 else S
                        pe.wait_ge(k_ready[s], count(it, NATT, a + 1))
                        pe.wait_ge(qbd_ready[s], count(it, NATT, a + 1))
                        for pair in range(PAIRS):
                            await_score_bank(pe, it, a, s, pair)
                            for g in (2 * pair, 2 * pair + 1):
                                if a == 2:
                                    pe.matmul(score[:, g], ident16[:], causal[:].unsqueeze(1).broadcast_to([P, NB, S]),
                                              start=True, stop=False, skip_group_check=True)
                            for b in range(NB):
                                for g in (2 * pair, 2 * pair + 1):
                                    last = pe.matmul(score[:, g, b * S:b * S + width],
                                                     qbd[s][32 * g:32 * g + 32, b].rearrange("p h n -> p (h n)"),
                                                     kT[s][32 * g:32 * g + 32, b * S:b * S + width],
                                                     start=(a != 2), stop=True, skip_group_check=(a == 2))
                            last.then_inc(scored, 1)
                    if kind == "values":
                        await_bank(pe, it, s, f"o01 a{a}")
                        await_bank(pe, it, s, f"o23 a{a}")
                        pe.wait_ge(vbd_ready[s], count(it, NATT, a + 1))
                        pe.wait_ge(turned[s], count(it, NATT * PAIRS, a * PAIRS + PAIRS))
                        for name, t0 in (("o01", 0), ("o23", 2)):
                            ps = bank(s, f"{name} a{a}")
                            for t in (t0, t0 + 1):
                                for g in range(NG):
                                    for b in range(BT):
                                        c0 = ((t - t0) * NG + g) * VW
                                        last = pe.matmul(ps[S * b:S * b + S, c0:c0 + VW], probT[s][:, g, t * BT + b],
                                                         vbd[s][:, t * BT + b, g], start=True, stop=True)
                            last.then_inc(filled[s], 1)
                    if kind == "graph_out":
                        for i, name in enumerate(("self01", "self23")):
                            await_bank(pe, it, s, name)
                            for t in range(2):
                                tok = (2 * i + t) * P
                                last = pe.transpose(bank(s, name)[:, t * D:(t + 1) * D], sfT[s][:, tok:tok + P], ident[:])
                            last.then_inc(filled[s], 1)
                    if kind == "norm":
                        await_bank(pe, it, s, f"xn{a}")
                        pe.wait_ge(xn_ready[s], count(it, T * NBLK, T * a + T))
                        transposes(s, f"xn{a}", lambda t: xn[s][:, t])
                    if kind == "project":
                        att = ATTN_OF_BLOCK[a]
                        await_bank(pe, it, s, f"oT a{att}")
                        pe.wait_ge(o_ready[s], count(it, 2 * NATT, 2 * att + 2))
                        transposes(s, f"oT a{att}", lambda t: o[0][s][:, t])
                        await_bank(pe, it, s, f"y{a}")
                        pe.wait_ge(oT_ready[s], count(it, 2, att - 1))
                        pe.matmul(bank(s, f"y{a}")[:], w[PROJ[a]][:, 0], oT[s][:], start=True, stop=True).then_inc(filled[s], 1)
                    if kind == "hidden":
                        pe.wait_ge(xm_ready[s], count(it, NBLK, a + 1))
                        for u in range(BLOCKS[a][2]):
                            await_bank(pe, it, s, f"h{a}.{u}")
                            pe.matmul(bank(s, f"h{a}.{u}")[:], w[UP[a]][:, 0, u * D:(u + 1) * D], xm[s][:], start=True, stop=True
                                      ).then_inc(filled[s], 1)
                    if kind == "down":
                        await_bank(pe, it, s, f"y{a}")
                        nh = BLOCKS[a][2]
                        for u in range(nh):
                            pe.wait_ge(h_ready[s], count(it, NHID, HIDDEN_BEFORE[a] + u + 1))
                            last = pe.matmul(bank(s, f"y{a}")[:], w[DOWN[a]][:, u], hT[s][u], start=(u == 0), stop=(u == nh - 1))
                        last.then_inc(filled[s], 1)
                    if kind == "residual":
                        await_bank(pe, it, s, f"yT{a}")
                        pe.wait_ge(y_ready[s], count(it, NBLK, a + 1))
                        transposes(s, f"yT{a}", lambda t: yT[s][:, t * P:(t + 1) * P])


def kernel(**inputs):
    import numpy as _np
    import concourse.bacc as _bacc
    from concourse import mybir as _mybir
    from concourse.bass_utils import run_bass_kernel_spmd as _run

    nc = _bacc.Bacc("TRN2", target_bir_lowering=False, num_devices=1)
    arrays, args = {}, {}
    for name, value in inputs.items():
        a = _np.ascontiguousarray(value)
        if name == "L0_cond_b_bias":
            a = a.reshape(1)
        arrays[f"in_{name}"] = a
        args[name] = nc.dram_tensor(f"in_{name}", a.shape, _mybir.dt.from_np(a.dtype), kind="ExternalInput").ap()
    out = nc.dram_tensor("out_x", (B, S, D), _mybir.dt.float32, kind="ExternalOutput").ap()
    build(nc, args, out)
    r = _run(nc, [arrays], core_ids=[0])
    return r.results[0]["out_x"]
```

```python
from contextlib import ExitStack

import numpy as np

import concourse.bass as bass
from concourse import mybir

F32 = mybir.dt.float32
BF16 = mybir.dt.bfloat16
I32 = mybir.dt.int32
ALU = mybir.AluOpType
ACT = mybir.ActivationFunctionType
AX_X = mybir.AxisListType.X

P = 128
B, S, D = 128, 32, 128
L = 11
NONGT = 20
H, HD = 16, 8
GH = 4
NG = H // GH
STREAMS = 2
T = 4
BT = P // S
NB = T * BT
C = T * P
NIT = B * S // (C * STREAMS)
VW = HD + 1
SCALE = float(HD) ** -0.5
NEG = 9000000000000000.0
CAUSAL = -float(2 ** 100)
PAIRS = 2

BLOCKS = [
    ("attn", 1, 0, None),
    ("mlp", 1, 4, "Gelu"),
    ("mlp", 2, 1, "Gelu"),
    ("mlp", 2, 2, "Gelu_apprx_tanh"),
    ("attn", 3, 0, None),
    ("mlp", 3, 4, "Gelu"),
]
NBLK = len(BLOCKS)
EPS = [1e-5, 1e-5, 1e-6, 1e-6, 1e-5, 1e-5]

VECTORS = [
    ("L0_cond_b_self", 1), ("L0_cond_bq", 2), ("L0_cond_bk", 2),
    ("L1_cond_bproj", 1), ("L1_cond_b1", 4), ("L1_cond_b2", 1), ("L1_cond_g1", 1), ("L1_cond_be1", 1),
    ("L1_cond_g2", 1), ("L1_cond_be2", 1), ("L1_cond_bada", 6),
    ("L2_cond_ada_b", 6), ("L2_cond_ssm_b1", 1), ("L2_cond_ssm_b2", 1), ("L2_cond_ff_b1", 2), ("L2_cond_ff_b2", 1),
    ("L3_cond_g1_b", 1), ("L3_cond_b1_b", 1), ("L3_cond_a1_b", 1), ("L3_cond_g2_b", 1), ("L3_cond_b2_b", 1),
    ("L3_cond_a2_b", 1), ("L3_cond_ln1_g", 1), ("L3_cond_ln1_b", 1), ("L3_cond_ln2_g", 1), ("L3_cond_ln2_b", 1),
    ("L3_cond_qkv_b", 3), ("L3_cond_proj_b", 1), ("L3_cond_fc1_b", 4), ("L3_cond_fc2_b", 1),
]
ROW = {}
NROWS = 0
for _name, _k in VECTORS:
    ROW[_name] = NROWS
    NROWS += _k

DIRECT = [
    ("L1_cond_Wqkv", 1, 384), ("L1_cond_Wproj", 1, 128), ("L1_cond_W1", 1, 512), ("L1_cond_W2", 4, 128),
    ("L2_cond_ssm_w1", 1, 128), ("L2_cond_ssm_w2", 1, 128), ("L2_cond_ff_w1", 1, 256), ("L2_cond_ff_w2", 2, 128),
    ("L3_cond_qkv_w", 1, 384), ("L3_cond_proj_w", 1, 128), ("L3_cond_fc1_w", 1, 512), ("L3_cond_fc2_w", 4, 128),
]
MODW = [("L1_cond_Wada", 6), ("L2_cond_ada_w", 6), ("L3_cond_g1_w", 1), ("L3_cond_b1_w", 1), ("L3_cond_a1_w", 1),
        ("L3_cond_g2_w", 1), ("L3_cond_b2_w", 1), ("L3_cond_a2_w", 1)]

ATTN_OF_BLOCK = {0: 2, 4: 3}
NATT = 4


def list_fills():
    names = ["xT", "qcT", "self"]
    for d in range(2):
        names += [f"q a{d}", f"k a{d}", f"v a{d}", f"oA a{d}", f"oB a{d}"]
    names += ["self01", "self23"]
    for j, (kind, _, hidden, _) in enumerate(BLOCKS):
        names.append(f"xn{j}")
        if kind == "attn":
            a = ATTN_OF_BLOCK[j]
            names += [f"q a{a}", f"k a{a}", f"v a{a}", f"oA a{a}", f"oB a{a}", f"oT a{a}"]
        else:
            names += [f"h{j}.{u}" for u in range(hidden)]
        names += [f"y{j}", f"yT{j}"]
    return names


FILLS = list_fills()
NF = len(FILLS)
FILL = {name: n for n, name in enumerate(FILLS)}
assert NF % 2 == 0
HIDDEN_BEFORE = [sum(b[2] for b in BLOCKS[:j]) for j in range(NBLK + 1)]
NHID = HIDDEN_BEFORE[-1]


def list_stages():
    stages = [("graph_in", 0)]
    for d in range(2):
        stages += [("qkv", d), ("softmax", d), ("values", d)]
    stages.append(("graph_out", 0))
    for j, (kind, *_rest) in enumerate(BLOCKS):
        stages += [("stats", j), ("norm", j), ("modulate", j)]
        if kind == "attn":
            a = ATTN_OF_BLOCK[j]
            stages += [("qkv", a), ("softmax", a), ("values", a), ("project", j)]
        else:
            stages += [("hidden", j), ("down", j)]
        stages.append(("residual", j))
    stages.append(("store", 0))
    return stages


STAGES = list_stages()
LAG = 6


def order():
    out = []
    for n in range(len(STAGES) + LAG):
        if n < len(STAGES):
            out.append((*STAGES[n], 0))
        if n >= LAG:
            out.append((*STAGES[n - LAG], 1))
    return out


ORDER = order()


USES = [(a, s) for kind, a, s in ORDER if kind == "softmax"]
SLOT = {use: n for n, use in enumerate(USES)}
assert USES[-1][0] == NATT - 1
NSLOT = len(SLOT)


def build(nc, t_in, out):
    with ExitStack() as ctx:
        def sb(name, shape, dt=F32):
            return ctx.enter_context(nc.sbuf_tensor(name, shape, dt))

        def sem(name):
            return ctx.enter_context(nc.semaphore(name))

        def per_stream(make, name, *args):
            return [make(f"{name}_{s}", *args) for s in range(STREAMS)]

        ident = sb("ident", [P, P])
        ident16 = sb("ident16", [P, P], BF16)
        col_i = sb("col_i", [P, P], I32)
        part_i = sb("part_i", [P, P], I32)
        col = sb("col", [P, P])
        part = sb("part", [P, P])
        part32 = sb("part32", [P, S])
        quad = sb("quad", [P, S])
        later = sb("later", [P, S])
        head_lo = sb("head_lo", [P, GH])
        head_hi = sb("head_hi", [P, GH])
        head_mask = sb("head_mask", [P, GH])
        seq_mask = sb("seq_mask", [P, BT])
        causal = sb("causal", [P, S], BF16)
        neg_half = sb("neg_half", [P, T])
        wait_slot = sb("wait_slot", [P, 1])
        zero_col = sb("zero_col", [P, 1])
        rows = sb("rows", [NROWS, D])
        cols = sb("cols", [P, NROWS])
        qb_col = sb("qb_col", [P, NATT])
        wb = sb("wb", [P, L])
        bb = sb("bb", [P, 1])
        bout = sb("bout", [P, 2, D])
        bout_sum = sb("bout_sum", [P, D])
        w = {name: sb(f"w_{name}", [P, k, n]) for name, k, n in DIRECT}
        wT = sb("wT", [P, 8, D])
        cond_in = sb("cond_in", [P, D])
        condT = sb("condT", [P, B])
        siluT = sb("siluT", [P, B])
        sig = sb("sig", [P, B])
        mod = sb("mod", [P, 3 * NBLK, B])

        x_in = per_stream(sb, "x_in", [P, BT, D])
        q_in = per_stream(sb, "q_in", [P, BT, D])
        adj = per_stream(sb, "adj", [P, T * S, L], I32)
        u_sum = per_stream(sb, "u_sum", [P, T * S])
        c_sum = per_stream(sb, "c_sum", [P, T * S])
        edge = per_stream(sb, "edge", [P, 2, T, S])
        adj_w = per_stream(sb, "adj_w", [P, T * S, L])
        row_sum = per_stream(sb, "row_sum", [P, BT])
        row_flag = per_stream(sb, "row_flag", [P, BT])
        x = per_stream(sb, "x", [P, BT, D])
        xn = per_stream(sb, "xn", [P, BT, D])
        xm0 = per_stream(sb, "xm0", [P, C])
        xm = per_stream(sb, "xm", [P, C])
        xT = xm0
        sfT = xm
        stats = per_stream(sb, "stats", [P, T, 6])
        mv = per_stream(sb, "mv", [P, T, 2])
        veps = per_stream(sb, "veps", [P, T])
        rstd = per_stream(sb, "rstd", [P, T])
        mod_t = per_stream(sb, "mod_t", [P, 3 * NBLK, NB])
        mod_b = per_stream(sb, "mod_b", [P, 3 * NBLK, NB])
        qT = per_stream(sb, "qT", [P, C])
        kT = per_stream(sb, "kT", [P, C])
        kbd = per_stream(sb, "kbd", [P, NB * GH * S])
        v = per_stream(sb, "v", [P, T, D])
        vbd = per_stream(sb, "vbd", [P, T * H, BT, VW])
        prob_g = per_stream(sb, "prob_g", [P, NG, T * GH, S])
        prob = per_stream(sb, "prob", [P, NG, T * GH, S])
        probT = per_stream(sb, "probT", [P, NG, T * GH, S])
        mx = per_stream(sb, "mx", [P, NG, T * GH])
        recip = per_stream(sb, "recip", [P, 2, H // 2 * BT])
        o = [per_stream(sb, "o0", [P, BT, D]), xn]
        oT = per_stream(sb, "oT", [P, C])
        qcT = oT
        sfP = oT
        yT = [a[:].rearrange("p t f -> p (t f)") for a in v]
        hT = [[prob[s][:, u].rearrange("p b m -> p (b m)") for u in range(4)] for s in range(STREAMS)]

        flat = [q[:] for q in kbd]
        flat += [q[:].rearrange("p g b m -> p (g b m)") for q in prob]
        wmod, place = {}, {"L1_cond_Wada": (0, 0), "L2_cond_ada_w": (0, 6 * D)}
        for n_, (name_, _) in enumerate(MODW[2:]):
            place[name_] = (1, n_ * D)
        for name_, k_ in MODW:
            i_, at_ = place[name_]
            wmod[name_] = flat[i_][:, at_:at_ + k_ * D]
        raw = flat[2][:, 0:8 * D].rearrange("p (a i) -> p a i", a=8)
        sc1 = flat[3][:, 0:NBLK * B].rearrange("p (j b) -> p j b", j=NBLK)
        alpha = flat[3][:, NBLK * B:(NBLK + 2) * B].rearrange("p (j b) -> p j b", j=2)

        work = [[ctx.enter_context(nc.psum_tensor(f"work_{s}{i}", [P, C], F32)) for i in range(2)]
                for s in range(STREAMS)]
        score = ctx.enter_context(nc.psum_tensor("score", [P, NG, NB * S], F32))

        vec_loaded = sem("vec_loaded")
        bcast_loaded = sem("bcast_loaded")
        raw_loaded = sem("raw_loaded")
        wmod_loaded = sem("wmod_loaded")
        w_loaded = sem("w_loaded")
        const_step = sem("const_step")
        masks_step = sem("masks_step")
        ident16_ready = sem("ident16_ready")
        setup_filled = sem("setup_filled")
        cond_ready = sem("cond_ready")
        cols_ready = sem("cols_ready")
        sig_ready = sem("sig_ready")
        silu_ready = sem("silu_ready")
        wT_ready = sem("wT_ready")
        sc1_ready = sem("sc1_ready")
        alpha_ready = sem("alpha_ready")
        mod_ready = sem("mod_ready")
        x_loaded = per_stream(sem, "x_loaded")
        q_loaded = per_stream(sem, "q_loaded")
        adj_loaded = per_stream(sem, "adj_loaded")
        x_stored = per_stream(sem, "x_stored")
        filled = per_stream(sem, "filled")
        xT_ready = per_stream(sem, "xT_ready")
        qcT_ready = per_stream(sem, "qcT_ready")
        sf_ready = per_stream(sem, "sf_ready")
        q_ready = per_stream(sem, "q_ready")
        k_ready = per_stream(sem, "k_ready")
        v_ready = per_stream(sem, "v_ready")
        kbd_ready = per_stream(sem, "kbd_ready")
        vbd_ready = per_stream(sem, "vbd_ready")
        exped = per_stream(sem, "exped")
        oT_ready = per_stream(sem, "oT_ready")
        h_ready = per_stream(sem, "h_ready")
        flag_ready = per_stream(sem, "flag_ready")
        rsum_ready = per_stream(sem, "rsum_ready")
        qm_ready = per_stream(sem, "qm_ready")
        adjw_ready = per_stream(sem, "adjw_ready")
        edge_step = per_stream(sem, "edge_step")
        edge_ready = per_stream(sem, "edge_ready")
        biased = per_stream(sem, "biased")
        maxed = per_stream(sem, "maxed")
        shifted = per_stream(sem, "shifted")
        turned = per_stream(sem, "turned")
        recip_ready = per_stream(sem, "recip_ready")
        o_ready = per_stream(sem, "o_ready")
        osum_step = per_stream(sem, "osum_step")
        out_step = per_stream(sem, "out_step")
        x_ready = per_stream(sem, "x_ready")
        stats_ready = per_stream(sem, "stats_ready")
        mv_ready = per_stream(sem, "mv_ready")
        veps_ready = per_stream(sem, "veps_ready")
        rstd_ready = per_stream(sem, "rstd_ready")
        xn_ready = per_stream(sem, "xn_ready")
        scaled = per_stream(sem, "scaled")
        xm_ready = per_stream(sem, "xm_ready")
        modc_ready = per_stream(sem, "modc_ready")
        y_ready = per_stream(sem, "y_ready")
        carrier = sem("carrier")
        scored = sem("scored")

        x_tok = t_in["x"].rearrange("(c t b) n f -> c t n b f", t=T, b=BT)
        out_tok = out.rearrange("(c t b) n f -> c t n b f", t=T, b=BT)
        adj_tok = t_in["mask_BxSxSx11_ik0"].rearrange("b n m l -> (b n) (m l)").rearrange(
            "(c t p) e -> c p t e", t=T, p=P)
        cond_tok = t_in["cond_1024"].rearrange("(c t b) f -> c t b f", t=T, b=BT)

        def vec(name, k=0):
            return cols[:, ROW[name] + k:ROW[name] + k + 1]

        def bank(s, name):
            return work[s][FILL[name] % 2]

        def count(it, per, k):
            return it * per + k

        def await_fill(eng, it, s, name):
            eng.wait_ge(filled[s], count(it, NF, FILL[name] + 1))

        def await_x(eng, it, s, k):
            eng.wait_ge(x_ready[s], count(it, NBLK + 1, k + 1))

        read_by = {"xT": (xT_ready, 1, 1), "qcT": (qcT_ready, 1, 1), "self": (sf_ready, 2, 2),
                   "self01": (out_step, 2, 1), "self23": (out_step, 2, 2)}
        for a_ in range(NATT):
            read_by[f"q a{a_}"] = (q_ready, NATT, a_ + 1)
            read_by[f"k a{a_}"] = (k_ready, NATT, a_ + 1)
            read_by[f"v a{a_}"] = (v_ready, NATT, a_ + 1)
            read_by[f"oA a{a_}"] = (o_ready, 2 * NATT, 2 * a_ + 1)
            read_by[f"oB a{a_}"] = (o_ready, 2 * NATT, 2 * a_ + 2)
        for j_, a_ in ATTN_OF_BLOCK.items():
            read_by[f"oT a{a_}"] = (oT_ready, 2, a_ - 1)
        for j_ in range(NBLK):
            read_by[f"xn{j_}"] = (scaled, NBLK, j_ + 1)
            read_by[f"y{j_}"] = (y_ready, NBLK, j_ + 1)
            read_by[f"yT{j_}"] = (x_ready, NBLK + 1, j_ + 3)
            for u_ in range(BLOCKS[j_][2]):
                read_by[f"h{j_}.{u_}"] = (h_ready, NHID, HIDDEN_BEFORE[j_] + u_ + 1)

        def await_bank(eng, it, s, name):
            n = FILL[name]
            if n < 2:
                await_x(eng, it, s, 0)
            else:
                signal, per, k = read_by[FILLS[n - 2]]
                eng.wait_ge(signal[s], count(it, per, k))

        def await_score_bank(eng, it, a, s, pair):
            n = SLOT[a, s]
            pa, ps = USES[n - 1]
            if n == 0:
                await_x(eng, it, ps, 0)
            elif pa < 2:
                eng.wait_ge(biased[ps], count(it, 2 * PAIRS, pa * PAIRS + pair + 1))
            else:
                eng.wait_ge(shifted[ps], count(it, NATT * PAIRS, pa * PAIRS + pair + 1))

        def await_pair(eng, it, a, s, pair):
            eng.wait_ge(scored, count(it, NSLOT * PAIRS, SLOT[a, s] * PAIRS + pair + 1))

        def q_weight(a):
            return {0: wT[:, 2, :], 1: wT[:, 3, :], 2: w["L1_cond_Wqkv"][:, 0, 0:D],
                    3: w["L3_cond_qkv_w"][:, 0, 0:D]}[a]

        def k_weight(a):
            return {0: wT[:, 4, :], 1: wT[:, 5, :], 2: w["L1_cond_Wqkv"][:, 0, D:2 * D],
                    3: w["L3_cond_qkv_w"][:, 0, D:2 * D]}[a]

        def v_weight(a):
            return {0: wT[:, 6, :], 1: wT[:, 7, :], 2: w["L1_cond_Wqkv"][:, 0, 2 * D:3 * D],
                    3: w["L3_cond_qkv_w"][:, 0, 2 * D:3 * D]}[a]

        def modw(j):
            layer, second = BLOCKS[j][1], j % 2
            if layer == 3:
                n = ("g2", "b2", "a2") if second else ("g1", "b1", "a1")
                return [wmod[f"L3_cond_{q}_w"] for q in n]
            m = wmod["L1_cond_Wada" if layer == 1 else "L2_cond_ada_w"]
            return [m[:, (3 * second + k) * D:(3 * second + k + 1) * D] for k in (1, 0, 2)]

        def modb(j):
            layer, second = BLOCKS[j][1], j % 2
            if layer == 3:
                n = ("g2", "b2", "a2") if second else ("g1", "b1", "a1")
                return [vec(f"L3_cond_{q}_b") for q in n]
            m = "L1_cond_bada" if layer == 1 else "L2_cond_ada_b"
            return [vec(m, 3 * second + k) for k in (1, 0, 2)]

        GAIN = {0: ("L1_cond_g1", "L1_cond_be1"), 1: ("L1_cond_g2", "L1_cond_be2"),
                4: ("L3_cond_ln1_g", "L3_cond_ln1_b"), 5: ("L3_cond_ln2_g", "L3_cond_ln2_b")}
        OUT_BIAS = ["L1_cond_bproj", "L1_cond_b2", "L2_cond_ssm_b2", "L2_cond_ff_b2", "L3_cond_proj_b",
                    "L3_cond_fc2_b"]
        HID_BIAS = [None, "L1_cond_b1", "L2_cond_ssm_b1", "L2_cond_ff_b1", None, "L3_cond_fc1_b"]
        UP = [None, "L1_cond_W1", "L2_cond_ssm_w1", "L2_cond_ff_w1", None, "L3_cond_fc1_w"]
        DOWN = [None, "L1_cond_W2", "L2_cond_ssm_w2", "L2_cond_ff_w2", None, "L3_cond_fc2_w"]
        PROJ = {0: "L1_cond_Wproj", 4: "L3_cond_proj_w"}

        SETUP_BANKS = [work[0][0], work[0][1], work[1][0], work[1][1], score[:, 0], score[:, 1],
                       score[:, 2], score[:, 3], work[0][0]]

        block = ctx.enter_context(nc.Block())

        @block.sync
        def _(sp):
            def load_inputs(c, s):
                for t in range(T):
                    sp.dma_start(x_in[s][S * t:S * t + S], x_tok[c, t]).then_inc(x_loaded[s], 16)
                for t in range(T):
                    src = cond_tok[c, t].unsqueeze(0).broadcast_to([S, BT, D])
                    sp.dma_start(q_in[s][S * t:S * t + S], src).then_inc(q_loaded[s], 16)
                sp.dma_start(adj[s][:].rearrange("p (t m) l -> p t (m l)", t=T), adj_tok[c]).then_inc(adj_loaded[s], 16)

            sp.dma_start(cond_in[:], t_in["cond_1024"]).then_inc(vec_loaded, 16)
            for name, k in VECTORS:
                src = t_in[name]
                if len(src.shape) == 2:
                    src = src.rearrange("a n -> (a n)")
                sp.dma_start(rows[ROW[name]:ROW[name] + k, :], src.rearrange("(k n) -> k n", k=k)).then_inc(vec_loaded, 16)
            sp.dma_start(raw[:, 0:2, :], t_in["L0_cond_W_self"].rearrange("f (a i) -> f a i", a=2)).then_inc(raw_loaded, 16)
            sp.dma_start(raw[:, 2:4, :], t_in["L0_cond_Wq"].rearrange("a f i -> f a i")).then_inc(raw_loaded, 16)
            sp.dma_start(raw[:, 4:6, :], t_in["L0_cond_Wk"].rearrange("a f i -> f a i")).then_inc(raw_loaded, 16)
            sp.dma_start(raw[:, 6:8, :], t_in["L0_cond_Wout"].rearrange("a h g f -> (h g) a f")).then_inc(raw_loaded, 16)
            for name, k in MODW:
                sp.dma_start(wmod[name], t_in[name]).then_inc(wmod_loaded, 16)
            for s in range(STREAMS):
                load_inputs(s, s)
            for name, k, n in DIRECT:
                sp.dma_start(w[name][:], t_in[name].rearrange("(k p) n -> p k n", p=P)).then_inc(w_loaded, 16)

            for s in range(STREAMS):
                sp.sem_inc(x_stored[s], 16 * T)

            with sp.Fori(0, NIT) as it:
                for kind, a, s in ORDER:
                    if kind == "stats" and a == 0:
                        await_x(sp, it, s, 1)
                        load_inputs((it * STREAMS + STREAMS + s) % (NIT * STREAMS), s)
                    if kind == "store":
                        await_x(sp, it, s, NBLK + 1)
                        for t in range(T):
                            sp.dma_start(out_tok[it * STREAMS + s, t], x[s][S * t:S * t + S]).then_inc(x_stored[s], 16)
            for s in range(STREAMS):
                sp.wait_ge(x_stored[s], 16 * T * (NIT + 1))
                sp.wait_ge(x_loaded[s], 16 * T * (NIT + 1))
                sp.wait_ge(q_loaded[s], 16 * T * (NIT + 1))
                sp.wait_ge(adj_loaded[s], 16 * (NIT + 1))

        @block.gpsimd
        def _(pool):
            pool.dma_start(wb[:], t_in["L0_cond_w_bias"].unsqueeze(0).broadcast_to([P, L])).then_inc(bcast_loaded, 16)
            pool.dma_start(bb[:], t_in["L0_cond_b_bias"].rearrange("(a b) -> a b", a=1).broadcast_to([P, 1])).then_inc(bcast_loaded, 16)
            pool.dma_start(bout[:].rearrange("p a f -> p (a f)"),
                           t_in["L0_cond_bout"].rearrange("a f -> (a f)").unsqueeze(0).broadcast_to([P, 2 * D])
                           ).then_inc(bcast_loaded, 16)
            pool.memset(ident[:], 0.0).then_inc(const_step, 1)
            pool.iota(col_i[:], [[1, P]], base=0, channel_multiplier=0).then_inc(const_step, 1)
            pool.iota(part_i[:], [[0, P]], base=0, channel_multiplier=1).then_inc(const_step, 1)
            pool.memset(neg_half[:], -0.5).then_inc(const_step, 1)
            pool.memset(zero_col[:], 0.0).then_inc(const_step, 1)
            pool.wait_ge(const_step, 1)
            pool.affine_select(out=ident[:], in_=ident[:], compare_op=ALU.not_equal, fill=1.0, base=0,
                               pattern=[[-1, P]], channel_multiplier=1).then_inc(const_step, 1)
            for s in range(STREAMS):
                pool.memset(prob_g[s][:], 0.0).then_inc(const_step, 1)
            pool.wait_ge(masks_step, 9)
            for s in range(STREAMS):
                pool.tensor_copy(vbd[s][:, :, :, HD], seq_mask[:].unsqueeze(1).broadcast_to([P, T * H, BT])
                                 ).then_inc(const_step, 1)
            pool.wait_ge(bcast_loaded, 16 * 3)
            pool.tensor_tensor(bout_sum[:], bout[:, 0], bout[:, 1], ALU.add).then_inc(const_step, 1)
            pool.wait_ge(sig_ready, 1)
            pool.tensor_tensor(siluT[:], condT[:], sig[:], ALU.mult).then_inc(silu_ready, 1)
            pool.wait_ge(const_step, 11)
            pool.wait_ge(mod_ready, NBLK)

            with pool.Fori(0, NIT) as it:
                for kind, a, s in ORDER:
                    if kind == "graph_in":
                        mine = mod[:, :, bass.ds(it * (STREAMS * NB) + s * NB, NB)]
                        pool.tensor_copy(mod_t[s][:], mine).then_inc(modc_ready[s], 1)
                        pool.wait_ge(modc_ready[s], count(it, 2, 1))
                        pool.sem_inc(carrier, 1)
                        pool.tensor_copy(mod_b[s][:].rearrange("p j (b t) -> p j b t", b=BT),
                                         mod_t[s][:].rearrange("p j (t b) -> p j b t", b=BT)).then_inc(modc_ready[s], 1)
                        pool.wait_ge(q_loaded[s], count(it, 16 * T, 16 * T))
                        pool.wait_ge(flag_ready[s], count(it, 1, 1))
                        pool.tensor_tensor(q_in[s][:], q_in[s][:], row_flag[s][:].unsqueeze(2).broadcast_to([P, BT, D]),
                                           ALU.mult).then_inc(qm_ready[s], 1)
                    if kind == "qkv":
                        width = NONGT if a < 2 else S
                        pool.wait_ge(k_ready[s], count(it, NATT, a + 1))
                        keys = kT[s][:].rearrange("p (b m) -> p b m", m=S)[:, :, 0:width]
                        pool.tensor_tensor(kbd[s][:, 0:NB * GH * width].rearrange("p (b h m) -> p b h m", h=GH, m=width),
                                           keys.unsqueeze(2).broadcast_to([P, NB, GH, width]),
                                           head_mask[:].unsqueeze(1).unsqueeze(3).broadcast_to([P, NB, GH, width]),
                                           ALU.mult).then_inc(kbd_ready[s], 1)
                        pool.wait_ge(v_ready[s], count(it, NATT, a + 1))
                        pool.tensor_tensor(vbd[s][:, :, :, 0:HD],
                                           v[s][:].rearrange("p t (h d) -> p (t h) d", d=HD).unsqueeze(2).broadcast_to([P, T * H, BT, HD]),
                                           seq_mask[:].unsqueeze(1).unsqueeze(3).broadcast_to([P, T * H, BT, HD]),
                                           ALU.mult).then_inc(vbd_ready[s], 1)
                    if kind == "graph_out":
                        pool.wait_ge(o_ready[s], count(it, 2 * NATT, 4))
                        pool.tensor_tensor(o[0][s][:], o[0][s][:], o[1][s][:], ALU.add).then_inc(osum_step[s], 1)
                        pool.wait_ge(osum_step[s], count(it, 2, 1))
                        pool.tensor_tensor(o[0][s][:], o[0][s][:], bout_sum[:].unsqueeze(1).broadcast_to([P, BT, D]),
                                           ALU.add).then_inc(osum_step[s], 1)
                    if kind == "stats":
                        pool.wait_ge(veps_ready[s], count(it, NBLK, a + 1))
                        pool.tensor_tensor(rstd[s][:], veps[s][:], neg_half[:], ALU.pow).then_inc(rstd_ready[s], 1)

        @block.scalar
        def _(act):
            act.wait_ge(setup_filled, 1)
            act.activation(condT[:], SETUP_BANKS[0][:, 0:B], ACT.Copy).then_inc(cond_ready, 1)
            act.activation(sig[:], SETUP_BANKS[0][:, 0:B], ACT.Exp, scale=-1.0).then_inc(cond_ready, 1)
            act.activation(cols[:], SETUP_BANKS[0][:, B:B + NROWS], ACT.Copy).then_inc(cols_ready, 1)
            for g in range(2):
                act.wait_ge(setup_filled, 2 + g)
                act.activation(wT[:, 4 * g:4 * g + 4, :].rearrange("p a n -> p (a n)"), SETUP_BANKS[1 + g][:],
                               ACT.Copy).then_inc(wT_ready, 1)
            act.wait_ge(cols_ready, 1)
            for j in (4, 5):
                act.wait_ge(setup_filled, 4 + j)
                act.wait_ge(sc1_ready, 2 * j + 2)
                act.activation(alpha[:, j - 4], SETUP_BANKS[3 + j][:, 2 * B:3 * B], ACT.Tanh, bias=modb(j)[2]
                               ).then_inc(alpha_ready, 1)
            act.wait_ge(const_step, 11)
            act.wait_ge(masks_step, 14)

            with act.Fori(0, NIT) as it:
                for kind, a, s in ORDER:
                    if kind == "graph_in":
                        await_fill(act, it, s, "xT")
                        act.activation(xT[s][:], bank(s, "xT")[:], ACT.Copy).then_inc(xT_ready[s], 1)
                        await_fill(act, it, s, "qcT")
                        act.activation(qcT[s][:], bank(s, "qcT")[:], ACT.Copy).then_inc(qcT_ready[s], 1)
                        await_fill(act, it, s, "self")
                        act.activation(sfT[s][:], bank(s, "self")[:], ACT.Identity, bias=vec("L0_cond_b_self")
                                       ).then_inc(sf_ready[s], 1)
                        act.activation(sfP[s][:].rearrange("p (b t n) -> p b t n", b=BT, t=T),
                                       bank(s, "self")[:].rearrange("p (t b n) -> p b t n", b=BT, t=T),
                                       ACT.Identity, bias=vec("L0_cond_b_self")).then_inc(sf_ready[s], 1)
                    if kind == "qkv":
                        await_fill(act, it, s, f"q a{a}")
                        act.activation(qT[s][:], bank(s, f"q a{a}")[:], ACT.Identity, scale=SCALE, bias=qb_col[:, a:a + 1]
                                       ).then_inc(q_ready[s], 1)
                        kb = {0: vec("L0_cond_bk", 0), 1: vec("L0_cond_bk", 1), 2: zero_col[:], 3: vec("L3_cond_qkv_b", 1)}[a]
                        await_fill(act, it, s, f"k a{a}")
                        act.activation(kT[s][:], bank(s, f"k a{a}")[:], ACT.Identity, bias=kb).then_inc(k_ready[s], 1)
                        await_fill(act, it, s, f"v a{a}")
                        act.activation(v[s][:].rearrange("p t f -> p (t f)"), bank(s, f"v a{a}")[:], ACT.Copy
                                       ).then_inc(v_ready[s], 1)
                    if kind == "softmax":
                        for pair in range(PAIRS):
                            act.wait_ge(shifted[s], count(it, NATT * PAIRS, a * PAIRS + pair + 1))
                            if a < 2:
                                e = prob_g[s][:, 2 * pair:2 * pair + 2, :, 0:NONGT].rearrange("p g q m -> p (g q) m")
                            else:
                                e = prob[s][:, 2 * pair:2 * pair + 2]
                            act.activation(e, e, ACT.Exp).then_inc(exped[s], 1)
                    if kind == "project":
                        att = ATTN_OF_BLOCK[a]
                        await_fill(act, it, s, f"oT a{att}")
                        act.activation(oT[s][:], bank(s, f"oT a{att}")[:], ACT.Identity,
                                       bias=zero_col[:] if att == 2 else vec("L3_cond_qkv_b", 2)).then_inc(oT_ready[s], 1)
                    if kind == "hidden":
                        for u in range(BLOCKS[a][2]):
                            await_fill(act, it, s, f"h{a}.{u}")
                            f = ACT.Gelu if BLOCKS[a][3] == "Gelu" else ACT.Gelu_apprx_tanh
                            act.activation(hT[s][u], bank(s, f"h{a}.{u}")[:], f, bias=vec(HID_BIAS[a], u)
                                           ).then_inc(h_ready[s], 1)

        @block.vector
        def _(dve):
            dve.wait_ge(const_step, 6)
            dve.tensor_copy(ident16[:], ident[:]).then_inc(ident16_ready, 1)
            dve.tensor_copy(col[:], col_i[:]).then_inc(masks_step, 1)
            dve.tensor_copy(part[:], part_i[:]).then_inc(masks_step, 1)
            dve.wait_ge(masks_step, 2)
            dve.transpose(part32[:], col[:, 0:S]).then_inc(masks_step, 1)
            dve.wait_ge(masks_step, 3)
            dve.tensor_tensor(quad[:], part[:, 0:S], part32[:], ALU.subtract).then_inc(masks_step, 1)
            head8 = col[:, 0:S].rearrange("p (h d) -> p h d", d=HD)[:, :, 0]
            dve.tensor_tensor(head_lo[:], part32[:, 0:GH], head8, ALU.subtract).then_inc(masks_step, 1)
            dve.wait_ge(masks_step, 5)
            dve.tensor_scalar(head_hi[:], head_lo[:], float(HD), None, ALU.is_lt).then_inc(masks_step, 1)
            dve.tensor_scalar(head_mask[:], head_lo[:], 0.0, None, ALU.is_ge).then_inc(masks_step, 1)
            dve.wait_ge(masks_step, 7)
            dve.tensor_tensor(head_mask[:], head_mask[:], head_hi[:], ALU.mult).then_inc(masks_step, 1)
            dve.tensor_tensor(seq_mask[:], col[:, 0:P].rearrange("p (b n) -> p b n", n=S)[:, :, 0], quad[:, 0:BT],
                              ALU.is_equal).then_inc(masks_step, 1)
            dve.tensor_tensor(later[:], col[:, 0:S], part32[:], ALU.is_gt).then_inc(masks_step, 1)
            dve.wait_ge(masks_step, 10)
            dve.tensor_scalar(causal[:], later[:], CAUSAL, None, ALU.mult).then_inc(masks_step, 1)
            dve.wait_ge(cond_ready, 2)
            dve.tensor_scalar(sig[:], sig[:], 1.0, None, ALU.add).then_inc(cond_ready, 1)
            dve.wait_ge(cond_ready, 3)
            dve.reciprocal(sig[:], sig[:]).then_inc(sig_ready, 1)
            dve.wait_ge(cols_ready, 1)
            dve.tensor_scalar(qb_col[:, 0:2], cols[:, ROW["L0_cond_bq"]:ROW["L0_cond_bq"] + 2], SCALE, None, ALU.mult
                              ).then_inc(masks_step, 1)
            dve.tensor_scalar(qb_col[:, 3:4], vec("L3_cond_qkv_b", 0), SCALE, None, ALU.mult).then_inc(masks_step, 1)
            dve.memset(qb_col[:, 2:3], 0.0).then_inc(masks_step, 1)
            for j in range(NBLK):
                ps = SETUP_BANKS[3 + j]
                sc_b, sh_b, gt_b = modb(j)
                dve.wait_ge(setup_filled, 4 + j)
                scale, shift, gate = mod[:, 3 * j], mod[:, 3 * j + 1], mod[:, 3 * j + 2]
                if j in GAIN:
                    g, be = (vec(n) for n in GAIN[j])
                    dve.tensor_scalar(sc1[:, j], ps[:, 0:B], sc_b, 1.0, ALU.add, ALU.add).then_inc(sc1_ready, 1)
                    dve.tensor_scalar(shift, ps[:, B:2 * B], sh_b, None, ALU.add).then_inc(sc1_ready, 1)
                else:
                    dve.tensor_scalar(scale, ps[:, 0:B], sc_b, 1.0, ALU.add, ALU.add).then_inc(sc1_ready, 1)
                    dve.tensor_scalar(shift, ps[:, B:2 * B], sh_b, None, ALU.add).then_inc(sc1_ready, 1)
                dve.wait_ge(sc1_ready, 2 * j + 2)
                if BLOCKS[j][1] < 3:
                    last = dve.tensor_scalar(gate, ps[:, 2 * B:3 * B], gt_b, None, ALU.add)
                else:
                    dve.wait_ge(alpha_ready, j - 3)
                    last = dve.tensor_scalar(gate, alpha[:, j - 4], 0.1, None, ALU.mult)
                if j in GAIN:
                    dve.tensor_scalar(scale, sc1[:, j], g, None, ALU.mult)
                    last = dve.scalar_tensor_tensor(out=shift, in0=sc1[:, j], scalar=be, in1=shift, op0=ALU.mult, op1=ALU.add)
                last.then_inc(mod_ready, 1)
            for s in range(STREAMS):
                dve.memset(mx[s][:], 0.0).then_inc(x_ready[s], 1)

            with dve.Fori(0, NIT) as it:
                def chain(sem_, per, k):
                    dve.wait_ge(sem_, count(it, per, k))

                for kind, a, s in ORDER:
                    if kind == "graph_in":
                        dve.wait_ge(x_loaded[s], count(it, 16 * T, 16 * T))
                        dve.tensor_reduce(row_sum[s][:], x_in[s][:], AX_X, ALU.add).then_inc(rsum_ready[s], 1)
                        chain(rsum_ready[s], 1, 1)
                        dve.tensor_scalar(row_flag[s][:], row_sum[s][:], 0.0, None, ALU.not_equal).then_inc(flag_ready[s], 1)
                        dve.wait_ge(bcast_loaded, 16 * 3)
                        dve.wait_ge(adj_loaded[s], count(it, 16, 16))
                        dve.tensor_tensor(adj_w[s][:], adj[s][:], wb[:].unsqueeze(1).broadcast_to([P, T * S, L]),
                                          ALU.mult).then_inc(adjw_ready[s], 1)
                        dve.tensor_reduce(c_sum[s][:], adj[s][:], AX_X, ALU.add).then_inc(edge_step[s], 1)
                        dve.wait_ge(adjw_ready[s], count(it, 1, 1))
                        dve.tensor_reduce(u_sum[s][:], adj_w[s][:], AX_X, ALU.add).then_inc(edge_step[s], 1)
                        chain(edge_step[s], 4, 1)
                        dve.tensor_scalar(c_sum[s][:], c_sum[s][:], 0.0, NEG, ALU.is_gt, ALU.mult).then_inc(edge_step[s], 1)
                        chain(edge_step[s], 4, 2)
                        dve.tensor_scalar(u_sum[s][:], u_sum[s][:], bb[:], None, ALU.add).then_inc(edge_step[s], 1)
                        chain(edge_step[s], 4, 4)
                        dve.scalar_tensor_tensor(out=edge[s][:, 0].rearrange("p t m -> p (t m)"), in0=c_sum[s][:], scalar=-NEG,
                                                 in1=u_sum[s][:], op0=ALU.add, op1=ALU.add).then_inc(edge_ready[s], 1)
                        chain(edge_ready[s], 2, 1)
                        dve.transpose(edge[s][:, 1].rearrange("p t m -> p (t m)"), edge[s][:, 0].rearrange("p t m -> p (t m)")
                                      ).then_inc(edge_ready[s], 1)
                    if kind == "softmax":
                        step = a * PAIRS
                        n = NATT * PAIRS
                        if a < 2:
                            pg = prob_g[s]
                            if a == 0:
                                chain(edge_ready[s], 2, 2)
                            for pair in range(PAIRS):
                                await_pair(dve, it, a, s, pair)
                                for g in (2 * pair, 2 * pair + 1):
                                    last = dve.tensor_tensor(
                                        pg[:, g, :, 0:NONGT].rearrange("p (t h) m -> p t h m", t=T),
                                        score[:, g, 0:T * GH * NONGT].rearrange("p (t h m) -> p t h m", t=T, m=NONGT),
                                        edge[s][:, a, :, 0:NONGT].unsqueeze(2).broadcast_to([P, T, GH, NONGT]), ALU.add)
                                last.then_inc(biased[s], 1)
                            src = [pg[:, 2 * q:2 * q + 2, :, 0:NONGT].rearrange("p g q m -> p (g q) m") for q in range(PAIRS)]
                            dst = src
                            for pair in range(PAIRS):
                                chain(biased[s], 2 * PAIRS, PAIRS * a + pair + 1)
                                dve.tensor_reduce(mx[s][:, 2 * pair:2 * pair + 2].rearrange("p g q -> p (g q)"), src[pair], AX_X,
                                                  ALU.max).then_inc(maxed[s], 1)
                        else:
                            src = [score[:, 2 * q:2 * q + 2].rearrange("p g (q m) -> p (g q) m", m=S) for q in range(PAIRS)]
                            dst = [prob[s][:, 2 * q:2 * q + 2].rearrange("p g q m -> p (g q) m") for q in range(PAIRS)]
                            for pair in range(PAIRS):
                                await_pair(dve, it, a, s, pair)
                                dve.tensor_reduce(mx[s][:, 2 * pair:2 * pair + 2].rearrange("p g q -> p (g q)"), src[pair], AX_X,
                                                  ALU.max).then_inc(maxed[s], 1)
                        width = NONGT if a < 2 else S
                        for pair in range(PAIRS):
                            chain(maxed[s], n, step + pair + 1)
                            m = mx[s][:, 2 * pair:2 * pair + 2].rearrange("p g q -> p (g q)").unsqueeze(2)
                            dve.tensor_tensor(dst[pair], src[pair], m.broadcast_to([P, 2 * NB, width]), ALU.subtract
                                              ).then_inc(shifted[s], 1)
                        pr = prob_g[s] if a < 2 else prob[s]
                        for pair in range(PAIRS):
                            dve.wait_ge(exped[s], count(it, n, step + pair + 1))
                            dve.transpose(probT[s][:, 2 * pair:2 * pair + 2].rearrange("p g q n -> p (g q n)"),
                                          pr[:, 2 * pair:2 * pair + 2].rearrange("p g q n -> p (g q n)")
                                          ).then_inc(turned[s], 1)
                    if kind == "values":
                        dst = o[a] if a < 2 else o[0]
                        hh = H // 2
                        halves = [bank(s, f"o{c} a{a}")[:, 0:hh * BT * VW].rearrange("p (h b c) -> p h b c", b=BT, c=VW)
                                  for c in "AB"]
                        for i, c in enumerate("AB"):
                            await_fill(dve, it, s, f"o{c} a{a}")
                            dve.reciprocal(recip[s][:, i].rearrange("p (h b) -> p h b", b=BT), halves[i][:, :, :, HD]
                                           ).then_inc(recip_ready[s], 1)
                        for i in range(2):
                            chain(recip_ready[s], 2 * NATT, 2 * a + i + 1)
                            dve.tensor_tensor(dst[s][:, :, hh * HD * i:hh * HD * (i + 1)].rearrange("p b (h d) -> p h b d", d=HD),
                                              halves[i][:, :, :, 0:HD],
                                              recip[s][:, i].rearrange("p (h b) -> p h b", b=BT).unsqueeze(3).broadcast_to([P, hh, BT, HD]),
                                              ALU.mult).then_inc(o_ready[s], 1)
                    if kind == "graph_out":
                        dve.wait_ge(osum_step[s], count(it, 2, 2))
                        dve.wait_ge(x_stored[s], count(it, 16 * T, 16 * T))
                        for i, name in enumerate(("self01", "self23")):
                            await_fill(dve, it, s, name)
                            dve.tensor_tensor(o[1][s][:, 2 * i:2 * i + 2], bank(s, name)[:, 0:2 * D].rearrange("p (t f) -> p t f", f=D),
                                              o[0][s][:, 2 * i:2 * i + 2], ALU.add).then_inc(out_step[s], 1)
                        chain(out_step[s], 2, 2)
                        dve.scalar_tensor_tensor(out=x[s][:].rearrange("p t f -> p (t f)"), in0=o[1][s][:].rearrange("p t f -> p (t f)"),
                                                 scalar=0.0, in1=x_in[s][:].rearrange("p t f -> p (t f)"), op0=ALU.max,
                                                 op1=ALU.add).then_inc(x_ready[s], 1)
                    if kind == "stats":
                        await_x(dve, it, s, a + 1)
                        for t in range(T):
                            dve.bn_stats(stats[s][:, t], x[s][:, t]).then_inc(stats_ready[s], 1)
                        chain(stats_ready[s], T * NBLK, T * a + T)
                        dve.memset(wait_slot[:], 0.0)
                        for t in range(T):
                            dve.bn_aggr(mv[s][:, t], stats[s][:, t]).then_inc(mv_ready[s], 1)
                        chain(mv_ready[s], T * NBLK, T * a + T)
                        dve.tensor_scalar(veps[s][:], mv[s][:, :, 1], EPS[a], None, ALU.add).then_inc(veps_ready[s], 1)
                    if kind == "norm":
                        dve.wait_ge(rstd_ready[s], count(it, NBLK, a + 1))
                        for t in range(T):
                            last = dve.tensor_scalar(xn[s][:, t], x[s][:, t], mv[s][:, t, 0:1], rstd[s][:, t:t + 1],
                                                     ALU.subtract, ALU.mult)
                            last.then_inc(xn_ready[s], 1)
                    if kind == "modulate":
                        if a == 0:
                            dve.wait_ge(modc_ready[s], count(it, 2, 2))
                        m = mod_t[s] if BLOCKS[a][0] == "attn" else mod_b[s]
                        await_fill(dve, it, s, f"xn{a}")
                        ps = bank(s, f"xn{a}")[:].rearrange("p (b n) -> p b n", n=S)
                        dve.tensor_tensor(xm0[s][:].rearrange("p (b n) -> p b n", n=S), ps,
                                          m[:, 3 * a].unsqueeze(2).broadcast_to([P, NB, S]), ALU.mult).then_inc(scaled[s], 1)
                        chain(scaled[s], NBLK, a + 1)
                        dve.tensor_tensor(xm[s][:].rearrange("p (b n) -> p b n", n=S), xm0[s][:].rearrange("p (b n) -> p b n", n=S),
                                          m[:, 3 * a + 1].unsqueeze(2).broadcast_to([P, NB, S]), ALU.add).then_inc(xm_ready[s], 1)
                    if kind in ("project", "down"):
                        await_fill(dve, it, s, f"y{a}")
                        dve.scalar_tensor_tensor(out=yT[s].rearrange("p (b n) -> p b n", n=S),
                                                 in0=bank(s, f"y{a}")[:].rearrange("p (b n) -> p b n", n=S),
                                                 scalar=vec(OUT_BIAS[a]), in1=mod_b[s][:, 3 * a + 2].unsqueeze(2).broadcast_to([P, NB, S]),
                                                 op0=ALU.add, op1=ALU.mult).then_inc(y_ready[s], 1)
                    if kind == "residual":
                        await_fill(dve, it, s, f"yT{a}")
                        dve.tensor_tensor(x[s][:].rearrange("p t f -> p (t f)"), bank(s, f"yT{a}")[:],
                                          x[s][:].rearrange("p t f -> p (t f)"), ALU.add).then_inc(x_ready[s], 1)

        @block.tensor
        def _(pe):
            pe.wait_ge(const_step, 6)
            pe.wait_ge(vec_loaded, 16 * (len(VECTORS) + 1))
            pe.transpose(SETUP_BANKS[0][:, 0:B], cond_in[:], ident[:])
            pe.transpose(SETUP_BANKS[0][:, B:B + NROWS], rows[:], ident[0:NROWS, 0:NROWS]).then_inc(setup_filled, 1)
            pe.wait_ge(raw_loaded, 16 * 4)
            for g in range(2):
                for k in range(4):
                    last = pe.transpose(SETUP_BANKS[1 + g][:, k * D:(k + 1) * D], raw[:, 4 * g + k], ident[:])
                last.then_inc(setup_filled, 1)
            pe.wait_ge(wmod_loaded, 16 * len(MODW))
            pe.wait_ge(silu_ready, 1)
            pe.wait_ge(cols_ready, 1)
            for j in range(NBLK):
                for k, wk in enumerate(modw(j)):
                    last = pe.matmul(SETUP_BANKS[3 + j][:, k * B:(k + 1) * B], wk, siluT[:] if BLOCKS[j][1] < 3 else condT[:],
                                     start=True, stop=True)
                last.then_inc(setup_filled, 1)
            pe.wait_ge(w_loaded, 16 * len(DIRECT))
            pe.wait_ge(wT_ready, 2)
            pe.wait_ge(ident16_ready, 1)
            pe.wait_ge(masks_step, 14)
            pe.wait_ge(mod_ready, NBLK)
            pe.wait_ge(const_step, 11)

            with pe.Fori(0, NIT) as it:
                def to_features(s, name, src, by_tiles):
                    ps = bank(s, name)[:].rearrange("p (t b n) -> p b t n" if by_tiles else "p (b t n) -> p b t n", t=T, n=S)
                    for b in range(BT):
                        last = pe.transpose(ps[:, b], src[:, b], ident[:])
                    last.then_inc(filled[s], 1)

                def to_tokens(s, name, src, first, n):
                    for b in range(n):
                        last = pe.transpose(bank(s, name)[:, b * D:(b + 1) * D], src[:, (first + b) * P:(first + b + 1) * P],
                                            ident[:])
                    last.then_inc(filled[s], 1)

                for kind, a, s in ORDER:
                    if kind == "graph_in":
                        pe.wait_ge(x_loaded[s], count(it, 16 * T, 16 * T))
                        await_bank(pe, it, s, "xT")
                        to_features(s, "xT", x_in[s], True)
                        await_bank(pe, it, s, "qcT")
                        pe.wait_ge(qm_ready[s], count(it, 1, 1))
                        to_features(s, "qcT", q_in[s], True)
                        await_bank(pe, it, s, "self")
                        pe.wait_ge(xT_ready[s], count(it, 1, 1))
                        pe.matmul(bank(s, "self")[:], wT[:, 0], xT[s][:], start=True, stop=False)
                        pe.wait_ge(qcT_ready[s], count(it, 1, 1))
                        pe.matmul(bank(s, "self")[:], wT[:, 1], qcT[s][:], start=False, stop=True).then_inc(filled[s], 1)
                    if kind == "qkv":
                        if a < 2:
                            pe.wait_ge(sf_ready[s], count(it, 2, 1))
                        else:
                            pe.wait_ge(xm_ready[s], count(it, NBLK, 1 if a == 2 else 5))
                        src = sfT[s] if a < 2 else xm[s]
                        await_bank(pe, it, s, f"q a{a}")
                        pe.matmul(bank(s, f"q a{a}")[:], q_weight(a), src[:], start=True, stop=True).then_inc(filled[s], 1)
                        await_bank(pe, it, s, f"k a{a}")
                        pe.matmul(bank(s, f"k a{a}")[:], k_weight(a), src[:], start=True, stop=True).then_inc(filled[s], 1)
                        await_bank(pe, it, s, f"v a{a}")
                        for t in range(T):
                            last = pe.matmul(bank(s, f"v a{a}")[:, t * D:(t + 1) * D], src[:, t * P:(t + 1) * P], v_weight(a),
                                             start=True, stop=True)
                        last.then_inc(filled[s], 1)
                    if kind == "softmax":
                        width = NONGT if a < 2 else S
                        pe.wait_ge(q_ready[s], count(it, NATT, a + 1))
                        pe.wait_ge(kbd_ready[s], count(it, NATT, a + 1))
                        for pair in range(PAIRS):
                            await_score_bank(pe, it, a, s, pair)
                            for g in (2 * pair, 2 * pair + 1):
                                if a == 2:
                                    pe.matmul(score[:, g], ident16[:], causal[:].unsqueeze(1).broadcast_to([P, NB, S]),
                                              start=True, stop=False, skip_group_check=True)
                            pe.sem_inc(carrier, 1)
                            cw = GH * width
                            for t in range(T):
                                for b in range(BT):
                                    q = t * BT + b
                                    for g in (2 * pair, 2 * pair + 1):
                                        last = pe.matmul(score[S * b:S * b + S, g, t * cw:(t + 1) * cw],
                                                         qT[s][32 * g:32 * g + 32, q * S:(q + 1) * S],
                                                         kbd[s][32 * g:32 * g + 32, q * cw:(q + 1) * cw],
                                                         start=(a != 2), stop=True, skip_group_check=(a == 2),
                                                         tile_position=(32 * g, S * b))
                            last.then_inc(scored, 1)
                    if kind == "values":
                        pe.wait_ge(vbd_ready[s], count(it, NATT, a + 1))
                        for pair, c in enumerate("AB"):
                            await_bank(pe, it, s, f"o{c} a{a}")
                            pe.wait_ge(turned[s], count(it, NATT * PAIRS, a * PAIRS + pair + 1))
                            ps = bank(s, f"o{c} a{a}")
                            for h in range(2 * GH):
                                g, hg = 2 * pair + h // GH, h % GH
                                for t in range(T):
                                    last = pe.matmul(ps[S * t:S * t + S, h * BT * VW:(h + 1) * BT * VW],
                                                     probT[s][:, g, t * GH + hg],
                                                     vbd[s][:, t * H + 2 * GH * pair + h].rearrange("p b c -> p (b c)"),
                                                     start=True, stop=True)
                            last.then_inc(filled[s], 1)
                    if kind == "graph_out":
                        for i, name in enumerate(("self01", "self23")):
                            await_bank(pe, it, s, name)
                            pe.wait_ge(sf_ready[s], count(it, 2, 2))
                            to_tokens(s, name, sfP[s], 2 * i, 2)
                    if kind == "norm":
                        await_bank(pe, it, s, f"xn{a}")
                        pe.wait_ge(xn_ready[s], count(it, T * NBLK, T * a + T))
                        to_features(s, f"xn{a}", xn[s], BLOCKS[a][0] == "attn")
                    if kind == "project":
                        att = ATTN_OF_BLOCK[a]
                        await_bank(pe, it, s, f"oT a{att}")
                        pe.wait_ge(o_ready[s], count(it, 2 * NATT, 2 * att + 2))
                        to_features(s, f"oT a{att}", o[0][s], False)
                        await_bank(pe, it, s, f"y{a}")
                        pe.wait_ge(oT_ready[s], count(it, 2, att - 1))
                        pe.matmul(bank(s, f"y{a}")[:], w[PROJ[a]][:, 0], oT[s][:], start=True, stop=True).then_inc(filled[s], 1)
                    if kind == "hidden":
                        pe.wait_ge(xm_ready[s], count(it, NBLK, a + 1))
                        for u in range(BLOCKS[a][2]):
                            await_bank(pe, it, s, f"h{a}.{u}")
                            pe.matmul(bank(s, f"h{a}.{u}")[:], w[UP[a]][:, 0, u * D:(u + 1) * D], xm[s][:], start=True, stop=True
                                      ).then_inc(filled[s], 1)
                    if kind == "down":
                        await_bank(pe, it, s, f"y{a}")
                        nh = BLOCKS[a][2]
                        for u in range(nh):
                            pe.wait_ge(h_ready[s], count(it, NHID, HIDDEN_BEFORE[a] + u + 1))
                            last = pe.matmul(bank(s, f"y{a}")[:], w[DOWN[a]][:, u], hT[s][u], start=(u == 0), stop=(u == nh - 1))
                        last.then_inc(filled[s], 1)
                    if kind == "residual":
                        await_bank(pe, it, s, f"yT{a}")
                        pe.wait_ge(y_ready[s], count(it, NBLK, a + 1))
                        to_tokens(s, f"yT{a}", yT[s], 0, BT)


def kernel(**inputs):
    import numpy as _np
    import concourse.bacc as _bacc
    from concourse import mybir as _mybir
    from concourse.bass_utils import run_bass_kernel_spmd as _run

    nc = _bacc.Bacc("TRN2", target_bir_lowering=False, num_devices=1)
    arrays, args = {}, {}
    for name, value in inputs.items():
        a = _np.ascontiguousarray(value)
        if name == "L0_cond_b_bias":
            a = a.reshape(1)
        arrays[f"in_{name}"] = a
        args[name] = nc.dram_tensor(f"in_{name}", a.shape, _mybir.dt.from_np(a.dtype), kind="ExternalInput").ap()
    out = nc.dram_tensor("out_x", (B, S, D), _mybir.dt.float32, kind="ExternalOutput").ap()
    build(nc, args, out)
    r = _run(nc, [arrays], core_ids=[0])
    return r.results[0]["out_x"]
```

```python
from contextlib import ExitStack

import numpy as np

import concourse.bass as bass
from concourse import mybir

F32 = mybir.dt.float32
BF16 = mybir.dt.bfloat16
I32 = mybir.dt.int32
ALU = mybir.AluOpType
ACT = mybir.ActivationFunctionType
AX_X = mybir.AxisListType.X

P = 128
B, S, D = 128, 32, 128
L = 11
NONGT = 20
H, HD = 16, 8
GH = 4
NG = H // GH
STREAMS = 2
T = 4
BT = P // S
NB = T * BT
C = T * P
NIT = B * S // (C * STREAMS)
VW = HD + 1
SCALE = float(HD) ** -0.5
NEG = 9000000000000000.0
CAUSAL = -float(2 ** 100)
DVE_NORMS = 2
PAIRS = 2

BLOCKS = [
    ("attn", 1, 0, None),
    ("mlp", 1, 4, "Gelu"),
    ("mlp", 2, 1, "Gelu"),
    ("mlp", 2, 2, "Gelu_apprx_tanh"),
    ("attn", 3, 0, None),
    ("mlp", 3, 4, "Gelu"),
]
NBLK = len(BLOCKS)
EPS = [1e-5, 1e-5, 1e-6, 1e-6, 1e-5, 1e-5]

VECTORS = [
    ("L0_cond_b_self", 1), ("L0_cond_bq", 2), ("L0_cond_bk", 2),
    ("L1_cond_bproj", 1), ("L1_cond_b1", 4), ("L1_cond_b2", 1), ("L1_cond_g1", 1), ("L1_cond_be1", 1),
    ("L1_cond_g2", 1), ("L1_cond_be2", 1), ("L1_cond_bada", 6),
    ("L2_cond_ada_b", 6), ("L2_cond_ssm_b1", 1), ("L2_cond_ssm_b2", 1), ("L2_cond_ff_b1", 2), ("L2_cond_ff_b2", 1),
    ("L3_cond_g1_b", 1), ("L3_cond_b1_b", 1), ("L3_cond_a1_b", 1), ("L3_cond_g2_b", 1), ("L3_cond_b2_b", 1),
    ("L3_cond_a2_b", 1), ("L3_cond_ln1_g", 1), ("L3_cond_ln1_b", 1), ("L3_cond_ln2_g", 1), ("L3_cond_ln2_b", 1),
    ("L3_cond_qkv_b", 3), ("L3_cond_proj_b", 1), ("L3_cond_fc1_b", 4), ("L3_cond_fc2_b", 1),
]
ROW = {}
NROWS = 0
for _name, _k in VECTORS:
    ROW[_name] = NROWS
    NROWS += _k

DIRECT = [
    ("L1_cond_Wqkv", 1, 384), ("L1_cond_Wproj", 1, 128), ("L1_cond_W1", 1, 512), ("L1_cond_W2", 4, 128),
    ("L2_cond_ssm_w1", 1, 128), ("L2_cond_ssm_w2", 1, 128), ("L2_cond_ff_w1", 1, 256), ("L2_cond_ff_w2", 2, 128),
    ("L3_cond_qkv_w", 1, 384), ("L3_cond_proj_w", 1, 128), ("L3_cond_fc1_w", 1, 512), ("L3_cond_fc2_w", 4, 128),
]
MODW = [("L1_cond_Wada", 6), ("L2_cond_ada_w", 6), ("L3_cond_g1_w", 1), ("L3_cond_b1_w", 1), ("L3_cond_a1_w", 1),
        ("L3_cond_g2_w", 1), ("L3_cond_b2_w", 1), ("L3_cond_a2_w", 1)]

ATTN_OF_BLOCK = {0: 2, 4: 3}
NATT = 4


def list_fills():
    names = ["xT", "qcT", "self"]
    for d in range(2):
        names += [f"q a{d}", f"k a{d}", f"v a{d}"]
    names += ["oA a0", "oB a0", "self01", "self23", "oA a1", "oB a1"]
    for j, (kind, _, hidden, _) in enumerate(BLOCKS):
        names.append(f"xn{j}")
        if kind == "attn":
            a = ATTN_OF_BLOCK[j]
            names += [f"q a{a}", f"k a{a}", f"v a{a}", f"oA a{a}", f"oB a{a}", f"oT a{a}"]
        else:
            names += [f"h{j}.{u}" for u in range(hidden)]
        names += [f"y{j}", f"yT{j}"]
    return names


FILLS = list_fills()
NF = len(FILLS)
FILL = {name: n for n, name in enumerate(FILLS)}
assert NF % 2 == 0
HIDDEN_BEFORE = [sum(b[2] for b in BLOCKS[:j]) for j in range(NBLK + 1)]
NHID = HIDDEN_BEFORE[-1]


def by_pair(kind, a):
    return [(kind, a * PAIRS + pair) for pair in range(PAIRS)]


def list_stages():
    stages = [("graph_in", 0), ("self", 0), ("edges", 0)]
    stages += [("keys", 0), ("values_in", 0), *by_pair("scores", 0), ("keys", 1), ("values_in", 1),
               *by_pair("softmax", 0), *by_pair("scores", 1), *by_pair("turn", 0), *by_pair("values", 0),
               *by_pair("softmax", 1), ("self_out", 0), *by_pair("turn", 1), *by_pair("values", 1), ("graph_out", 0)]
    for j, (kind, *_rest) in enumerate(BLOCKS):
        stages += [("stats", j), ("norm", j), ("modulate", j)]
        if kind == "attn":
            a = ATTN_OF_BLOCK[j]
            stages += [("keys", a), ("values_in", a), *by_pair("scores", a), *by_pair("softmax", a),
                       *by_pair("turn", a), *by_pair("values", a), ("gather", j), ("project", j)]
        else:
            stages += [("hidden", j), ("down", j)]
        stages.append(("residual", j))
    stages.append(("store", 0))
    return stages


STAGES = list_stages()
HEAD = 3
MERGE = {
    "tensor": ("000000001110100000010001100101011011101100110111011110000001011010001100110110111001110010"
               "01101010101000110100010100010110101100101101011001111100011001101001111111"),
    "vector": ("001001100001000000010000011100111110100111110110010101011001001001001001110111011001100111"
               "00110001011010001010010011011010100010110100010111011101011010010111101111"),
    "scalar": ("000001001101000000101101100011001111110000010011000110110101110001100001101101110101000010"
               "10111110010010101001100111101000101100000011010001110100111111001111111101"),
    "gpsimd": ("000010100000000000101001011110001111011110111101010000011011000001100111110010011000111010"
               "10101001011100000101110101000111001001101001010101111101100011001011111111"),
}
MERGE["sync"] = MERGE["vector"]


def order(merge):
    first = [(*st, 0, 0) for st in STAGES[HEAD:]] + [(*st, 0, 1) for st in STAGES[:HEAD]]
    second = [(*st, 1, 0) for st in STAGES]
    streams = [iter(first), iter(second)]
    assert merge.count("0") == merge.count("1") == len(STAGES)
    return [next(streams[int(s)]) for s in merge]


PROLOGUE = [(*st, 0, 0) for st in STAGES[:HEAD]]
ORDERS = {engine: order(merge) for engine, merge in MERGE.items()}


def score_uses(stages):
    return [(q, s, ahead) for kind, q, s, ahead in stages if kind == "scores"]


USES = score_uses(ORDERS["tensor"])
SLOT = {(q, s): (n, ahead) for n, (q, s, ahead) in enumerate(USES)}
NSLOT = len(USES)
EARLY = len(score_uses(PROLOGUE))
assert HEAD <= 3
assert all(use[1:] == (0, 1) for use in USES[NSLOT - EARLY:])


def build(nc, t_in, out):
    with ExitStack() as ctx:
        def sb(name, shape, dt=F32):
            return ctx.enter_context(nc.sbuf_tensor(name, shape, dt))

        def sem(name):
            return ctx.enter_context(nc.semaphore(name))

        def per_stream(make, name, *args):
            return [make(f"{name}_{s}", *args) for s in range(STREAMS)]

        ident = sb("ident", [P, P])
        ident16 = sb("ident16", [P, P], BF16)
        col_i = sb("col_i", [P, P], I32)
        part_i = sb("part_i", [P, S], I32)
        col = sb("col", [P, P])
        part = sb("part", [P, S])
        part32 = sb("part32", [P, S])
        quad = sb("quad", [P, S])
        later = sb("later", [P, S])
        head_lo = sb("head_lo", [P, GH])
        head_hi = sb("head_hi", [P, GH])
        head_mask = sb("head_mask", [P, GH])
        quad_mask = sb("quad_mask", [P, NG])
        causal = sb("causal", [P, S], BF16)
        rep32 = sb("rep32", [P, NG, S])
        sel = sb("sel", [P, BT, P])
        neg_half = sb("neg_half", [P, T])
        wait_slot = sb("wait_slot", [P, 1])
        table_slot = sb("table_slot", [P, STREAMS, NATT + NBLK])
        zero_col = sb("zero_col", [P, 1])
        rows = sb("rows", [NROWS, D])
        cols = sb("cols", [P, NROWS])
        kb_head = sb("kb_head", [P, NATT, GH])
        qb_col = sb("qb_col", [P, NATT])
        wb = sb("wb", [P, L])
        bb = sb("bb", [P, 1])
        bout = sb("bout", [P, 2, D])
        bout_sum = sb("bout_sum", [P, D])
        w = {name: sb(f"w_{name}", [P, k, n]) for name, k, n in DIRECT}
        wT = sb("wT", [P, 8, D])
        mod = sb("mod", [P, 3 * NBLK, B + NB])

        x_in = per_stream(sb, "x_in", [P, BT, D])
        q_in = per_stream(sb, "q_in", [P, BT, D])
        adj = per_stream(sb, "adj", [P, T * S, L], I32)
        u_sum = per_stream(sb, "u_sum", [P, T * S])
        c_sum = per_stream(sb, "c_sum", [P, T * S])
        edge = per_stream(sb, "edge", [P, 2, T, S])
        row_sum = per_stream(sb, "row_sum", [P, BT])
        row_flag = per_stream(sb, "row_flag", [P, BT])
        x = per_stream(sb, "x", [P, BT, D])
        xn = per_stream(sb, "xn", [P, BT, D])
        xm0 = per_stream(sb, "xm0", [P, C])
        xm = per_stream(sb, "xm", [P, C])
        xT = xm0
        sfT = xm
        stats = per_stream(sb, "stats", [P, T, 6])
        mv = per_stream(sb, "mv", [P, T, 2])
        veps = per_stream(sb, "veps", [P, T])
        rstd = per_stream(sb, "rstd", [P, T])
        nmr = per_stream(sb, "nmr", [P, BT - DVE_NORMS])
        mod_b = per_stream(sb, "mod_b", [P, 3 * NBLK, NB])
        qd = per_stream(sb, "qd", [P, NB, NG, S])
        vt = per_stream(sb, "vt", [P, C])
        kbd = [per_stream(sb, f"kbd{i}", [P, NB * GH * S]) for i in range(2)]
        vbd = [per_stream(sb, f"vbd{i}", [P, NB * GH, NG, VW]) for i in range(2)]
        prob_g = per_stream(sb, "prob_g", [P, BT, T * GH, S])
        prob = per_stream(sb, "prob", [P, BT, T * GH, S])
        probT = [[k[:].rearrange("p (g q n) -> p g q n", g=BT, n=S) for k in ks] for ks in kbd]
        adj_w = [q[:].rearrange("p g q m -> p (g q m)")[:, 0:T * S * L].rearrange("p (m l) -> p m l", l=L) for q in prob]
        mx = per_stream(sb, "mx", [P, BT, T * GH])
        recip = per_stream(sb, "recip", [P, PAIRS, 2 * H])
        o = [per_stream(sb, "o0", [P, BT, D]), xn]
        oT = per_stream(sb, "oT", [P, C])
        qcT = oT
        yT = [a[:] for a in vt]
        hT = [[prob[s][:, u].rearrange("p b m -> p (b m)") for u in range(4)] for s in range(STREAMS)]

        cond_in, condT, siluT, sig = (x[0][:, k] for k in range(4))
        flat = [q[:] for q in kbd[0]]
        flat += [q[:].rearrange("p g b m -> p (g b m)") for q in prob]
        wmod, place = {}, {"L1_cond_Wada": (0, 0), "L2_cond_ada_w": (0, 6 * D)}
        for n_, (name_, _) in enumerate(MODW[2:]):
            place[name_] = (1, n_ * D)
        for name_, k_ in MODW:
            i_, at_ = place[name_]
            wmod[name_] = flat[i_][:, at_:at_ + k_ * D]
        raw = flat[2][:, 0:8 * D].rearrange("p (a i) -> p a i", a=8)
        sc1 = flat[3][:, 0:NBLK * B].rearrange("p (j b) -> p j b", j=NBLK)
        alpha = flat[3][:, NBLK * B:(NBLK + 2) * B].rearrange("p (j b) -> p j b", j=2)

        work = [[ctx.enter_context(nc.psum_tensor(f"work_{s}{i}", [P, C], F32)) for i in range(2)]
                for s in range(STREAMS)]
        score = ctx.enter_context(nc.psum_tensor("score", [P, BT, NB * S], F32))

        vec_loaded = sem("vec_loaded")
        bcast_loaded = sem("bcast_loaded")
        raw_loaded = sem("raw_loaded")
        wmod_loaded = sem("wmod_loaded")
        w_loaded = sem("w_loaded")
        const_step = sem("const_step")
        masks_step = sem("masks_step")
        ident16_ready = sem("ident16_ready")
        rep_ready = sem("rep_ready")
        setup_filled = sem("setup_filled")
        cond_ready = sem("cond_ready")
        cols_ready = sem("cols_ready")
        sig_ready = sem("sig_ready")
        silu_ready = sem("silu_ready")
        wT_ready = sem("wT_ready")
        sc1_ready = sem("sc1_ready")
        alpha_ready = sem("alpha_ready")
        mod_ready = sem("mod_ready")
        x_loaded = per_stream(sem, "x_loaded")
        q_loaded = per_stream(sem, "q_loaded")
        adj_loaded = per_stream(sem, "adj_loaded")
        x_stored = per_stream(sem, "x_stored")
        filled = per_stream(sem, "filled")
        xT_ready = per_stream(sem, "xT_ready")
        qcT_ready = per_stream(sem, "qcT_ready")
        sf_ready = per_stream(sem, "sf_ready")
        q_ready = per_stream(sem, "q_ready")
        vt_ready = per_stream(sem, "vt_ready")
        kbd_ready = per_stream(sem, "kbd_ready")
        vbd_ready = per_stream(sem, "vbd_ready")
        exped = per_stream(sem, "exped")
        oT_ready = per_stream(sem, "oT_ready")
        h_ready = per_stream(sem, "h_ready")
        flag_ready = per_stream(sem, "flag_ready")
        rsum_ready = per_stream(sem, "rsum_ready")
        qm_ready = per_stream(sem, "qm_ready")
        adjw_ready = per_stream(sem, "adjw_ready")
        edge_step = per_stream(sem, "edge_step")
        edge_ready = per_stream(sem, "edge_ready")
        maxed = per_stream(sem, "maxed")
        shifted = per_stream(sem, "shifted")
        turned = per_stream(sem, "turned")
        recip_ready = per_stream(sem, "recip_ready")
        o_ready = per_stream(sem, "o_ready")
        osum_step = per_stream(sem, "osum_step")
        out_step = per_stream(sem, "out_step")
        gsum_ready = per_stream(sem, "gsum_ready")
        x_ready = per_stream(sem, "x_ready")
        stats_ready = per_stream(sem, "stats_ready")
        mv_ready = per_stream(sem, "mv_ready")
        veps_ready = per_stream(sem, "veps_ready")
        rstd_ready = per_stream(sem, "rstd_ready")
        nmr_ready = per_stream(sem, "nmr_ready")
        xn_ready = per_stream(sem, "xn_ready")
        xn_act_ready = per_stream(sem, "xn_act_ready")
        scaled = per_stream(sem, "scaled")
        xm_ready = per_stream(sem, "xm_ready")
        modc_ready = per_stream(sem, "modc_ready")
        y_ready = per_stream(sem, "y_ready")
        carrier = sem("carrier")
        scored = sem("scored")

        x_tok = t_in["x"].rearrange("(c t b) n f -> c t n b f", t=T, b=BT)
        out_tok = out.rearrange("(c t b) n f -> c t n b f", t=T, b=BT)
        adj_tok = t_in["mask_BxSxSx11_ik0"].rearrange("b n m l -> (b n) (m l)").rearrange(
            "(c t p) e -> c p t e", t=T, p=P)
        cond_tok = t_in["cond_1024"].rearrange("(c t b) f -> c t b f", t=T, b=BT)

        def vec(name, k=0):
            return cols[:, ROW[name] + k:ROW[name] + k + 1]

        def bank(s, name):
            return work[s][FILL[name] % 2]

        def count(it, per, k):
            return it[0] * per + (it[1] * per + k)

        def await_fill(eng, it, s, name):
            eng.wait_ge(filled[s], count(it, NF, FILL[name] + 1))

        def await_x(eng, it, s, k):
            eng.wait_ge(x_ready[s], count(it, NBLK + 1, k + 1))

        read_by = {"xT": (xT_ready, 1, 1), "qcT": (qcT_ready, 1, 1), "self": (sf_ready, 1, 1),
                   "self01": (out_step, 2, 1), "self23": (out_step, 2, 2)}
        for a_ in range(NATT):
            read_by[f"q a{a_}"] = (q_ready, NATT, a_ + 1)
            read_by[f"k a{a_}"] = (kbd_ready, NATT, a_ + 1)
            read_by[f"v a{a_}"] = (vt_ready, NATT, a_ + 1)
            read_by[f"oA a{a_}"] = (o_ready, 2 * NATT, 2 * a_ + 1)
            read_by[f"oB a{a_}"] = (o_ready, 2 * NATT, 2 * a_ + 2)
        for j_, a_ in ATTN_OF_BLOCK.items():
            read_by[f"oT a{a_}"] = (oT_ready, 2, a_ - 1)
        for j_ in range(NBLK):
            read_by[f"xn{j_}"] = (scaled, NBLK, j_ + 1)
            read_by[f"y{j_}"] = (y_ready, NBLK, j_ + 1)
            read_by[f"yT{j_}"] = (x_ready, NBLK + 1, j_ + 3)
            for u_ in range(BLOCKS[j_][2]):
                read_by[f"h{j_}.{u_}"] = (h_ready, NHID, HIDDEN_BEFORE[j_] + u_ + 1)

        def await_bank(eng, it, s, name):
            n = FILL[name]
            if n < 2:
                await_x(eng, it, s, 0)
            else:
                signal, per, k = read_by[FILLS[n - 2]]
                eng.wait_ge(signal[s], count(it, per, k))

        def await_score_bank(eng, it, q, s):
            n, ahead = SLOT[q, s]
            same = [m for m in range(NSLOT) if USES[m][0] % PAIRS == q % PAIRS]
            m = same[same.index(n) - 1]
            wraps = m >= n
            pq, ps, before = USES[m]
            if it[1] < ahead and wraps | (m < NSLOT - EARLY):
                return
            if wraps and not before:
                await_x(eng, it, ps, 0)
                return
            it = (it[0], it[1] - ahead + before - wraps)
            eng.wait_ge(shifted[ps], count(it, NATT * PAIRS, pq + 1))

        def await_scores(eng, it, q, s):
            n, ahead = SLOT[q, s]
            eng.wait_ge(scored, count((it[0], it[1] - ahead), NSLOT, EARLY + n + 1))

        def q_weight(a):
            return {0: wT[:, 2, :], 1: wT[:, 3, :], 2: w["L1_cond_Wqkv"][:, 0, 0:D],
                    3: w["L3_cond_qkv_w"][:, 0, 0:D]}[a]

        def k_weight(a):
            return {0: wT[:, 4, :], 1: wT[:, 5, :], 2: w["L1_cond_Wqkv"][:, 0, D:2 * D],
                    3: w["L3_cond_qkv_w"][:, 0, D:2 * D]}[a]

        def v_weight(a):
            return {0: wT[:, 6, :], 1: wT[:, 7, :], 2: w["L1_cond_Wqkv"][:, 0, 2 * D:3 * D],
                    3: w["L3_cond_qkv_w"][:, 0, 2 * D:3 * D]}[a]

        def modw(j):
            layer, second = BLOCKS[j][1], j % 2
            if layer == 3:
                n = ("g2", "b2", "a2") if second else ("g1", "b1", "a1")
                return [wmod[f"L3_cond_{q}_w"] for q in n]
            m = wmod["L1_cond_Wada" if layer == 1 else "L2_cond_ada_w"]
            return [m[:, (3 * second + k) * D:(3 * second + k + 1) * D] for k in (1, 0, 2)]

        def modb(j):
            layer, second = BLOCKS[j][1], j % 2
            if layer == 3:
                n = ("g2", "b2", "a2") if second else ("g1", "b1", "a1")
                return [vec(f"L3_cond_{q}_b") for q in n]
            m = "L1_cond_bada" if layer == 1 else "L2_cond_ada_b"
            return [vec(m, 3 * second + k) for k in (1, 0, 2)]

        GAIN = {0: ("L1_cond_g1", "L1_cond_be1"), 1: ("L1_cond_g2", "L1_cond_be2"),
                4: ("L3_cond_ln1_g", "L3_cond_ln1_b"), 5: ("L3_cond_ln2_g", "L3_cond_ln2_b")}
        OUT_BIAS = ["L1_cond_bproj", "L1_cond_b2", "L2_cond_ssm_b2", "L2_cond_ff_b2", "L3_cond_proj_b",
                    "L3_cond_fc2_b"]
        HID_BIAS = [None, "L1_cond_b1", "L2_cond_ssm_b1", "L2_cond_ff_b1", None, "L3_cond_fc1_b"]
        UP = [None, "L1_cond_W1", "L2_cond_ssm_w1", "L2_cond_ff_w1", None, "L3_cond_fc1_w"]
        DOWN = [None, "L1_cond_W2", "L2_cond_ssm_w2", "L2_cond_ff_w2", None, "L3_cond_fc2_w"]
        GELU = {"Gelu": ACT.Gelu, "Gelu_apprx_tanh": ACT.Gelu_apprx_tanh}
        PROJ = {0: "L1_cond_Wproj", 4: "L3_cond_proj_w"}

        SETUP_BANKS = [work[0][0], work[0][1], work[1][0], work[1][1], score[:, 0], score[:, 1],
                       score[:, 2], score[:, 3], work[1][0]]

        block = ctx.enter_context(nc.Block())

        def load_vectors(eng, vectors):
            for name, k in vectors:
                src = t_in[name]
                if len(src.shape) == 2:
                    src = src.rearrange("a n -> (a n)")
                eng.dma_start(rows[ROW[name]:ROW[name] + k, :], src.rearrange("(k n) -> k n", k=k)).then_inc(vec_loaded, 16)

        @block.sync
        def _(sp):
            def load_inputs(c, s):
                for t in range(T):
                    sp.dma_start(x_in[s][S * t:S * t + S], x_tok[c, t]).then_inc(x_loaded[s], 16)
                for t in range(T):
                    src = cond_tok[c, t].unsqueeze(0).broadcast_to([S, BT, D])
                    sp.dma_start(q_in[s][S * t:S * t + S], src).then_inc(q_loaded[s], 16)
                sp.dma_start(adj[s][:].rearrange("p (t m) l -> p t (m l)", t=T), adj_tok[c]).then_inc(adj_loaded[s], 16)

            sp.dma_start(cond_in, t_in["cond_1024"]).then_inc(vec_loaded, 16)
            load_vectors(sp, VECTORS[0::2])
            sp.dma_start(raw[:, 0:2, :], t_in["L0_cond_W_self"].rearrange("f (a i) -> f a i", a=2)).then_inc(raw_loaded, 16)
            sp.dma_start(raw[:, 2:4, :], t_in["L0_cond_Wq"].rearrange("a f i -> f a i")).then_inc(raw_loaded, 16)
            sp.dma_start(raw[:, 4:6, :], t_in["L0_cond_Wk"].rearrange("a f i -> f a i")).then_inc(raw_loaded, 16)
            sp.dma_start(raw[:, 6:8, :], t_in["L0_cond_Wout"].rearrange("a h g f -> (h g) a f")).then_inc(raw_loaded, 16)
            load_inputs(0, 0)
            for name, k in MODW:
                sp.dma_start(wmod[name], t_in[name]).then_inc(wmod_loaded, 16)
            load_inputs(1, 1)
            for name, k, n in DIRECT:
                sp.dma_start(w[name][:], t_in[name].rearrange("(k p) n -> p k n", p=P)).then_inc(w_loaded, 16)

            for s in range(STREAMS):
                sp.sem_inc(x_stored[s], 16 * T)

            def stage(it, kind, a, s):
                if kind == "stats" and a == 0:
                    await_x(sp, it, s, 1)
                    load_inputs((it[0] * STREAMS + STREAMS + s) % (NIT * STREAMS), s)
                if kind == "store":
                    await_x(sp, it, s, NBLK + 1)
                    for t in range(T):
                        sp.dma_start(out_tok[it[0] * STREAMS + s, t], x[s][S * t:S * t + S]).then_inc(x_stored[s], 16)

            with sp.Fori(0, NIT) as it:
                for kind, a, s, ahead in ORDERS["sync"]:
                    stage((it, ahead), kind, a, s)
            for s in range(STREAMS):
                sp.wait_ge(x_stored[s], 16 * T * (NIT + 1))
                sp.wait_ge(x_loaded[s], 16 * T * (NIT + 1))
                sp.wait_ge(q_loaded[s], 16 * T * (NIT + 1))
                sp.wait_ge(adj_loaded[s], 16 * (NIT + 1))

        @block.gpsimd
        def _(pool):
            pool.dma_start(wb[:], t_in["L0_cond_w_bias"].unsqueeze(0).broadcast_to([P, L])).then_inc(bcast_loaded, 16)
            pool.dma_start(bb[:], t_in["L0_cond_b_bias"].rearrange("(a b) -> a b", a=1).broadcast_to([P, 1])).then_inc(bcast_loaded, 16)
            pool.dma_start(bout[:].rearrange("p a f -> p (a f)"),
                           t_in["L0_cond_bout"].rearrange("a f -> (a f)").unsqueeze(0).broadcast_to([P, 2 * D])
                           ).then_inc(bcast_loaded, 16)
            pool.memset(ident[:], 0.0).then_inc(const_step, 1)
            pool.iota(col_i[:], [[1, P]], base=0, channel_multiplier=0).then_inc(const_step, 1)
            pool.iota(part_i[:], [[0, S]], base=0, channel_multiplier=1).then_inc(const_step, 1)
            pool.memset(neg_half[:], -0.5).then_inc(const_step, 1)
            pool.memset(zero_col[:], 0.0).then_inc(const_step, 1)
            pool.wait_ge(const_step, 1)
            pool.affine_select(out=ident[:], in_=ident[:], compare_op=ALU.not_equal, fill=1.0, base=0,
                               pattern=[[-1, P]], channel_multiplier=1).then_inc(const_step, 1)
            for s in range(STREAMS):
                pool.memset(prob_g[s][:], 0.0).then_inc(const_step, 1)
                pool.memset(qd[s][:], 0.0).then_inc(const_step, 1)
            pool.wait_ge(masks_step, 9)
            for vb in vbd[0] + vbd[1]:
                pool.tensor_copy(vb[:, :, :, HD], quad_mask[:].unsqueeze(1).broadcast_to([P, NB * GH, NG])
                                 ).then_inc(const_step, 1)
            pool.wait_ge(bcast_loaded, 16 * 3)
            pool.tensor_tensor(bout_sum[:], bout[:, 0], bout[:, 1], ALU.add).then_inc(const_step, 1)
            pool.wait_ge(sig_ready, 1)
            pool.tensor_tensor(siluT, condT, sig, ALU.mult).then_inc(silu_ready, 1)
            pool.wait_ge(const_step, 15)

            def stage(it, kind, a, s):
                if kind == "graph_in":
                    pool.wait_ge(q_loaded[s], count(it, 16 * T, 16 * T))
                    pool.wait_ge(flag_ready[s], count(it, 1, 1))
                    pool.tensor_tensor(q_in[s][:], q_in[s][:], row_flag[s][:].unsqueeze(2).broadcast_to([P, BT, D]),
                                       ALU.mult).then_inc(qm_ready[s], 1)
                if kind == "keys" and a == 0:
                    await_x(pool, it, s, 0)
                    pool.sem_inc(carrier, 1)
                    mine = mod[:, :, bass.ds(it[0] * (STREAMS * NB) + (it[1] * STREAMS + s) * NB, NB)]
                    pool.tensor_copy(mod_b[s][:].rearrange("p j (b t) -> p j b t", b=BT),
                                     mine.rearrange("p j (t b) -> p j b t", b=BT)).then_inc(modc_ready[s], 1)
                if kind == "values_in":
                    pool.wait_ge(vt_ready[s], count(it, NATT, a + 1))
                    pool.tensor_tensor(vbd[a % 2][s][:, :, :, 0:HD],
                                       vt[s][:].rearrange("p (q d) -> p q d", d=HD).unsqueeze(2).broadcast_to([P, NB * GH, NG, HD]),
                                       quad_mask[:].unsqueeze(1).unsqueeze(3).broadcast_to([P, NB * GH, NG, HD]),
                                       ALU.mult).then_inc(vbd_ready[s], 1)
                if kind == "self_out":
                    pool.wait_ge(o_ready[s], count(it, 2 * NATT, 2))
                    pool.tensor_tensor(o[0][s][:], o[0][s][:], bout_sum[:].unsqueeze(1).broadcast_to([P, BT, D]),
                                       ALU.add).then_inc(osum_step[s], 1)
                if kind == "stats":
                    pool.wait_ge(veps_ready[s], count(it, NBLK, a + 1))
                    pool.tensor_tensor(rstd[s][:], veps[s][:], neg_half[:], ALU.pow).then_inc(rstd_ready[s], 1)

            for kind, a, s, ahead in PROLOGUE:
                stage((0, ahead), kind, a, s)
            pool.wait_ge(mod_ready, NBLK + 1)
            with pool.Fori(0, NIT) as it:
                for kind, a, s, ahead in ORDERS["gpsimd"]:
                    stage((it, ahead), kind, a, s)

        @block.scalar
        def _(act):
            load_vectors(act, VECTORS[1::2])
            act.wait_ge(setup_filled, 1)
            act.activation(condT, SETUP_BANKS[0][:, 0:B], ACT.Copy).then_inc(cond_ready, 1)
            act.activation(sig, SETUP_BANKS[0][:, 0:B], ACT.Exp, scale=-1.0).then_inc(cond_ready, 1)
            act.activation(cols[:], SETUP_BANKS[0][:, B:B + NROWS], ACT.Copy).then_inc(cols_ready, 1)
            for g in range(2):
                act.wait_ge(setup_filled, 2 + g)
                act.activation(wT[:, 4 * g:4 * g + 4, :].rearrange("p a n -> p (a n)"), SETUP_BANKS[1 + g][:],
                               ACT.Copy).then_inc(wT_ready, 1)
            act.wait_ge(cols_ready, 1)
            act.wait_ge(const_step, 15)
            act.wait_ge(masks_step, 18)

            def stage(it, kind, a, s):
                if kind == "graph_in":
                    await_fill(act, it, s, "xT")
                    act.activation(xT[s][:], bank(s, "xT")[:], ACT.Copy).then_inc(xT_ready[s], 1)
                    await_fill(act, it, s, "qcT")
                    act.activation(qcT[s][:], bank(s, "qcT")[:], ACT.Copy).then_inc(qcT_ready[s], 1)
                if kind == "self":
                    await_fill(act, it, s, "self")
                    act.activation(sfT[s][:], bank(s, "self")[:], ACT.Identity, bias=vec("L0_cond_b_self")
                                   ).then_inc(sf_ready[s], 1)
                if kind == "keys":
                    await_fill(act, it, s, f"q a{a}")
                    if a == 1:
                        await_scores(act, it, PAIRS - 1, s)
                    for g in range(NG):
                        rows_g = slice(32 * g, 32 * g + 32)
                        last = act.activation(qd[s][rows_g, :, g], bank(s, f"q a{a}")[rows_g].rearrange("p (q n) -> p q n", n=S),
                                              ACT.Identity, scale=SCALE, bias=qb_col[rows_g, a:a + 1])
                    last.then_inc(q_ready[s], 1)
                    width = NONGT if a < 2 else S
                    await_fill(act, it, s, f"k a{a}")
                    keys = bank(s, f"k a{a}")[:].rearrange("p (b m) -> p b m", m=S)[:, :, 0:width]
                    blocks = kbd[a % 2][s][:, 0:NB * GH * width].rearrange("p (b h m) -> p b h m", h=GH, m=width)
                    for h in range(GH):
                        last = act.activation(blocks[:, :, h], keys, ACT.Identity, scale=head_mask[:, h:h + 1],
                                              bias=kb_head[:, a, h:h + 1])
                    last.then_inc(kbd_ready[s], 1)
                    act.activation(table_slot[:, s, a:a + 1], zero_col[:], ACT.Exp)
                if kind == "softmax":
                    pair = a % PAIRS
                    act.wait_ge(shifted[s], count(it, NATT * PAIRS, a + 1))
                    if a < 2 * PAIRS:
                        e = prob_g[s][:, 2 * pair:2 * pair + 2, :, 0:NONGT].rearrange("p g q m -> p (g q) m")
                    else:
                        e = prob[s][:, 2 * pair:2 * pair + 2]
                    act.activation(e, e, ACT.Exp).then_inc(exped[s], 1)
                if kind == "gather":
                    att = ATTN_OF_BLOCK[a]
                    await_fill(act, it, s, f"oT a{att}")
                    act.activation(oT[s][:], bank(s, f"oT a{att}")[:], ACT.Identity,
                                   bias=zero_col[:] if att == 2 else vec("L3_cond_qkv_b", 2)).then_inc(oT_ready[s], 1)
                if kind == "norm":
                    act.wait_ge(nmr_ready[s], count(it, NBLK, a + 1))
                    for b in range(DVE_NORMS, BT):
                        act.activation(xn[s][:, b], x[s][:, b], ACT.Identity, scale=rstd[s][:, b:b + 1],
                                       bias=nmr[s][:, b - DVE_NORMS:b - DVE_NORMS + 1]).then_inc(xn_act_ready[s], 1)
                    if BLOCKS[a][0] == "mlp":
                        act.activation(table_slot[:, s, NATT + a:NATT + a + 1], zero_col[:], GELU[BLOCKS[a][3]])
                if kind == "hidden":
                    for u in range(BLOCKS[a][2]):
                        await_fill(act, it, s, f"h{a}.{u}")
                        act.activation(hT[s][u], bank(s, f"h{a}.{u}")[:], GELU[BLOCKS[a][3]], bias=vec(HID_BIAS[a], u)
                                       ).then_inc(h_ready[s], 1)

            for kind, a, s, ahead in PROLOGUE:
                stage((0, ahead), kind, a, s)
            for j in (4, 5):
                act.wait_ge(setup_filled, 4 + j)
                act.wait_ge(sc1_ready, 2 * j + 2)
                act.activation(alpha[:, j - 4], SETUP_BANKS[3 + j][:, 2 * B:3 * B], ACT.Tanh, bias=modb(j)[2]
                               ).then_inc(alpha_ready, 1)
            with act.Fori(0, NIT) as it:
                for kind, a, s, ahead in ORDERS["scalar"]:
                    stage((it, ahead), kind, a, s)

        @block.vector
        def _(dve):
            for s in range(STREAMS):
                dve.memset(mx[s][:], 0.0).then_inc(x_ready[s], 1)
            dve.wait_ge(const_step, 6)
            dve.tensor_copy(ident16[:], ident[:]).then_inc(ident16_ready, 1)
            dve.tensor_copy(col[:], col_i[:]).then_inc(masks_step, 1)
            dve.tensor_copy(part[:], part_i[:]).then_inc(masks_step, 1)
            dve.wait_ge(masks_step, 2)
            dve.transpose(part32[:], col[:, 0:S]).then_inc(masks_step, 1)
            dve.wait_ge(masks_step, 3)
            dve.tensor_tensor(quad[:], part[:], part32[:], ALU.subtract).then_inc(masks_step, 1)
            head8 = col[:, 0:S].rearrange("p (h d) -> p h d", d=HD)[:, :, 0]
            dve.tensor_tensor(head_lo[:], part32[:, 0:GH], head8, ALU.subtract).then_inc(masks_step, 1)
            dve.wait_ge(masks_step, 5)
            dve.tensor_scalar(head_hi[:], head_lo[:], float(HD), None, ALU.is_lt).then_inc(masks_step, 1)
            dve.tensor_scalar(head_mask[:], head_lo[:], 0.0, None, ALU.is_ge).then_inc(masks_step, 1)
            dve.wait_ge(masks_step, 7)
            dve.tensor_tensor(head_mask[:], head_mask[:], head_hi[:], ALU.mult).then_inc(masks_step, 1)
            dve.tensor_tensor(quad_mask[:], col[:, 0:P].rearrange("p (b n) -> p b n", n=S)[:, :, 0], quad[:, 0:BT],
                              ALU.is_equal).then_inc(masks_step, 1)
            dve.tensor_tensor(rep32[:], col[:, 0:S].unsqueeze(1).broadcast_to([P, NG, S]),
                              part32[:].unsqueeze(1).broadcast_to([P, NG, S]), ALU.is_equal).then_inc(rep_ready, 1)
            dve.wait_ge(rep_ready, 1)
            dve.wait_ge(masks_step, 9)
            for b in range(BT):
                last = dve.tensor_scalar(sel[:, b], rep32[:].rearrange("p g n -> p (g n)"), quad_mask[:, b:b + 1], None,
                                         ALU.mult)
            last.then_inc(rep_ready, 1)
            dve.tensor_tensor(later[:], col[:, 0:S], part32[:], ALU.is_gt).then_inc(masks_step, 1)
            dve.wait_ge(masks_step, 10)
            dve.tensor_scalar(causal[:], later[:], CAUSAL, None, ALU.mult).then_inc(masks_step, 1)
            dve.wait_ge(cond_ready, 2)
            dve.tensor_scalar(sig, sig, 1.0, None, ALU.add).then_inc(cond_ready, 1)
            dve.wait_ge(cond_ready, 3)
            dve.reciprocal(sig, sig).then_inc(sig_ready, 1)
            dve.wait_ge(cols_ready, 1)
            dve.tensor_scalar(qb_col[:, 0:2], cols[:, ROW["L0_cond_bq"]:ROW["L0_cond_bq"] + 2], SCALE, None, ALU.mult
                              ).then_inc(masks_step, 1)
            dve.tensor_scalar(qb_col[:, 3:4], vec("L3_cond_qkv_b", 0), SCALE, None, ALU.mult).then_inc(masks_step, 1)
            dve.memset(qb_col[:, 2:3], 0.0).then_inc(masks_step, 1)
            dve.memset(kb_head[:, 2], 0.0).then_inc(masks_step, 1)
            for a, kb in ((0, vec("L0_cond_bk", 0)), (1, vec("L0_cond_bk", 1)), (3, vec("L3_cond_qkv_b", 1))):
                dve.tensor_scalar(kb_head[:, a], head_mask[:], kb, None, ALU.mult).then_inc(masks_step, 1)
            def stage(it, kind, a, s):
                def chain(sem_, per, k):
                    dve.wait_ge(sem_, count(it, per, k))

                if kind == "graph_in":
                    dve.wait_ge(x_loaded[s], count(it, 16 * T, 16 * T))
                    dve.tensor_reduce(row_sum[s][:], x_in[s][:], AX_X, ALU.add).then_inc(rsum_ready[s], 1)
                    chain(rsum_ready[s], 1, 1)
                    dve.tensor_scalar(row_flag[s][:], row_sum[s][:], 0.0, None, ALU.not_equal).then_inc(flag_ready[s], 1)
                if kind == "edges":
                    dve.wait_ge(bcast_loaded, 16 * 3)
                    dve.wait_ge(wT_ready, 2)
                    dve.wait_ge(adj_loaded[s], count(it, 16, 16))
                    dve.tensor_tensor(adj_w[s][:], adj[s][:], wb[:].unsqueeze(1).broadcast_to([P, T * S, L]),
                                      ALU.mult).then_inc(adjw_ready[s], 1)
                    dve.tensor_reduce(c_sum[s][:], adj[s][:], AX_X, ALU.add).then_inc(edge_step[s], 1)
                    dve.wait_ge(adjw_ready[s], count(it, 1, 1))
                    dve.tensor_reduce(u_sum[s][:], adj_w[s][:], AX_X, ALU.add).then_inc(edge_step[s], 1)
                    chain(edge_step[s], 4, 1)
                    dve.tensor_scalar(c_sum[s][:], c_sum[s][:], 0.0, NEG, ALU.is_gt, ALU.mult).then_inc(edge_step[s], 1)
                    chain(edge_step[s], 4, 2)
                    dve.tensor_scalar(u_sum[s][:], u_sum[s][:], bb[:], None, ALU.add).then_inc(edge_step[s], 1)
                    chain(edge_step[s], 4, 4)
                    dve.scalar_tensor_tensor(out=edge[s][:, 0].rearrange("p t m -> p (t m)"), in0=c_sum[s][:], scalar=-NEG,
                                             in1=u_sum[s][:], op0=ALU.add, op1=ALU.add).then_inc(edge_ready[s], 1)
                    chain(edge_ready[s], 2, 1)
                    dve.transpose(edge[s][:, 1].rearrange("p t m -> p (t m)"), edge[s][:, 0].rearrange("p t m -> p (t m)")
                                  ).then_inc(edge_ready[s], 1)
                if kind == "values_in":
                    await_fill(dve, it, s, f"v a{a}")
                    if a:
                        dve.wait_ge(vbd_ready[s], count(it, NATT, a))
                    dve.transpose(vt[s][:], bank(s, f"v a{a}")[:]).then_inc(vt_ready[s], 1)
                if kind == "softmax":
                    pair, graph = a % PAIRS, a < 2 * PAIRS
                    banks = slice(2 * pair, 2 * pair + 2)
                    width = NONGT if graph else S
                    await_scores(dve, it, a, s)
                    src = score[:, banks, 0:T * GH * width].rearrange("p b (q m) -> p b q m", m=width)
                    dst = (prob_g if graph else prob)[s][:, banks, :, 0:width]
                    m = mx[s][:, banks]
                    dve.tensor_reduce(m, src, AX_X, ALU.max).then_inc(maxed[s], 1)
                    chain(maxed[s], NATT * PAIRS, a + 1)
                    dve.tensor_tensor(dst, src, m.unsqueeze(3).broadcast_to([P, 2, T * GH, width]), ALU.subtract
                                      ).then_inc(shifted[s], 1)
                if kind == "turn":
                    att, pair = divmod(a, PAIRS)
                    banks = slice(2 * pair, 2 * pair + 2)
                    pr = prob_g[s] if att < 2 else prob[s]
                    dve.wait_ge(exped[s], count(it, NATT * PAIRS, a + 1))
                    dve.transpose(probT[att % 2][s][:, banks].rearrange("p b q n -> p (b q n)"),
                                  pr[:, banks].rearrange("p b q n -> p (b q n)")).then_inc(turned[s], 1)
                if kind == "values":
                    att, i = divmod(a, PAIRS)
                    name = f"o{'AB'[i]} a{att}"
                    dst = o[att] if att < 2 else o[0]
                    half = bank(s, name)[:, 0:2 * H * VW].rearrange("p (q c) -> p q c", c=VW)
                    await_fill(dve, it, s, name)
                    dve.reciprocal(recip[s][:, i], half[:, :, HD]).then_inc(recip_ready[s], 1)
                    chain(recip_ready[s], 2 * NATT, a + 1)
                    dve.tensor_tensor(dst[s][:, 2 * i:2 * i + 2].rearrange("p b (h d) -> p (b h) d", d=HD), half[:, :, 0:HD],
                                      recip[s][:, i].unsqueeze(2).broadcast_to([P, 2 * H, HD]), ALU.mult
                                      ).then_inc(o_ready[s], 1)
                if kind == "self_out":
                    dve.wait_ge(osum_step[s], count(it, 1, 1))
                    for i, name in enumerate(("self01", "self23")):
                        await_fill(dve, it, s, name)
                        dve.tensor_tensor(o[0][s][:, 2 * i:2 * i + 2], bank(s, name)[:, 0:2 * D].rearrange("p (t f) -> p t f", f=D),
                                          o[0][s][:, 2 * i:2 * i + 2], ALU.add).then_inc(out_step[s], 1)
                if kind == "graph_out":
                    chain(out_step[s], 2, 2)
                    chain(o_ready[s], 2 * NATT, 4)
                    dve.tensor_tensor(o[1][s][:], o[0][s][:], o[1][s][:], ALU.add).then_inc(gsum_ready[s], 1)
                    chain(gsum_ready[s], 1, 1)
                    dve.wait_ge(x_stored[s], count(it, 16 * T, 16 * T))
                    dve.scalar_tensor_tensor(out=x[s][:].rearrange("p t f -> p (t f)"), in0=o[1][s][:].rearrange("p t f -> p (t f)"),
                                             scalar=0.0, in1=x_in[s][:].rearrange("p t f -> p (t f)"), op0=ALU.max,
                                             op1=ALU.add).then_inc(x_ready[s], 1)
                if kind == "stats":
                    await_x(dve, it, s, a + 1)
                    for t in range(T):
                        dve.bn_stats(stats[s][:, t], x[s][:, t]).then_inc(stats_ready[s], 1)
                    chain(stats_ready[s], T * NBLK, T * a + T)
                    dve.memset(wait_slot[:], 0.0)
                    for t in range(T):
                        dve.bn_aggr(mv[s][:, t], stats[s][:, t]).then_inc(mv_ready[s], 1)
                    chain(mv_ready[s], T * NBLK, T * a + T)
                    dve.tensor_scalar(veps[s][:], mv[s][:, :, 1], EPS[a], None, ALU.add).then_inc(veps_ready[s], 1)
                if kind == "norm":
                    dve.wait_ge(rstd_ready[s], count(it, NBLK, a + 1))
                    dve.scalar_tensor_tensor(out=nmr[s][:], in0=mv[s][:, DVE_NORMS:, 0], scalar=-1.0,
                                             in1=rstd[s][:, DVE_NORMS:], op0=ALU.mult, op1=ALU.mult).then_inc(nmr_ready[s], 1)
                    for b in range(DVE_NORMS):
                        dve.tensor_scalar(xn[s][:, b], x[s][:, b], mv[s][:, b, 0:1], rstd[s][:, b:b + 1],
                                          ALU.subtract, ALU.mult).then_inc(xn_ready[s], 1)
                if kind == "modulate":
                    if a == 0:
                        dve.wait_ge(modc_ready[s], count(it, 1, 1))
                    m = mod_b[s]
                    await_fill(dve, it, s, f"xn{a}")
                    ps = bank(s, f"xn{a}")[:].rearrange("p (b n) -> p b n", n=S)
                    dve.tensor_tensor(xm0[s][:].rearrange("p (b n) -> p b n", n=S), ps,
                                      m[:, 3 * a].unsqueeze(2).broadcast_to([P, NB, S]), ALU.mult).then_inc(scaled[s], 1)
                    chain(scaled[s], NBLK, a + 1)
                    dve.tensor_tensor(xm[s][:].rearrange("p (b n) -> p b n", n=S), xm0[s][:].rearrange("p (b n) -> p b n", n=S),
                                      m[:, 3 * a + 1].unsqueeze(2).broadcast_to([P, NB, S]), ALU.add).then_inc(xm_ready[s], 1)
                if kind in ("project", "down"):
                    await_fill(dve, it, s, f"y{a}")
                    dve.scalar_tensor_tensor(out=yT[s].rearrange("p (b n) -> p b n", n=S),
                                             in0=bank(s, f"y{a}")[:].rearrange("p (b n) -> p b n", n=S),
                                             scalar=vec(OUT_BIAS[a]), in1=mod_b[s][:, 3 * a + 2].unsqueeze(2).broadcast_to([P, NB, S]),
                                             op0=ALU.add, op1=ALU.mult).then_inc(y_ready[s], 1)
                if kind == "residual":
                    await_fill(dve, it, s, f"yT{a}")
                    dve.tensor_tensor(x[s][:].rearrange("p t f -> p (t f)"), bank(s, f"yT{a}")[:],
                                      x[s][:].rearrange("p t f -> p (t f)"), ALU.add).then_inc(x_ready[s], 1)

            for kind, a, s, ahead in PROLOGUE:
                stage((0, ahead), kind, a, s)
            for j in range(NBLK):
                ps = SETUP_BANKS[3 + j]
                sc_b, sh_b, gt_b = modb(j)
                dve.wait_ge(setup_filled, 4 + j)
                scale, shift, gate = (mod[:, 3 * j + k, 0:B] for k in range(3))
                if j in GAIN:
                    g, be = (vec(n) for n in GAIN[j])
                    dve.tensor_scalar(sc1[:, j], ps[:, 0:B], sc_b, 1.0, ALU.add, ALU.add).then_inc(sc1_ready, 1)
                    dve.tensor_scalar(shift, ps[:, B:2 * B], sh_b, None, ALU.add).then_inc(sc1_ready, 1)
                else:
                    dve.tensor_scalar(scale, ps[:, 0:B], sc_b, 1.0, ALU.add, ALU.add).then_inc(sc1_ready, 1)
                    dve.tensor_scalar(shift, ps[:, B:2 * B], sh_b, None, ALU.add).then_inc(sc1_ready, 1)
                dve.wait_ge(sc1_ready, 2 * j + 2)
                if BLOCKS[j][1] < 3:
                    last = dve.tensor_scalar(gate, ps[:, 2 * B:3 * B], gt_b, None, ALU.add)
                else:
                    dve.wait_ge(alpha_ready, j - 3)
                    last = dve.tensor_scalar(gate, alpha[:, j - 4], 0.1, None, ALU.mult)
                if j in GAIN:
                    dve.tensor_scalar(scale, sc1[:, j], g, None, ALU.mult)
                    last = dve.scalar_tensor_tensor(out=shift, in0=sc1[:, j], scalar=be, in1=shift, op0=ALU.mult, op1=ALU.add)
                last.then_inc(mod_ready, 1)
            dve.memset(mod[:, :, B:B + NB], 0.0).then_inc(mod_ready, 1)
            with dve.Fori(0, NIT) as it:
                for kind, a, s, ahead in ORDERS["vector"]:
                    stage((it, ahead), kind, a, s)

        @block.tensor
        def _(pe):
            pe.wait_ge(const_step, 6)
            pe.wait_ge(vec_loaded, 16 * (len(VECTORS) + 1))
            pe.transpose(SETUP_BANKS[0][:, 0:B], cond_in, ident[:])
            pe.transpose(SETUP_BANKS[0][:, B:B + NROWS], rows[:], ident[0:NROWS, 0:NROWS]).then_inc(setup_filled, 1)
            pe.wait_ge(raw_loaded, 16 * 4)
            for g in range(2):
                for k in range(4):
                    last = pe.transpose(SETUP_BANKS[1 + g][:, k * D:(k + 1) * D], raw[:, 4 * g + k], ident[:])
                last.then_inc(setup_filled, 1)
            pe.wait_ge(wT_ready, 2)
            pe.wait_ge(cols_ready, 1)
            pe.wait_ge(cond_ready, 2)

            def to_features(s, name, src, await_seq=lambda b: None):
                for b in range(BT):
                    await_seq(b)
                    last = pe.transpose(bank(s, name)[:, b * P:(b + 1) * P], src[:, b], ident[:])
                last.then_inc(filled[s], 1)

            def to_tokens(s, name, src, first, n):
                for b in range(n):
                    last = pe.transpose(bank(s, name)[:, b * D:(b + 1) * D], src[:, (first + b) * P:(first + b + 1) * P],
                                        ident[:])
                last.then_inc(filled[s], 1)

            def stage(it, kind, a, s):
                if kind == "graph_in":
                    pe.wait_ge(x_loaded[s], count(it, 16 * T, 16 * T))
                    await_bank(pe, it, s, "xT")
                    to_features(s, "xT", x_in[s])
                    await_bank(pe, it, s, "qcT")
                    pe.wait_ge(qm_ready[s], count(it, 1, 1))
                    to_features(s, "qcT", q_in[s])
                if kind == "self":
                    await_bank(pe, it, s, "self")
                    pe.wait_ge(xT_ready[s], count(it, 1, 1))
                    pe.matmul(bank(s, "self")[:], wT[:, 0], xT[s][:], start=True, stop=False)
                    pe.wait_ge(qcT_ready[s], count(it, 1, 1))
                    pe.matmul(bank(s, "self")[:], wT[:, 1], qcT[s][:], start=False, stop=True).then_inc(filled[s], 1)
                src = sfT[s] if a < 2 else xm[s]
                if kind == "keys":
                    if a < 2:
                        pe.wait_ge(sf_ready[s], count(it, 1, 1))
                    else:
                        pe.wait_ge(xm_ready[s], count(it, NBLK, 1 if a == 2 else 5))
                    await_bank(pe, it, s, f"q a{a}")
                    pe.matmul(bank(s, f"q a{a}")[:], q_weight(a), src[:], start=True, stop=True).then_inc(filled[s], 1)
                    await_bank(pe, it, s, f"k a{a}")
                    pe.matmul(bank(s, f"k a{a}")[:], k_weight(a), src[:], start=True, stop=True).then_inc(filled[s], 1)
                if kind == "values_in":
                    await_bank(pe, it, s, f"v a{a}")
                    pe.matmul(bank(s, f"v a{a}")[:], v_weight(a), src[:], start=True, stop=True).then_inc(filled[s], 1)
                if kind == "scores":
                    att, pair = divmod(a, PAIRS)
                    cw = GH * (NONGT if att < 2 else S)
                    if pair == 0:
                        pe.wait_ge(q_ready[s], count(it, NATT, att + 1))
                        pe.wait_ge(kbd_ready[s], count(it, NATT, att + 1))
                    await_score_bank(pe, it, a, s)
                    if att < 2:
                        pe.wait_ge(edge_ready[s], count(it, 2, att + 1))
                    for b in (2 * pair, 2 * pair + 1):
                        if att == 2:
                            pe.matmul(score[:, b], ident16[:], causal[:].unsqueeze(1).broadcast_to([P, NB, S]),
                                      start=True, stop=False, skip_group_check=True)
                        if att < 2:
                            pe.matmul(score[:, b, 0:T * cw].rearrange("p (t h m) -> p t h m", t=T, h=GH), sel[:, b],
                                      edge[s][:, att, :, 0:NONGT].unsqueeze(2).broadcast_to([P, T, GH, NONGT]),
                                      start=True, stop=False, skip_group_check=True)
                    for b in (2 * pair, 2 * pair + 1):
                        for t in range(T):
                            q = b * T + t
                            last = pe.matmul(score[:, b, t * cw:(t + 1) * cw], qd[s][:, q].rearrange("p g n -> p (g n)"),
                                             kbd[att % 2][s][:, q * cw:(q + 1) * cw],
                                             start=(att == 3), stop=True, skip_group_check=(att < 3))
                    last.then_inc(scored, 1)
                if kind == "values":
                    att, pair = divmod(a, PAIRS)
                    name = f"o{'AB'[pair]} a{att}"
                    pe.wait_ge(vbd_ready[s], count(it, NATT, att + 1))
                    await_bank(pe, it, s, name)
                    pe.wait_ge(turned[s], count(it, NATT * PAIRS, a + 1))
                    out_h = bank(s, name)[:, 0:2 * H * VW].rearrange("p (b g h c) -> p b g h c", b=2, h=GH, c=VW)
                    for b in range(2):
                        for h in range(GH):
                            for t in range(T):
                                q = (2 * pair + b) * T + t
                                last = pe.matmul(out_h[S * t:S * t + S, b, :, h],
                                                 probT[att % 2][s][:, 2 * pair + b, t * GH + h],
                                                 vbd[att % 2][s][:, q * GH + h], start=True, stop=True)
                    last.then_inc(filled[s], 1)
                if kind == "self_out":
                    for i, name in enumerate(("self01", "self23")):
                        await_bank(pe, it, s, name)
                        pe.wait_ge(sf_ready[s], count(it, 1, 1))
                        to_tokens(s, name, sfT[s], 2 * i, 2)
                if kind == "norm":
                    await_bank(pe, it, s, f"xn{a}")
                    def await_xn(b):
                        if b < DVE_NORMS:
                            pe.wait_ge(xn_ready[s], count(it, DVE_NORMS * NBLK, DVE_NORMS * a + b + 1))
                        else:
                            pe.wait_ge(xn_act_ready[s], count(it, (BT - DVE_NORMS) * NBLK, (BT - DVE_NORMS) * a + b - DVE_NORMS + 1))
                    to_features(s, f"xn{a}", xn[s], await_xn)
                if kind == "gather":
                    att = ATTN_OF_BLOCK[a]
                    await_bank(pe, it, s, f"oT a{att}")
                    pe.wait_ge(o_ready[s], count(it, 2 * NATT, 2 * att + 2))
                    to_features(s, f"oT a{att}", o[0][s])
                if kind == "project":
                    att = ATTN_OF_BLOCK[a]
                    await_bank(pe, it, s, f"y{a}")
                    pe.wait_ge(oT_ready[s], count(it, 2, att - 1))
                    pe.matmul(bank(s, f"y{a}")[:], w[PROJ[a]][:, 0], oT[s][:], start=True, stop=True).then_inc(filled[s], 1)
                if kind == "hidden":
                    pe.wait_ge(xm_ready[s], count(it, NBLK, a + 1))
                    for u in range(BLOCKS[a][2]):
                        await_bank(pe, it, s, f"h{a}.{u}")
                        pe.matmul(bank(s, f"h{a}.{u}")[:], w[UP[a]][:, 0, u * D:(u + 1) * D], xm[s][:], start=True, stop=True
                                  ).then_inc(filled[s], 1)
                if kind == "down":
                    await_bank(pe, it, s, f"y{a}")
                    nh = BLOCKS[a][2]
                    for u in range(nh):
                        pe.wait_ge(h_ready[s], count(it, NHID, HIDDEN_BEFORE[a] + u + 1))
                        last = pe.matmul(bank(s, f"y{a}")[:], w[DOWN[a]][:, u], hT[s][u], start=(u == 0), stop=(u == nh - 1))
                    last.then_inc(filled[s], 1)
                if kind == "residual":
                    await_bank(pe, it, s, f"yT{a}")
                    pe.wait_ge(y_ready[s], count(it, NBLK, a + 1))
                    to_tokens(s, f"yT{a}", yT[s], 0, BT)

            for kind, a, s, ahead in PROLOGUE:
                stage((0, ahead), kind, a, s)
            pe.wait_ge(wmod_loaded, 16 * len(MODW))
            pe.wait_ge(silu_ready, 1)
            for j in range(NBLK):
                for k, wk in enumerate(modw(j)):
                    last = pe.matmul(SETUP_BANKS[3 + j][:, k * B:(k + 1) * B], wk, siluT if BLOCKS[j][1] < 3 else condT,
                                     start=True, stop=True)
                last.then_inc(setup_filled, 1)
            pe.wait_ge(w_loaded, 16 * len(DIRECT))
            pe.wait_ge(ident16_ready, 1)
            pe.wait_ge(masks_step, 14)
            pe.wait_ge(rep_ready, 2)
            pe.wait_ge(mod_ready, NBLK + 1)
            pe.wait_ge(const_step, 15)
            with pe.Fori(0, NIT) as it:
                for kind, a, s, ahead in ORDERS["tensor"]:
                    stage((it, ahead), kind, a, s)


def kernel(**inputs):
    import numpy as _np
    import concourse.bacc as _bacc
    from concourse import mybir as _mybir
    from concourse.bass_utils import run_bass_kernel_spmd as _run

    nc = _bacc.Bacc("TRN2", target_bir_lowering=False, num_devices=1)
    arrays, args = {}, {}
    for name, value in inputs.items():
        a = _np.ascontiguousarray(value)
        if name == "L0_cond_b_bias":
            a = a.reshape(1)
        arrays[f"in_{name}"] = a
        args[name] = nc.dram_tensor(f"in_{name}", a.shape, _mybir.dt.from_np(a.dtype), kind="ExternalInput").ap()
    out = nc.dram_tensor("out_x", (B, S, D), _mybir.dt.float32, kind="ExternalOutput").ap()
    build(nc, args, out)
    r = _run(nc, [arrays], core_ids=[0])
    return r.results[0]["out_x"]
```
